# Optimizing a Trainium2 kernel written in Bass

```python
import numpy as np
import jax
import jax.numpy as jnp

def _softmax(x, axis=-1):
    return jax.nn.softmax(x, axis=axis)

def _gelu(x):
    return jax.nn.gelu(x, approximate=True)

def _silu(x):
    return jax.nn.silu(x)

def _sigmoid(x):
    return jax.nn.sigmoid(x)

def _layernorm(x, axis=-1, eps=1e-05):
    m = jnp.mean(x, axis=axis, keepdims=True)
    v = jnp.var(x, axis=axis, keepdims=True)
    return (x - m) / jnp.sqrt(v + eps)

def _scatter_add(tgt, idx, src, axis=0):
    return tgt.at[idx].add(src)

def _segment_sum(src, seg, n):
    return jax.ops.segment_sum(src, seg, n)
kernel_name = 'mk_gnn_preln_d2_gnn_r8_c55686'

def setup_inputs(seed: int=0):
    np.random.seed(seed)
    _w = jnp.asarray

    def _rec_inputs():
        import jax
        import jax.numpy as jnp
        _gk = jax.random.key(seed)
        x = -0.0005207 + 1.001 * jax.random.normal(jax.random.fold_in(_gk, 1), (6250, 128), jnp.float32)
        src = jax.random.randint(jax.random.fold_in(_gk, 2), (200000,), 0, 6250, jnp.int32)
        dst = jax.random.randint(jax.random.fold_in(_gk, 3), (200000,), 0, 6250, jnp.int32)
        _o = jnp.argsort(dst, stable=True)
        src = src[_o]
        dst = dst[_o]
        edge_attr_3 = -0.000451519 + 1.00018 * jax.random.normal(jax.random.fold_in(_gk, 12), (200000, 3), jnp.float32)
        edge_type_50 = jax.random.randint(jax.random.fold_in(_gk, 14), (200000,), 0, 50, jnp.int32)
        edge_weight = jax.random.uniform(jax.random.fold_in(_gk, 15), (200000,), jnp.float32, 0.0, 0.999998)
        return (x, src, dst, edge_attr_3, edge_type_50, edge_weight)
    x, src, dst, edge_attr_3, edge_type_50, edge_weight = _rec_inputs()

    def _L0_gnn_setup():
        import jax, jax.numpy as jnp
        import numpy as np
        N_ENT = 2048
        N_REL = 50
        D = 128
        B = 4
        E = 32768
        key = jax.random.key(seed)
        k1, k2, k3, k4, k5, k6 = jax.random.split(key, 6)
        x = jax.random.normal(k1, (N_ENT, D), dtype=jnp.float32)
        bases = jax.random.normal(k2, (B, D, D), dtype=jnp.float32) * 0.05
        comps = jax.random.normal(k3, (N_REL, B), dtype=jnp.float32)
        alpha = jax.random.normal(k4, (N_REL, 1), dtype=jnp.float32)
        edge_index = jax.random.randint(k5, (2, E), 0, N_ENT, dtype=jnp.int64)
        edge_type = jax.random.randint(k6, (E,), 0, N_REL, dtype=jnp.int64)
        return {'x': x, 'bases': bases, 'comps': comps, 'alpha': alpha, 'edge_index': edge_index, 'edge_type': edge_type}
    _L0_gnn_all = _L0_gnn_setup()
    _L0_gnn_in = {k: v for k, v in _L0_gnn_all.items() if k in ('bases', 'comps', 'alpha')}
    del _L0_gnn_all

    def _L1_gnn_setup():
        import jax, jax.numpy as jnp
        import numpy as np
        N = 6250
        E = 100000
        MUL = 32
        NB = 8
        R_MAX = 1.0
        AVG = 16.0
        SQ3 = 3.0 ** 0.5

        def _radial_embedding(r):
            x = jnp.clip(r / R_MAX, 0.0, 1.0)
            centers = jnp.arange(NB, dtype=jnp.float32) / (NB - 1)
            sigma = 1.0 / (NB - 1)
            emb = jnp.exp(-0.5 * ((x[:, None] - centers[None, :]) / sigma) ** 2)
            emb = emb * NB ** 0.5 * (r <= R_MAX).astype(jnp.float32)[:, None]
            return emb
        key = jax.random.key(seed)
        k = jax.random.split(key, 12)
        inp = {'node_feats': jax.random.normal(k[0], (N, 4 * MUL), dtype=jnp.float32), 'edge_vec': jax.random.normal(k[1], (E, 3), dtype=jnp.float32), 'edge_length': jax.random.uniform(k[2], (E,), dtype=jnp.float32), 'senders': jax.random.randint(k[3], (E,), 0, N, dtype=jnp.int32), 'receivers': jax.random.randint(k[4], (E,), 0, N, dtype=jnp.int32), 'num_nodes': N, 'W_up0': jax.random.normal(k[5], (MUL, MUL), dtype=jnp.float32), 'W_up1': jax.random.normal(k[6], (MUL, MUL), dtype=jnp.float32), 'mlp_w0': jax.random.normal(k[7], (NB, 64), dtype=jnp.float32) / NB ** 0.5, 'mlp_b0': jnp.zeros((64,), dtype=jnp.float32), 'mlp_w1': jax.random.normal(k[8], (64, 64), dtype=jnp.float32) / 8.0, 'mlp_b1': jnp.zeros((64,), dtype=jnp.float32), 'mlp_w2': jax.random.normal(k[9], (64, 4 * MUL), dtype=jnp.float32) / 8.0, 'mlp_b2': jnp.zeros((4 * MUL,), dtype=jnp.float32), 'W_out0': jax.random.normal(k[10], (2 * MUL, MUL), dtype=jnp.float32), 'W_out1': jax.random.normal(k[11], (2 * MUL, MUL), dtype=jnp.float32)}
        return inp
    _L1_gnn_all = _L1_gnn_setup()
    _L1_gnn_in = {k: v for k, v in _L1_gnn_all.items() if k in ('W_up0', 'W_up1', 'mlp_w0', 'mlp_b0', 'mlp_w1', 'mlp_b1', 'mlp_w2', 'mlp_b2', 'W_out0', 'W_out1')}
    del _L1_gnn_all
    return {'x': x, 'src': src, 'dst': dst, 'edge_attr_3': edge_attr_3, 'edge_type_50': edge_type_50, 'edge_weight': edge_weight, 'L0_gnn_bases': _L0_gnn_in['bases'], 'L0_gnn_comps': _L0_gnn_in['comps'], 'L0_gnn_alpha': _L0_gnn_in['alpha'], 'L1_gnn_W_up0': _L1_gnn_in['W_up0'], 'L1_gnn_W_up1': _L1_gnn_in['W_up1'], 'L1_gnn_mlp_w0': _L1_gnn_in['mlp_w0'], 'L1_gnn_mlp_b0': _L1_gnn_in['mlp_b0'], 'L1_gnn_mlp_w1': _L1_gnn_in['mlp_w1'], 'L1_gnn_mlp_b1': _L1_gnn_in['mlp_b1'], 'L1_gnn_mlp_w2': _L1_gnn_in['mlp_w2'], 'L1_gnn_mlp_b2': _L1_gnn_in['mlp_b2'], 'L1_gnn_W_out0': _L1_gnn_in['W_out0'], 'L1_gnn_W_out1': _L1_gnn_in['W_out1']}

def reference(x, src, dst, edge_attr_3, edge_type_50, edge_weight, L0_gnn_bases, L0_gnn_comps, L0_gnn_alpha, L1_gnn_W_up0, L1_gnn_W_up1, L1_gnn_mlp_w0, L1_gnn_mlp_b0, L1_gnn_mlp_w1, L1_gnn_mlp_b1, L1_gnn_mlp_w2, L1_gnn_mlp_b2, L1_gnn_W_out0, L1_gnn_W_out1):
    import jax
    import jax.numpy as jnp

    def _L0_gnn_ref(x, bases, comps, alpha, edge_index, edge_type):
        import jax, jax.numpy as jnp
        import numpy as np
        N_ENT = 2048
        N_REL = 50
        D = 128
        B = 4
        E = 32768
        n = x.shape[0]
        row, col = (edge_index[0], edge_index[1])
        ones = jnp.ones(row.shape, x.dtype)
        deg = jax.ops.segment_sum(ones, row, num_segments=n)
        deg_inv = jnp.where(deg > 0, jax.lax.rsqrt(jnp.maximum(deg, 1.0)), 0.0)
        norm = deg_inv[row] * deg_inv[col]
        h_j = x[col]
        c_e = comps[edge_type]
        hj_b = c_e[:, :, None] * h_j[:, None, :]
        msg = jnp.einsum('ebd,bdf->ef', hj_b, bases)
        msg = msg * alpha[edge_type] * norm[:, None]
        out = jax.ops.segment_sum(msg, row, num_segments=n)
        return out

    def _L1_gnn_ref(node_feats, edge_vec, edge_length, senders, receivers, num_nodes, W_up0, W_up1, mlp_w0, mlp_b0, mlp_w1, mlp_b1, mlp_w2, mlp_b2, W_out0, W_out1):
        import jax, jax.numpy as jnp
        import numpy as np
        N = 6250
        E = 100000
        MUL = 32
        NB = 8
        R_MAX = 1.0
        AVG = 16.0
        SQ3 = 3.0 ** 0.5

        def _radial_embedding(r):
            x = jnp.clip(r / R_MAX, 0.0, 1.0)
            centers = jnp.arange(NB, dtype=jnp.float32) / (NB - 1)
            sigma = 1.0 / (NB - 1)
            emb = jnp.exp(-0.5 * ((x[:, None] - centers[None, :]) / sigma) ** 2)
            emb = emb * NB ** 0.5 * (r <= R_MAX).astype(jnp.float32)[:, None]
            return emb
        f32 = jnp.float32
        rhat = edge_vec / (jnp.linalg.norm(edge_vec, axis=-1, keepdims=True) + 1e-12)
        Y1 = SQ3 * rhat
        emb = _radial_embedding(edge_length)
        h = jax.nn.silu(emb @ mlp_w0 + mlp_b0)
        h = jax.nn.silu(h @ mlp_w1 + mlp_b1)
        w = (h @ mlp_w2 + mlp_b2).reshape(-1, 4, MUL)
        s = node_feats[:, :MUL]
        v = node_feats[:, MUL:].reshape(-1, MUL, 3)
        xs = s @ W_up0 / f32(MUL) ** 0.5
        xv = jnp.einsum('nmc,mk->nkc', v, W_up1) / f32(MUL) ** 0.5
        ss = xs[senders]
        vv = xv[senders]
        m0 = w[:, 0] * ss
        m1 = w[:, 1][:, :, None] * ss[:, :, None] * Y1[:, None, :]
        m2 = w[:, 2][:, :, None] * vv
        m3 = w[:, 3] * (jnp.einsum('emc,ec->em', vv, Y1) / SQ3)
        mid_s = jnp.concatenate([m0, m3], axis=1)
        mid_v = jnp.concatenate([m1, m2], axis=1)
        msg_s = jax.ops.segment_sum(mid_s, receivers, num_segments=num_nodes)
        msg_v = jax.ops.segment_sum(mid_v, receivers, num_segments=num_nodes)
        out_s = msg_s @ W_out0 / f32(2 * MUL) ** 0.5
        out_v = jnp.einsum('nmc,mk->nkc', msg_v, W_out1) / f32(2 * MUL) ** 0.5
        out = jnp.concatenate([out_s, out_v.reshape(-1, 3 * MUL)], axis=1)
        return out / max(AVG, 1e-08)
    edge_index = jnp.stack([src, dst])
    h = jnp.maximum(_layernorm(x, axis=-1), 0.0)
    x = x + _L0_gnn_ref(h, L0_gnn_bases, L0_gnn_comps, L0_gnn_alpha, edge_index, edge_type_50)
    h = jnp.maximum(_layernorm(x, axis=-1), 0.0)
    x = x + _L1_gnn_ref(h, edge_attr_3, edge_weight, src, dst, 6250, L1_gnn_W_up0, L1_gnn_W_up1, L1_gnn_mlp_w0, L1_gnn_mlp_b0, L1_gnn_mlp_w1, L1_gnn_mlp_b1, L1_gnn_mlp_w2, L1_gnn_mlp_b2, L1_gnn_W_out0, L1_gnn_W_out1)
    return x

_drawn_inputs = setup_inputs


def setup_inputs(seed=0):
    import zlib

    import numpy as np

    out = dict(_drawn_inputs(seed))
    spreads = {'L1_gnn_mlp_b0': (0.0, 0.413), 'L1_gnn_mlp_b1': (0.0, 0.1), 'L1_gnn_mlp_b2': (0.0, 0.1)}
    factors = {}
    for name, (base, spread) in spreads.items():
        noise = np.random.default_rng([zlib.crc32(name.encode()), seed]).standard_normal(out[name].shape)
        drawn = base * np.exp(spread * noise) if base else spread * noise
        out[name] = jnp.asarray(drawn.astype(out[name].dtype))
    for name, factor in factors.items():
        out[name] = (out[name] * factor).astype(out[name].dtype)
    return out
```

```python
import numpy as np
import concourse.bass as bass
import concourse.mybir as mybir
from contextlib import ExitStack

F32, BF16, I32 = mybir.dt.float32, mybir.dt.bfloat16, mybir.dt.int32
ALU = mybir.AluOpType
ACT = mybir.ActivationFunctionType

P = 128
D = 128
NODES = 6250
NT = -(-NODES // P) + 1
NPAD = NT * P
EDGES = 200000
TPS = 4
RING = 8
GROUPS = 16
TILES = 1568
TPG = TILES // GROUPS
PASSES = TILES // (TPS * RING)
STEPS = TILES // TPS
BLOCKS = 13
COLS = BLOCKS * P
EPG = TPG * P
PAD_NODE = NODES
NB = 4
EMB_PARTS = [(n * 3200, (n + 1) * 3200) for n in range(4)]
NREL = 50
CENTERS = 8
HID = 64
MUL = 32
GSLOT = 4
AHEAD = GSLOT - 1
CHUNK = 16
NCH = TILES // CHUNK
EPS = 1e-5
DB = 5
SQ3 = 3.0 ** 0.5


def build(nc, a, out):
    ctx = ExitStack()
    with ctx:
        def sb(name, shape, dt=F32):
            return ctx.enter_context(nc.sbuf_tensor(name, shape, dt))

        def ps(name, shape, dt=F32):
            return ctx.enter_context(nc.psum_tensor(name, shape, dt))

        def sem(name):
            return ctx.enter_context(nc.semaphore(name))

        def dram(name, shape):
            return nc.dram_tensor(name, shape, F32, kind="Internal").ap()

        ytab = dram("ytab", [NPAD, NB * D])
        xtab = dram("xtab", [NPAD, D])
        acc0 = [dram(f"acc0_{i}", [NPAD, D]) for i in range(TPS)]
        acc1 = [dram(f"acc1_{i}", [NPAD, 2 * D]) for i in range(TPS)]

        xn = sb("xn", [P, NT, D])
        edge = sb("edge", [P, COLS, 5])
        arena = sb("arena", [P, 12800])
        emb = arena
        rows_i = arena[:, 0:BLOCKS * 5 * P].bitcast(I32)
        src_rows = rows_i[:, 0:BLOCKS * P].rearrange("q (j e) -> q j e", j=BLOCKS)
        dst_rows = rows_i[:, BLOCKS * P:2 * BLOCKS * P].rearrange("q (j e) -> q j e", j=BLOCKS)
        attr_rows = arena[:, 2 * BLOCKS * P:5 * BLOCKS * P].rearrange("q (j e) -> q j e", j=BLOCKS)
        TY0 = BLOCKS * 5 * P
        typ = arena[0:64, TY0:TY0 + 2 * CHUNK * P].bitcast(I32).rearrange("q (b e) -> q b e", b=2)
        accin = arena[:, 0:2 * TPS * DB * D].rearrange("p (b r x) -> p b r x", b=2, r=TPS)
        coef_mem = sb("coef_mem", [P, COLS * NB])
        coef = coef_mem[:, :].rearrange("p (t b) -> p t b", b=NB)
        mid = coef_mem[:, 0:2 * TPS * 2 * D].rearrange("p (s i x) -> p s i x", s=2, i=TPS)
        M0 = 2 * TPS * 2 * D
        hid0 = coef_mem[:, M0:M0 + 256]
        hid1 = coef_mem[:, M0 + 256:M0 + 512]
        w01s = coef_mem[:, M0 + 512:M0 + 640].rearrange("p (i x) -> p i x", i=TPS)
        vdot = coef_mem[:, M0 + 768:M0 + 1152].rearrange("p (i c k) -> p i c k", i=TPS, c=3)
        vsum = coef_mem[:, M0 + 1152:M0 + 1408].rearrange("p (i c k) -> p i c k", i=TPS, c=2)
        gmem = sb("gmem", [P, GSLOT * TPS * NB * D])
        gat0 = gmem[:, :].rearrange("p (s i x) -> p s i x", s=GSLOT, i=TPS)
        gat1 = gmem[:, 0:GSLOT * TPS * D].rearrange("p (s i x) -> p s i x", s=GSLOT, i=TPS)
        OH = 2 * CHUNK * P
        typ_hot = gmem[0:64, 0:OH].rearrange("p (b e) -> p b e", b=2)
        lo_hot = gmem[:, OH:OH + CHUNK * P].bitcast(BF16).rearrange("p (b t x) -> p b t x", b=2, x=P)
        HI0 = OH + CHUNK * P
        hi_hot = gmem[:, HI0:HI0 + CHUNK * NT].bitcast(BF16).rearrange("p (b t x) -> p b t x", b=2, x=NT)
        node_out = gmem[:, 0:2 * 512].rearrange("p (b x) -> p b x", b=2)
        sum_out = sb("sum_out", [P, 2, TPS, 2 * D])
        same = sb("same", [P, 2, TPS, P])
        zero = sb("zero", [P, 800])
        ident = sb("ident", [P, P])
        iota = sb("iota", [P, P])
        pcol = sb("pcol", [P, 8])
        lo_f = sum_out[:, :, :, :].rearrange("p s i x -> p (s i x)")[:, 0:COLS]
        hi_f = sb("hi_f", [P, COLS])
        st_edge = sb("st_edge", [P, RING, TPS, 5])
        gidx = sb("gidx", [P, RING, TPS], I32)
        sidx = sb("sidx", [P, TPS, TPS], I32)
        dupd = sb("dupd", [P, TPS])
        bases = sb("bases", [P, NB, D])
        table = sb("table", [64, NB])
        alpha = sb("alpha", [64, 1])
        w_up = sb("w_up", [P, D])
        w_m0 = sb("w_m0", [P, GROUPS // 2, P])
        w_m1 = sb("w_m1", [P, P])
        w_m2 = sb("w_m2", [P, 2, P])
        b_m = sb("b_m", [P, 2])
        b2_row = sb("b2_row", [1, D])
        b2_four = sb("b2_four", [P, TPS, D])
        ones = sb("ones", [P, P])
        w_o = sb("w_o", [P, 2, D])
        w_o1 = sb("w_o1", [P, MUL])
        zero_b = sb("zero_b", [P, P], BF16)
        stats = sb("stats", [P, NT, 6])
        rstd = sb("rstd", [P, NT])
        nbias = sb("nbias", [P, NT])
        deg = sb("deg", [NT, P])
        dinv = sb("dinv", [P, NT])
        dpos = sb("dpos", [P, NT])
        hrow = sb("hrow", [P, 2, D])
        hrowT = sb("hrowT", [P, 2, D])
        tT = sb("tT", [P, 2 * D])
        moment = sb("moment", [P, 3, NT])

        bank = [ps(f"bank{i}", [P, 512]) for i in range(8)]

        ld_edge, ld_attr, ld_x, ld_const = sem("ld_edge"), sem("ld_attr"), sem("ld_x"), sem("ld_const")
        ld_w, ld_w0 = sem("ld_w"), sem("ld_w0")
        padded = sem("padded")
        zeroed = sem("zeroed")
        ld_typ = [sem("ld_typ0"), sem("ld_typ1")]
        turned = sem("turned")
        turned_out = sem("turned_out")
        dve_own = sem("dve_own")
        hots = sem("hots")
        chunk_mm = sem("chunk_mm")
        coef_out = sem("coef_out")
        deg_mm, deg_row, deg_t = sem("deg_mm"), sem("deg_row"), sem("deg_t")
        vec_done = sem("vec_done")
        root_done = sem("root_done")
        scale_done = sem("scale_done")
        wprep = sem("wprep")
        h_done = sem("h_done")
        h_turned = sem("h_turned")
        hT_out = sem("hT_out")
        node_mm = sem("node_mm")
        node_ev = sem("node_ev")
        st_tab = [sem("st_tab0"), sem("st_tab1")]
        ld_acc = [sem("ld_acc0"), sem("ld_acc1")]
        acc_used = sem("acc_used")
        x_done = sem("x_done")
        emb_ld, emb_v, emb_a, emb_ok = sem("emb_ld"), sem("emb_v"), sem("emb_a"), sem("emb_ok")
        st_out = sem("st_out")
        rows_ok = sem("rows_ok")
        mids_own, mids_own2 = sem("mids_own"), sem("mids_own2")
        fold_own, fold_t, fold_c, fold_mm = sem("fold_own"), sem("fold_t"), sem("fold_c"), sem("fold_mm")
        layer = []
        for n in range(2):
            layer.append({k: sem(f"{k}_l{n}") for k in (
                "staged",
                "spread",
                "same_ok",
                "ranked",
                "sidx_ok",
                "scaled",
                "mids_ok",
                "summed",
                "sum_ok",
                "out_free",
                "let_go",
                "sidx_tmp",
                "drained",
                "h0_mm", "h0_ok", "h1_mm", "h1_ok", "w_mm",
            )} | {"got": [sem(f"got{i}_l{n}") for i in range(GSLOT)],
                  "added": [sem(f"added{i}_l{n}") for i in range(TPS)]})

        def hold(eng):
            eng.wait_ge(padded, 1)

        block = ctx.enter_context(nc.Block())
        full = 12 * P * P
        more = EDGES // P - 12 * P
        tail = EDGES % P

        @block.sync
        def _(sp):
            sp.dma_start(ident[:, :], a["c_ident"]).then_inc(ld_const, 16)
            sp.dma_start(iota[:, :], a["c_iota"]).then_inc(ld_const, 16)
            sp.dma_start(pcol[:, :], a["c_pcol"]).then_inc(ld_const, 16)
            sp.wait_ge(padded, 1)
            sp.dma_start(table[0:NREL, :], a["L0_gnn_comps"]).then_inc(ld_const, 16)
            sp.dma_start(alpha[0:NREL, :], a["L0_gnn_alpha"]).then_inc(ld_const, 16)
            for v, name, w in ((src_rows, "src", 1), (dst_rows, "dst", 1), (attr_rows, "edge_attr_3", 3)):
                d = a[name] if w == 1 else a[name].rearrange("e c -> (e c)")
                s = ld_edge if w == 1 else ld_attr
                sp.dma_start(v[:, 0:12, :], d[0:full * w].rearrange("(j q e) -> q j e", q=P, e=P * w)).then_inc(s, 16)
                sp.dma_start(v[0:more, 12, :], d[full * w:(full + more * P) * w].rearrange("(q e) -> q e", e=P * w)).then_inc(s, 16)
                sp.dma_start(v[more:more + 1, 12, 0:tail * w], d[(full + more * P) * w:EDGES * w].rearrange("(q e) -> q e", q=1)).then_inc(s, 16)
            whole, rest = NODES // P, NODES % P
            sp.dma_start(xn[:, 0:whole, :], a["x"][0:whole * P, :].rearrange("(t p) d -> p t d", p=P)).then_inc(ld_x, 16)
            sp.dma_start(xn[0:rest, whole, :], a["x"][whole * P:NODES, :]).then_inc(ld_x, 16)
            sp.dma_start(bases[:, :, :], a["L0_gnn_bases"].rearrange("b d f -> d b f")).then_inc(ld_w, 16)
            sp.dma_start(w_up[0:MUL, 0:MUL], a["L1_gnn_W_up0"]).then_inc(ld_w, 16)
            for c in range(3):
                sp.dma_start(w_up[MUL + c:MUL + c + 3 * (MUL - 1) + 1:3, MUL * (c + 1):MUL * (c + 2)], a["L1_gnn_W_up1"]).then_inc(ld_w, 16)
            for q in range(GROUPS // 2):
                for h in range(2):
                    r = 2 * CENTERS * q + CENTERS * h
                    sp.dma_start(w_m0[r:r + CENTERS, q, HID * h:HID * (h + 1)], a["L1_gnn_mlp_w0"]).then_inc(ld_w0, 16)
            for h in range(2):
                r = slice(HID * h, HID * (h + 1))
                sp.dma_start(w_m1[r, r], a["L1_gnn_mlp_w1"]).then_inc(ld_w, 16)
                sp.dma_start(w_m2[r, h, :], a["L1_gnn_mlp_w2"]).then_inc(ld_w, 16)
                sp.dma_start(b_m[r, 0:1], a["L1_gnn_mlp_b0"].rearrange("(p o) -> p o", o=1)).then_inc(ld_w, 16)
                sp.dma_start(b_m[r, 1:2], a["L1_gnn_mlp_b1"].rearrange("(p o) -> p o", o=1)).then_inc(ld_w, 16)
                sp.dma_start(w_o1[r, :], a["L1_gnn_W_out1"]).then_inc(ld_w, 16)
            sp.dma_start(b2_row[:, :], a["L1_gnn_mlp_b2"].rearrange("(o f) -> o f", o=1)).then_inc(ld_w, 16)
            sp.dma_start(w_o[0:2 * MUL, 0, 0:MUL], a["L1_gnn_W_out0"]).then_inc(ld_w, 16)

            def clear(acc, r, w):
                k = NPAD * w // P // 800
                sp.dma_start(acc.rearrange("(p r) d -> p (r d)", p=P).rearrange("p (k x) -> p k x", k=k),
                             zero[:, :].unsqueeze(1).to_broadcast([P, k, 800])).then_inc(zeroed, 16)

            def types(b, e0, n):
                sp.dma_start(typ[:, b, 0:n], a["edge_type_50"].rearrange("(o e) -> o e", o=1)[:, bass.ds(e0, n)].to_broadcast([64, n])).then_inc(ld_typ[b], 16)
            types(0, 0, CHUNK * P)
            types(1, CHUNK * P, CHUNK * P)
            with sp.Fori(1, NCH // 2 - 1) as c:
                for b in range(2):
                    sp.wait_ge(hots, c * 2 + (b - 1))
                    types(b, c * (2 * CHUNK * P) + b * CHUNK * P, CHUNK * P)
            sp.wait_ge(hots, NCH - 3)
            types(0, (NCH - 2) * CHUNK * P, CHUNK * P)
            sp.wait_ge(padded, 2)
            types(1, (NCH - 1) * CHUNK * P, EDGES - (NCH - 1) * CHUNK * P)
            for r in range(TPS):
                clear(acc0[r], r, D)
                clear(acc1[r], r, 2 * D)

            def tables(tab, w, base):
                with sp.Fori(0, NT // 2) as t:
                    for b in range(2):
                        sp.wait_ge(node_ev, t * 2 + (base + b + 1))
                        sp.dma_start(tab[bass.ds(t * (2 * P) + b * P, P), :], node_out[:, b, 0:w]).then_inc(st_tab[b], 16)
            tables(ytab, NB * D, 0)
            for i in range(TPS):
                sp.wait_ge(layer[0]["added"][i], 16 * STEPS)
            for k in range(NT // DB):
                if k >= 2:
                    sp.wait_ge(acc_used, k - 1)
                for r in range(TPS):
                    sp.dma_start(accin[:, k % 2, r, :].rearrange("p (t d) -> p t d", t=DB),
                                 acc0[r][k * DB * P:(k + 1) * DB * P, :].rearrange("(t p) d -> p t d", p=P)).then_inc(ld_acc[k % 2], 16)
            tables(xtab, D, NT)
            sp.wait_ge(emb_v, 1)
            for g in range(GROUPS):
                n = min(EPG, EDGES - g * EPG)
                sp.dma_start(emb[CENTERS * g:CENTERS * (g + 1), 0:n],
                             a["edge_weight"].rearrange("(o e) -> o e", o=1)[:, g * EPG:g * EPG + n].to_broadcast([CENTERS, n])).then_inc(emb_ld, 16)
            for i in range(TPS):
                sp.wait_ge(layer[1]["added"][i], 16 * STEPS)
            sp.wait_ge(layer[1]["w_mm"], STEPS + 1)

            def bring(t, b):
                for r in range(TPS):
                    sp.dma_start(arena[:, (b * TPS + r) * 2 * D:(b * TPS + r + 1) * 2 * D], acc1[r][bass.ds(t * P, P), :]).then_inc(ld_acc[b], 16)
            bring(0, 0)
            bring(1, 1)
            with sp.Fori(1, NT // 2) as t:
                for b in range(2):
                    sp.wait_ge(fold_c, t * 2 + (b - 1))
                    bring(t * 2 + b, b)
            sp.wait_ge(x_done, NT)
            sp.dma_start(out[0:whole * P, :].rearrange("(t p) d -> p t d", p=P), xn[:, 0:whole, :]).then_inc(st_out, 16)
            sp.dma_start(out[whole * P:NODES, :], xn[0:rest, whole, :]).then_inc(st_out, 16)
            sp.wait_ge(st_out, 32)

        def pool_layer(pool, L, tab, acc, w, gat, zero_count):
            S = layer[L]

            def gather(j, s):
                slot = s % GSLOT
                pool.wait_ge(S["staged"], j * RING + (s + 1))
                pool.sem_inc(S["let_go"], 1)
                for i in range(TPS):
                    pool.indirect_dma_start(gat[:, slot, i, :], None, tab,
                                            bass.IndirectOffsetOnAxis(ap=gidx[:, s % RING, i:i + 1], axis=0)).then_inc(S["got"][slot], 16)

            for b in range(2):
                pool.wait_ge(st_tab[b], 16 * (L + 1) * (NT // 2))
            pool.wait_ge(zeroed, 16 * zero_count)
            for s in range(AHEAD):
                gather(0, s)
            with pool.Fori(0, PASSES) as j:
                for q in range(RING):
                    hold(pool)
                    pool.wait_ge(S["summed"], j * RING + q)
                    gather(j, q + AHEAD)
                    pool.wait_ge(S["sidx_ok"], j * RING + (q + 1))
                    for i in range(TPS):
                        pool.wait_ge(S["added"][i], j * (16 * RING) + 16 * q)
                    pool.sem_inc(S["out_free"], 1)
                    hold(pool)
                    pool.wait_ge(S["sum_ok"], j * RING + (q + 1))
                    for i in range(TPS):
                        pool.indirect_dma_start(acc[i], bass.IndirectOffsetOnAxis(ap=sidx[:, q % TPS, i:i + 1], axis=0),
                                                sum_out[:, q % 2, i, 0:w], None, compute_op=ALU.add).then_inc(S["added"][i], 16)
            for i in range(GSLOT):
                pool.wait_ge(S["got"][i], 16 * TPS * (STEPS // GSLOT + (1 if i < AHEAD else 0)))
            pool.sem_inc(S["drained"], 1)

        @block.gpsimd
        def _(pool):
            pool_layer(pool, 0, ytab, acc0, D, gat0, 2 * TPS)
            pool_layer(pool, 1, xtab, acc1, 2 * D, gat1, 2 * TPS)

        @block.scalar
        def _(act):
            def coef_copy(c, col, b):
                act.wait_ge(chunk_mm, c + 1)
                nc.scalar.copy(coef_mem[:, bass.ds(col, CHUNK * NB)], bank[b][:, 0:CHUNK * NB]).then_inc(coef_out, 1)
            with act.Fori(0, NCH // 2) as c:
                for b in range(2):
                    coef_copy(c * 2 + b, c * (2 * CHUNK * NB) + b * CHUNK * NB, b)

            def roots(v, n):
                act.wait_ge(vec_done, n)
                nc.scalar.activation(v, v, ACT.Sqrt).then_inc(root_done, 1)
            roots(dinv[:, :], 1)
            roots(rstd[:, :], 2)
            roots(lo_f[:, :], 3)

            def node_rows(base, w):
                def norm(n, b, start):
                    hold(act)
                    if not start:
                        act.wait_ge(h_turned, n + (base - 1))
                    nc.scalar.activation(hrow[:, b, :], xn[:, bass.ds(n, 1), :].rearrange("p o d -> p (o d)"), ACT.Relu,
                                         bias=nbias[:, bass.ds(n, 1)], scale=rstd[:, bass.ds(n, 1)]).then_inc(h_done, 1)

                def evict(n, t, b):
                    act.wait_ge(node_mm, n + (base + 1))
                    act.wait_ge(st_tab[b], t * 16 + 16 * (base // 2))
                    nc.scalar.copy(node_out[:, b, 0:w], bank[4 + b][:, 0:w]).then_inc(node_ev, 1)
                for b in range(2):
                    norm(b, b, True)
                with act.Fori(0, NT // 2 - 1) as t:
                    for b in range(2):
                        evict(t * 2 + b, t, b)
                        norm(t * 2 + (b + 2), b, False)
                for b in range(2):
                    evict(NT - 2 + b, NT // 2 - 1, b)

            act.wait_ge(scale_done, 1)
            act.wait_ge(ld_x, 32)
            node_rows(0, NB * D)

            S = layer[0]
            with act.Fori(0, PASSES) as j:
                for q in range(RING):
                    hold(act)
                    act.wait_ge(S["got"][q % GSLOT], j * (16 * TPS * RING // GSLOT) + 16 * TPS * (q // GSLOT + 1))
                    for i in range(TPS):
                        for b in range(NB):
                            g = gat0[:, q % GSLOT, i, b * D:(b + 1) * D]
                            last = nc.scalar.mul(g, g, coef_mem[:, bass.ds(j * (RING * TPS * NB) + (q * TPS + i) * NB + b, 1)])
                    last.then_inc(S["scaled"], 1)
                    act.wait_ge(S["summed"], j * RING + (q + 1))
                    act.wait_ge(S["out_free"], j * RING + q)
                    nc.scalar.copy(sum_out[:, q % 2, :, 0:D], bank[q % 2][:, :].rearrange("p (i x) -> p i x", i=TPS)).then_inc(S["sum_ok"], 1)

            roots(rstd[:, :], 4)
            act.wait_ge(scale_done, 2)
            act.wait_ge(layer[0]["drained"], 1)
            node_rows(NT, D)

            for n, (lo, hi) in enumerate(EMB_PARTS):
                act.wait_ge(emb_v, 2 + n)
                nc.scalar.activation(emb[:, lo:hi], emb[:, lo:hi], ACT.Square, bias=pcol[:, 4:5], scale=float(CENTERS - 1)).then_inc(emb_a, 1)
            for n, (lo, hi) in enumerate(EMB_PARTS):
                act.wait_ge(emb_a, n + 1)
                nc.scalar.activation(emb[:, lo:hi], emb[:, lo:hi], ACT.Exp, scale=-0.5).then_inc(emb_a, 1)

            S = layer[1]

            def mlp(n0):
                act.wait_ge(S["h0_mm"], n0)
                nc.scalar.activation(hid0, bank[6][:, 0:256], ACT.Silu, bias=b_m[:, 0:1]).then_inc(S["h0_ok"], 1)
                act.wait_ge(S["h1_mm"], n0)
                nc.scalar.activation(hid1, bank[6][:, 256:512], ACT.Silu, bias=b_m[:, 1:2]).then_inc(S["h1_ok"], 1)
            mlp(1)
            with act.Fori(0, PASSES) as j:
                for q in range(RING):
                    mlp(j * RING + (q + 2))
                    act.wait_ge(S["summed"], j * RING + (q + 1))
                    act.wait_ge(S["out_free"], j * RING + q)
                    for h in range(2):
                        last = nc.scalar.copy(sum_out[:, q % 2, 2 * h:2 * h + 2, :], bank[h][:, :].rearrange("p (i x) -> p i x", i=2))
                    last.then_inc(S["sum_ok"], 1)

        @block.vector
        def _(dve):
            own = [0]

            def link(ins):
                own[0] += 1
                ins.then_inc(dve_own, 1)
                dve.wait_ge(dve_own, own[0])

            V = nc.vector
            V.memset(src_rows[:, 12, :], PAD_NODE)
            V.memset(dst_rows[:, 12, :], PAD_NODE)
            V.memset(attr_rows[:, 12, :], 0.0)
            V.memset(xn[:, NODES // P:NT, :], 0.0)
            V.memset(w_up[:, :], 0.0)
            V.memset(w_m0[:, :, :], 0.0)
            V.memset(w_m1[:, :], 0.0)
            V.memset(w_m2[:, :, :], 0.0)
            V.memset(b2_four[:, :, :], 0.0)
            V.memset(w_o[:, :, :], 0.0)
            V.memset(table[:, :], 0.0)
            V.memset(alpha[:, :], 0.0)
            link(V.memset(zero[:, :], 0.0))
            V.memset(zero_b[:, :], 0.0)
            V.memset(ones[:, :], 1.0).then_inc(padded, 1)
            dve.wait_ge(ld_const, 80)
            link(V.tensor_scalar(table[:, :], table[:, :], alpha[:, 0:1], None, ALU.mult))

            dve.wait_ge(ld_edge, 96)
            ids = 2 * BLOCKS * P
            V.tensor_copy(arena[:, 0:ids], rows_i[:, 0:ids]).then_inc(rows_ok, 1)
            n = 0
            for f in range(5):
                for b0 in range(0, BLOCKS, 4):
                    k = min(4, BLOCKS - b0)
                    dve.wait_ge(turned, n + 1)
                    V.tensor_copy(edge[:, b0 * P:(b0 + k) * P, f], bank[n % 4][:, 0:k * P]).then_inc(turned_out, 1)
                    n += 1
                if f == 0:
                    dve.wait_ge(turned_out, n)
                    ii = lo_f[:, :].bitcast(I32)
                    hh = hi_f[:, :].bitcast(I32)
                    link(V.tensor_copy(ii, edge[:, :, 0]))
                    link(V.tensor_scalar(hh, ii, 7, None, ALU.logical_shift_right))
                    link(V.tensor_scalar(ii, ii, 127, None, ALU.bitwise_and))
                    link(V.tensor_copy(hi_f[:, :], hh))
                    link(V.tensor_copy(lo_f[:, :], ii))
            dve.wait_ge(turned_out, n)

            def chunk(c, t0, b, nld, free):
                dve.wait_ge(ld_typ[b], nld)
                if free is not None:
                    dve.wait_ge(chunk_mm, free)
                V.tensor_scalar(typ_hot[:, b, :], typ[:, b, :], pcol[0:64, 0:1], None, ALU.is_equal)
                V.tensor_tensor(lo_hot[:, b, :, :], iota[:, :].unsqueeze(1).to_broadcast([P, CHUNK, P]),
                                lo_f[:, bass.ds(t0, CHUNK)].unsqueeze(2).to_broadcast([P, CHUNK, P]), ALU.is_equal)
                V.tensor_tensor(hi_hot[:, b, :, 0:NT], iota[:, 0:NT].unsqueeze(1).to_broadcast([P, CHUNK, NT]),
                                hi_f[:, bass.ds(t0, CHUNK)].unsqueeze(2).to_broadcast([P, CHUNK, NT]), ALU.is_equal).then_inc(hots, 1)
            chunk(0, 0, 0, 16, None)
            chunk(1, CHUNK, 1, 16, None)
            with dve.Fori(1, NCH // 2 - 1) as c:
                for b in range(2):
                    chunk(c, c * (2 * CHUNK) + b * CHUNK, b, c * 16 + 16, c * 2 + (b - 1))
            chunk(0, (NCH - 2) * CHUNK, 0, 16 * NCH // 2, NCH - 3)
            dve.wait_ge(hots, NCH - 2)
            V.memset(typ[:, 1, EDGES - (NCH - 1) * CHUNK * P:], 0).then_inc(padded, 1)
            dve.wait_ge(padded, 2)
            chunk(0, (NCH - 1) * CHUNK, 1, 16 * NCH // 2, NCH - 2)

            dve.wait_ge(deg_mm, 1)
            V.tensor_copy(deg[:, :], bank[2][0:NT, 0:P]).then_inc(deg_row, 1)
            dve.wait_ge(deg_t, 1)
            link(V.tensor_scalar(dpos[:, :], bank[3][:, 0:NT], 0.0, None, ALU.is_gt))
            V.tensor_scalar(dinv[:, :], bank[3][:, 0:NT], 1.0, None, ALU.max).then_inc(vec_done, 1)

            mean, gap, var = (moment[:, k, :] for k in range(3))

            def statistics(n_vec, with_deg):
                with dve.Fori(0, NT // DB) as k:
                    for t in range(DB):
                        V.bn_stats(stats[:, bass.ds(k * DB + t, 1), :].rearrange("p o s -> p (o s)"),
                                   xn[:, bass.ds(k * DB + t, 1), :].rearrange("p o d -> p (o d)"))
                link(V.memset(dupd[:, :], 0.0))
                V.tensor_tensor(mean, stats[:, :, 1], stats[:, :, 4], ALU.add)
                V.tensor_tensor(var, stats[:, :, 2], stats[:, :, 5], ALU.add)
                link(V.tensor_tensor(gap, stats[:, :, 1], stats[:, :, 4], ALU.subtract))
                link(V.tensor_tensor(gap, gap, gap, ALU.mult))
                V.tensor_scalar(mean, mean, 0.5, None, ALU.mult)
                link(V.scalar_tensor_tensor(var, gap, D / 4.0, var, ALU.mult, ALU.add))
                V.tensor_scalar(rstd[:, :], var, 1.0 / D, EPS, ALU.mult, ALU.add).then_inc(vec_done, 1)
                dve.wait_ge(root_done, n_vec)
                link(V.reciprocal(rstd[:, :], rstd[:, :]))
                if with_deg:
                    link(V.reciprocal(dinv[:, :], dinv[:, :]))
                    link(V.tensor_tensor(dinv[:, :], dinv[:, :], dpos[:, :], ALU.mult))
                    link(V.tensor_tensor(rstd[:, :], rstd[:, :], dinv[:, :], ALU.mult))
                V.scalar_tensor_tensor(nbias[:, :], mean, -1.0, rstd[:, :], ALU.mult, ALU.mult).then_inc(scale_done, 1)

            dve.wait_ge(ld_x, 32)
            statistics(2, True)

            ex = [edge[:, :, 2 + c] for c in range(3)]
            link(V.tensor_tensor(lo_f[:, :], ex[0], ex[0], ALU.mult))
            for c in (1, 2):
                link(V.tensor_tensor(hi_f[:, :], ex[c], ex[c], ALU.mult))
                link(V.tensor_tensor(lo_f[:, :], lo_f[:, :], hi_f[:, :], ALU.add))
            V.tensor_scalar(lo_f[:, :], lo_f[:, :], 1.3e-35, None, ALU.max).then_inc(vec_done, 1)
            dve.wait_ge(root_done, 3)
            link(V.tensor_scalar(lo_f[:, :], lo_f[:, :], 1e-12, None, ALU.add))
            link(V.reciprocal(hi_f[:, :], lo_f[:, :]))
            for c in range(3):
                last = V.tensor_tensor(ex[c], ex[c], hi_f[:, :], ALU.mult)
            link(last)

            dve.wait_ge(ld_w, 16 * 17)
            dve.wait_ge(ld_w0, 16 * GROUPS)
            V.tensor_scalar(w_up[:, :], w_up[:, :], MUL ** -0.5, None, ALU.mult)
            V.tensor_scalar(w_m0[:, :, :], w_m0[:, :, :], CENTERS ** 0.5, None, ALU.mult)
            V.tensor_scalar(w_m2[:, :, MUL:2 * MUL], w_m2[:, :, MUL:2 * MUL], SQ3, None, ALU.mult)
            link(V.tensor_scalar(b2_row[:, MUL:2 * MUL], b2_row[:, MUL:2 * MUL], SQ3, None, ALU.mult))
            V.tensor_copy(b2_four[0:1, :, :], b2_row[:, :].unsqueeze(1).to_broadcast([1, TPS, D]))
            out_scale = (2 * MUL) ** -0.5 / 16.0
            h0, h1 = slice(0, 2 * MUL), slice(2 * MUL, 4 * MUL)
            V.tensor_scalar(w_o[h0, 0, 0:MUL], w_o[h0, 0, 0:MUL], out_scale, None, ALU.mult)
            V.tensor_scalar(w_o[h1, 0, MUL:D:3], w_o1[h1, :], out_scale, None, ALU.mult)
            V.tensor_scalar(w_o[h0, 1, MUL + 1:D:3], w_o1[h0, :], out_scale, None, ALU.mult)
            V.tensor_scalar(w_o[h1, 1, MUL + 2:D:3], w_o1[h1, :], out_scale, None, ALU.mult).then_inc(wprep, 1)

            def turned_rows(base):
                def pair(t, start):
                    for b in range(2):
                        if not start:
                            dve.wait_ge(node_mm, t * 2 + (base + b - 1))
                        dve.wait_ge(h_turned, t * 2 + (base + b + 1))
                        V.tensor_copy(hrowT[:, b, :], bank[6 + b][:, 0:P]).then_inc(hT_out, 1)
                pair(0, True)
                with dve.Fori(1, NT // 2) as t:
                    pair(t, False)

            turned_rows(0)

            def layer_steps(L, stage, body):
                S = layer[L]

                def same_rows(q):
                    tgt = st_edge[:, q % RING, :, L:L + 1]
                    V.tensor_tensor(same[:, q % 2, :, :], bank[2][:, :].rearrange("p (i x) -> p i x", i=TPS),
                                    tgt.to_broadcast([P, TPS, P]), ALU.is_equal).then_inc(S["same_ok"], 1)

                def scatter_rows(j, q):
                    dve.wait_ge(S["ranked"], j * RING + (q + 1))
                    dve.wait_ge(S["sidx_ok"], j * RING + q)
                    V.tensor_scalar(dupd[:, :], bank[3][:, TPS * (q % 2):TPS * (q % 2) + TPS], pcol[:, 2:3], pcol[:, 3:4], ALU.is_gt, ALU.mult).then_inc(S["sidx_tmp"], 1)
                    dve.wait_ge(S["sidx_tmp"], j * RING + (q + 1))
                    V.tensor_tensor(sidx[:, q % TPS, :], dupd[:, :], st_edge[:, q % RING, :, L], ALU.max).then_inc(S["sidx_ok"], 1)

                for s in range(AHEAD + 1):
                    stage(0, s)
                dve.wait_ge(S["spread"], 1)
                same_rows(0)
                scatter_rows(0, 0)
                with dve.Fori(0, PASSES) as j:
                    for q in range(RING):
                        hold(dve)
                        dve.wait_ge(S["summed"], j * RING + q)
                        stage(j, q + AHEAD + 1)
                        dve.wait_ge(S["spread"], j * RING + (q + 2))
                        same_rows(q + 1)
                        body(j, q)
                        dve.wait_ge(S["out_free"], j * RING + q)
                        scatter_rows(j, q + 1)

            S0, S1 = layer

            def stage0(j, s):
                c0 = (j * (RING * TPS)) + s * TPS
                V.tensor_copy(st_edge[:, s % RING, :, 0:2], edge[:, bass.ds(c0, TPS), 0:2])
                V.tensor_copy(gidx[:, s % RING, :], edge[:, bass.ds(c0, TPS), 1]).then_inc(S0["staged"], 1)
            layer_steps(0, stage0, lambda j, q: None)

            for k in range(NT // DB):
                dve.wait_ge(ld_acc[k % 2], 16 * TPS * (k // 2 + 1))
                w = accin[:, k % 2, :, :]
                V.tensor_tensor(w[:, 0, :], w[:, 0, :], w[:, 1, :], ALU.add)
                link(V.tensor_tensor(w[:, 2, :], w[:, 2, :], w[:, 3, :], ALU.add))
                link(V.tensor_tensor(w[:, 0, :], w[:, 0, :], w[:, 2, :], ALU.add))
                for t in range(DB):
                    n = k * DB + t
                    last = V.scalar_tensor_tensor(xn[:, n, :], w[:, 0, t * D:(t + 1) * D], dinv[:, n:n + 1], xn[:, n, :], ALU.mult, ALU.add)
                last.then_inc(acc_used, 1)
            dve.wait_ge(acc_used, NT // DB)
            statistics(4, False)
            V.memset(emb[:, :], 0.0).then_inc(emb_v, 1)
            turned_rows(NT)
            dve.wait_ge(emb_ld, 16 * GROUPS)
            for n, (lo, hi) in enumerate(EMB_PARTS):
                link(V.tensor_scalar(gmem[:, 4096:4096 + hi - lo], emb[:, lo:hi], 1.0, 1e9, ALU.is_gt, ALU.mult))
                link(V.tensor_scalar(emb[:, lo:hi], emb[:, lo:hi], 0.0, 1.0, ALU.max, ALU.min))
                V.tensor_tensor(emb[:, lo:hi], emb[:, lo:hi], gmem[:, 4096:4096 + hi - lo], ALU.add).then_inc(emb_v, 1)
                dve.wait_ge(emb_v, n + 2)

            def stage1(j, s):
                q = s % RING
                for g in range(2):
                    c0 = (j + s // RING) * 2 + (2 * q + g) * TPG
                    V.tensor_copy(st_edge[:, q, 2 * g:2 * g + 2, :], edge[:, bass.ds(c0, 2), :])
                    last = V.tensor_copy(gidx[:, q, 2 * g:2 * g + 2], edge[:, bass.ds(c0, 2), 0])
                last.then_inc(S1["staged"], 1)

            def mids(j, q):
                w = bank[4 + q % 2][:, :].rearrange("p (i x) -> p i x", i=TPS)
                g = gat1[:, q % GSLOT, :, :]
                gv = g[:, :, MUL:].rearrange("p i (c k) -> p i c k", c=3)
                m = mid[:, q % 2, :, :]
                mc = m[:, :, 2 * MUL:].rearrange("p i (c k) -> p i c k", c=3)
                unit = st_edge[:, q % RING, :, 2:5].unsqueeze(3).to_broadcast([P, TPS, 3, MUL])
                own1 = j * (3 * RING) + 3 * q
                dve.wait_ge(S1["got"][q % GSLOT], j * (16 * TPS * RING // GSLOT) + 16 * TPS * (q // GSLOT + 1))
                V.tensor_tensor(vdot[:, :, :, :], gv, unit, ALU.mult).then_inc(mids_own, 1)
                dve.wait_ge(S1["w_mm"], j * RING + (q + 1))
                V.tensor_tensor(w01s, w[:, :, MUL:2 * MUL], g[:, :, 0:MUL], ALU.mult).then_inc(mids_own, 1)
                V.tensor_tensor(m[:, :, 0:MUL], w[:, :, 0:MUL], g[:, :, 0:MUL], ALU.mult)
                V.tensor_tensor(mc[:, :, :, MUL:], w[:, :, 2 * MUL:3 * MUL].unsqueeze(2).to_broadcast([P, TPS, 3, MUL]), gv, ALU.mult)
                dve.wait_ge(mids_own, own1 + 1)
                V.tensor_tensor(vsum[:, :, 0, :], vdot[:, :, 0, :], vdot[:, :, 1, :], ALU.add).then_inc(mids_own, 1)
                dve.wait_ge(mids_own, own1 + 2)
                V.tensor_tensor(mc[:, :, :, 0:MUL], w01s.unsqueeze(2).to_broadcast([P, TPS, 3, MUL]), unit, ALU.mult)
                dve.wait_ge(mids_own, own1 + 3)
                V.tensor_tensor(vsum[:, :, 1, :], vsum[:, :, 0, :], vdot[:, :, 2, :], ALU.add).then_inc(mids_own2, 1)
                dve.wait_ge(mids_own2, j * RING + (q + 1))
                V.tensor_tensor(m[:, :, MUL:2 * MUL], w[:, :, 3 * MUL:], vsum[:, :, 1, :], ALU.mult).then_inc(S1["mids_ok"], 1)
            layer_steps(1, stage1, mids)

            def fold(t, n, b):
                dve.wait_ge(ld_acc[b], t * (16 * TPS) + 16 * TPS * (NT // DB // 2 + 1))
                w = arena[:, b * TPS * 2 * D:(b + 1) * TPS * 2 * D].rearrange("p (r x) -> p r x", r=TPS)
                V.tensor_tensor(w[:, 0, :], w[:, 0, :], w[:, 1, :], ALU.add).then_inc(fold_own, 1)
                V.tensor_tensor(w[:, 2, :], w[:, 2, :], w[:, 3, :], ALU.add).then_inc(fold_own, 1)
                dve.wait_ge(fold_own, n * 3 + 2)
                V.tensor_tensor(w[:, 0, :], w[:, 0, :], w[:, 2, :], ALU.add).then_inc(fold_own, 1)
                dve.wait_ge(fold_t, n + 1)
                V.tensor_copy(tT[:, :], bank[6][:, 0:2 * D]).then_inc(fold_c, 1)
                dve.wait_ge(fold_mm, n + 1)
                x = xn[:, bass.ds(n, 1), :].rearrange("p o d -> p (o d)")
                V.tensor_tensor(x, bank[4][:, 0:D], x, ALU.add).then_inc(x_done, 1)
            with dve.Fori(0, NT // 2) as t:
                for b in range(2):
                    fold(t, t * 2 + b, b)

        @block.tensor
        def _(pe):
            T = nc.tensor
            pe.wait_ge(ld_const, 80)
            n = 0
            for f in range(5):
                if f == 0:
                    pe.wait_ge(rows_ok, 1)
                if f == 2:
                    pe.wait_ge(ld_attr, 48)
                for b0 in range(0, BLOCKS, 4):
                    k = min(4, BLOCKS - b0)
                    if n >= 4:
                        pe.wait_ge(turned_out, n - 3)
                    for b in range(b0, b0 + k):
                        r = arena[:, f * BLOCKS * P + b * P:f * BLOCKS * P + (b + 1) * P] if f < 2 else \
                            attr_rows[:, b, f - 2:3 * P:3]
                        last = T.transpose(bank[n % 4][:, (b - b0) * P:(b - b0 + 1) * P], r, ident[:, :])
                    last.then_inc(turned, 1)
                    n += 1
            pe.wait_ge(turned_out, n)

            T.matmul(bank[2][0:NT, 0:P], zero_b[:, 0:NT], zero_b[:, :], start=True, stop=False)

            def chunk(c, b, free):
                pe.wait_ge(hots, c + 1)
                if free:
                    pe.wait_ge(coef_out, c - 1)
                for i in range(CHUNK):
                    T.matmul(bank[b][:, i * NB:(i + 1) * NB], typ_hot[:, b, i * P:(i + 1) * P], table[:, :], start=True, stop=True)
                for i in range(CHUNK):
                    last = T.matmul(bank[2][0:NT, 0:P], hi_hot[:, b, i, 0:NT], lo_hot[:, b, i, :], start=False, stop=False)
                last.then_inc(chunk_mm, 1)
            chunk(0, 0, False)
            chunk(1, 1, False)
            with pe.Fori(1, NCH // 2) as c:
                for b in range(2):
                    chunk(c * 2 + b, b, True)
            T.matmul(bank[2][0:NT, 0:P], zero_b[:, 0:NT], zero_b[:, :], start=False, stop=True).then_inc(deg_mm, 1)
            pe.wait_ge(deg_row, 1)
            T.transpose(bank[3][:, 0:NT], deg[:, :], ident[0:NT, 0:NT]).then_inc(deg_t, 1)

            def node_product(base, weights, w):
                def turn(n, b, start):
                    pe.wait_ge(h_done, n + (base + 1))
                    if not start:
                        pe.wait_ge(hT_out, n + (base - 1))
                    T.transpose(bank[6 + b][:, 0:P], hrow[:, b, :], ident[:, :]).then_inc(h_turned, 1)

                def pair(t, start, end):
                    for b in range(2):
                        pe.wait_ge(hT_out, t * 2 + (base + b + 1))
                        if not start:
                            pe.wait_ge(node_ev, t * 2 + (base + b - 1))
                        T.matmul(bank[4 + b][:, 0:w], hrowT[:, b, :], weights, start=True, stop=True).then_inc(node_mm, 1)
                        if not end:
                            turn(t * 2 + (b + 2), b, False)
                for b in range(2):
                    turn(b, b, True)
                pair(0, True, False)
                with pe.Fori(1, NT // 2 - 1) as t:
                    pair(t, False, False)
                pair(NT // 2 - 1, False, True)

            pe.wait_ge(ld_w, 16 * 17)
            pe.wait_ge(wprep, 1)
            node_product(0, bases[:, :, :].rearrange("p b d -> p (b d)"), NB * D)

            def layer_steps(L, pre, data):
                S = layer[L]

                def spread(j, q):
                    pe.wait_ge(S["staged"], j * RING + (q + 1))
                    pe.wait_ge(S["same_ok"], j * RING + q)
                    for i in range(TPS):
                        last = T.transpose(bank[2][:, i * P:(i + 1) * P], st_edge[:, q % RING, i, L:L + 1].to_broadcast([P, P]), ident[:, :])
                    last.then_inc(S["spread"], 1)

                def rank(j, q):
                    pe.wait_ge(S["same_ok"], j * RING + (q + 1))
                    pe.wait_ge(S["sidx_ok"], j * RING + (q - 1 if q else 0))
                    for i in range(TPS):
                        last = T.matmul(bank[3][:, TPS * (q % 2) + i:TPS * (q % 2) + i + 1], same[:, q % 2, i, :], pcol[:, 1:2], start=True, stop=True)
                    last.then_inc(S["ranked"], 1)

                spread(0, 0)
                pre(0, 0)
                rank(0, 0)
                with pe.Fori(0, PASSES) as j:
                    for q in range(RING):
                        spread(j, q + 1)
                        pre(j, q + 1)
                        rank(j, q + 1)
                        data(j, q)

            S0, S1 = layer

            def sum0(j, q):
                pe.wait_ge(S0["scaled"], j * RING + (q + 1))
                pe.wait_ge(S0["sum_ok"], j * RING + (q - 1 if q else 0))
                for i in range(TPS):
                    for b in range(NB):
                        last = T.matmul(bank[q % 2][:, i * D:(i + 1) * D], same[:, q % 2, i, :], gat0[:, q % GSLOT, i, b * D:(b + 1) * D], start=(b == 0), stop=(b == NB - 1))
                last.then_inc(S0["summed"], 1)
            layer_steps(0, lambda j, q: None, sum0)

            node_product(NT, w_up[:, :], D)

            def mlp(j, q):
                q8 = q % RING
                pe.wait_ge(S1["h1_ok"], j * RING + q)
                T.matmul(bank[6][:, 0:256], w_m0[:, q8, :], emb[:, bass.ds((j + q // RING) * 256, 256)], start=True, stop=True).then_inc(S1["h0_mm"], 1)
                pe.wait_ge(S1["h0_ok"], j * RING + (q + 1))
                T.matmul(bank[6][:, 256:512], w_m1[:, :], hid0, start=True, stop=True).then_inc(S1["h1_mm"], 1)
                pe.wait_ge(S1["h1_ok"], j * RING + (q + 1))
                pe.wait_ge(S1["mids_ok"], j * RING + (q - 1 if q else 0))
                wb = bank[4 + q % 2]
                T.matmul(wb[:, :], ones[:, :], b2_four[:, :, :].rearrange("o i d -> o (i d)"), start=True, stop=False)
                for i in range(TPS):
                    last = T.matmul(wb[:, i * P:(i + 1) * P], hid1[:, (i % 2) * P:(i % 2 + 1) * P], w_m2[:, i // 2, :], start=False, stop=(i == TPS - 1))
                last.then_inc(S1["w_mm"], 1)

            def sum1(j, q):
                pe.wait_ge(S1["mids_ok"], j * RING + (q + 1))
                pe.wait_ge(S1["sum_ok"], j * RING + q)
                for i in range(TPS):
                    last = T.matmul(bank[i // 2][:, (i % 2) * 2 * D:(i % 2 + 1) * 2 * D], same[:, q % 2, i, :], mid[:, q % 2, i, :], start=True, stop=True)
                last.then_inc(S1["summed"], 1)
            pe.wait_ge(emb_a, 2 * len(EMB_PARTS))
            layer_steps(1, mlp, sum1)

            def fold(n, b):
                pe.wait_ge(fold_own, n * 3 + 3)
                pe.wait_ge(fold_c, n)
                for h in range(2):
                    c0 = b * TPS * 2 * D + h * D
                    last = T.transpose(bank[6][:, h * P:(h + 1) * P], arena[:, c0:c0 + D], ident[:, :])
                last.then_inc(fold_t, 1)
                pe.wait_ge(fold_c, n + 1)
                pe.wait_ge(x_done, n)
                for h in range(2):
                    last = T.matmul(bank[4][:, 0:D], tT[:, h * P:(h + 1) * P], w_o[:, h, :], start=(h == 0), stop=(h == 1))
                last.then_inc(fold_mm, 1)
            with pe.Fori(0, NT // 2) as t:
                for b in range(2):
                    fold(t * 2 + b, b)


INPUTS = ("x", "src", "dst", "edge_attr_3", "edge_type_50", "edge_weight", "L0_gnn_bases", "L0_gnn_comps",
          "L0_gnn_alpha", "L1_gnn_W_up0", "L1_gnn_W_up1", "L1_gnn_mlp_w0", "L1_gnn_mlp_b0", "L1_gnn_mlp_w1",
          "L1_gnn_mlp_b1", "L1_gnn_mlp_w2", "L1_gnn_mlp_b2", "L1_gnn_W_out0", "L1_gnn_W_out1")


def constants():
    p = np.arange(P)
    pcol = np.zeros((P, 8), np.float32)
    pcol[:, 0] = p
    pcol[:, 1] = 2.0 ** (63 - p)
    pcol[:, 2] = 2.5 * 2.0 ** (63 - p)
    pcol[:, 3] = (NT - 1) * P + p
    pcol[:, 4] = -(p % CENTERS)
    return {"c_ident": np.eye(P, dtype=np.float32), "c_iota": np.tile(p.astype(np.float32), (P, 1)), "c_pcol": pcol}


def kernel(**inputs):
    import concourse.bacc as bacc
    from concourse.bass_utils import run_bass_kernel_spmd

    nc = bacc.Bacc("TRN2", target_bir_lowering=False, num_devices=1)
    arrays = {n: np.ascontiguousarray(inputs[n]) for n in INPUTS} | constants()
    aps = {n: nc.dram_tensor(f"in_{n}", v.shape, mybir.dt.from_np(v.dtype), kind="ExternalInput").ap() for n, v in arrays.items()}
    out = nc.dram_tensor("out", [NODES, D], F32, kind="ExternalOutput").ap()
    build(nc, aps, out)
    r = run_bass_kernel_spmd(nc, [{f"in_{n}": v for n, v in arrays.items()}], core_ids=[0])
    return r.results[0]["out"]
```

```python
import numpy as np
import concourse.bass as bass
import concourse.mybir as mybir
from contextlib import ExitStack

F32, BF16, I32 = mybir.dt.float32, mybir.dt.bfloat16, mybir.dt.int32
ALU = mybir.AluOpType
ACT = mybir.ActivationFunctionType
AXX = mybir.AxisListType.X

P = 128
D = 128
NODES = 6250
NT = -(-NODES // P) + 1
NPAD = NT * P
EDGES = 200000
TPS = 4
RING = 8
GROUPS = 16
TILES = 1568
TPG = TILES // GROUPS
PASSES = TILES // (TPS * RING)
STEPS = TILES // TPS
BLOCKS = 13
COLS = BLOCKS * P
WIN = P // 4
LEAD = 4
EPG = TPG * P
PAD_NODE = NODES
NB = 4
EMB_PARTS = [(n * 3200, (n + 1) * 3200) for n in range(4)]
NREL = 50
CENTERS = 8
HID = 64
MUL = 32
GSLOT = 4
GSLOT0 = 2
CHUNK = 16
NCH = TILES // CHUNK
EPS = 1e-5
DB = 5
SQ3 = 3.0 ** 0.5


def build(nc, a, out):
    ctx = ExitStack()
    with ctx:
        def sb(name, shape, dt=F32):
            return ctx.enter_context(nc.sbuf_tensor(name, shape, dt))

        def ps(name, shape, dt=F32):
            return ctx.enter_context(nc.psum_tensor(name, shape, dt))

        def sem(name):
            return ctx.enter_context(nc.semaphore(name))

        def dram(name, shape):
            return nc.dram_tensor(name, shape, F32, kind="Internal").ap()

        ytab = dram("ytab", [NPAD, NB * D])
        xtab = dram("xtab", [NPAD, D])
        acc0 = [dram(f"acc0_{i}", [NPAD, D]) for i in range(TPS)]
        acc1 = dram("acc1", [NPAD, 2 * D])

        xn = sb("xn", [P, NT, D])
        edge = sb("edge", [P, COLS, 6])
        arena = sb("arena", [P, 12800])
        emb = arena
        rows_i = arena[:, 0:BLOCKS * 5 * P].bitcast(I32)
        src_rows = rows_i[:, 0:BLOCKS * P].rearrange("q (j e) -> q j e", j=BLOCKS)
        dst_rows = rows_i[:, BLOCKS * P:2 * BLOCKS * P].rearrange("q (j e) -> q j e", j=BLOCKS)
        attr_rows = arena[:, 2 * BLOCKS * P:5 * BLOCKS * P].rearrange("q (j e) -> q j e", j=BLOCKS)
        TY0 = BLOCKS * 5 * P
        typ = arena[0:64, TY0:TY0 + 2 * CHUNK * P].bitcast(I32).rearrange("q (b e) -> q b e", b=2)
        accin = arena[:, 0:2 * TPS * DB * D].rearrange("p (b r x) -> p b r x", b=2, r=TPS)
        coef_mem = sb("coef_mem", [P, COLS * NB])
        coef = coef_mem[:, :].rearrange("p (t b) -> p t b", b=NB)
        mid = coef_mem[:, 0:2 * TPS * 2 * D].rearrange("p (s i x) -> p s i x", s=2, i=TPS)
        M0 = 2 * TPS * 2 * D
        hid0 = coef_mem[:, M0:M0 + 256]
        hid1 = coef_mem[:, M0 + 256:M0 + 512]
        w01s = coef_mem[:, M0 + 512:M0 + 640].rearrange("p (i x) -> p i x", i=TPS)
        vdot = coef_mem[:, M0 + 768:M0 + 1152].rearrange("p (i c k) -> p i c k", i=TPS, c=3)
        vsum = coef_mem[:, M0 + 1152:M0 + 1408].rearrange("p (i c k) -> p i c k", i=TPS, c=2)
        gmem = sb("gmem", [P, GSLOT0 * TPS * NB * D])
        gat0 = gmem[:, :].rearrange("p (s i x) -> p s i x", s=GSLOT0, i=TPS)
        gat1 = gmem[:, 0:GSLOT * TPS * D].rearrange("p (s i x) -> p s i x", s=GSLOT, i=TPS)
        OH = 2 * CHUNK * P
        typ_hot = gmem[0:64, 0:OH].rearrange("p (b e) -> p b e", b=2)
        lo_hot = gmem[:, 0:CHUNK * P].bitcast(BF16).rearrange("p (b t x) -> p b t x", b=2, x=P)
        HI0 = CHUNK * P
        hi_hot = gmem[:, HI0:HI0 + CHUNK * NT].bitcast(BF16).rearrange("p (b t x) -> p b t x", b=2, x=NT)
        thot = gmem[0:64, 0:1024].rearrange("p (s e) -> p s e", s=2)
        wedge = gmem[:, 1024:2048].rearrange("p (s i x) -> p s i x", s=2, i=TPS)
        wsum = gmem[:, 2048:3072].rearrange("p (s x) -> p s x", s=2)
        win = gmem[:, 3072:3584].rearrange("p (s x) -> p s x", s=TPS)
        near = gmem[:, 3584:3840].rearrange("p (s i x) -> p s i x", s=2, i=TPS)
        near1 = coef_mem[:, M0 + 1408:M0 + 1664].rearrange("p (s i x) -> p s i x", s=2, i=TPS)
        wbase1 = coef_mem[:, 0:TILES // 2]
        wbase0 = coef_mem[:, 1024:1024 + STEPS]
        emb_tmp = coef_mem[:, 0:3200]
        node_out = gmem[:, 0:2 * 512].rearrange("p (b x) -> p b x", b=2)
        sum_out = sb("sum_out", [P, 2, TPS, 2 * D])
        sum_out0 = sum_out[:, :, :, :].rearrange("p s i x -> p (s i x)").rearrange("p (s i x) -> p s i x", s=TPS, i=TPS)
        fold_in = arena[:, 0:2 * DB * 2 * D].rearrange("p (b t x) -> p b t x", b=2, t=DB)
        ulen, utmp = coef_mem[:, 0:COLS], coef_mem[:, COLS:2 * COLS]
        same = sb("same", [P, 2, TPS, P])
        zero = sb("zero", [P, 800])
        ident = sb("ident", [P, P])
        iota = sb("iota", [P, P])
        pcol = sb("pcol", [P, 8])
        lo_f = sum_out[:, :, :, :].rearrange("p s i x -> p (s i x)")[:, 0:COLS]
        hi_f = sb("hi_f", [P, COLS])
        local0 = hi_f
        base_row = sb("base_row", [1, 400], I32)
        fidx_all = sb("fidx_all", [P, STEPS // 2])
        fidx = sb("fidx", [P, 4], I32)
        ext = sb("ext", [P, 8])
        ext_t = sb("ext_t", [8, 2])
        flags = sb("flags", [1, 2], I32)
        st_edge = sb("st_edge", [P, RING, TPS, 6])
        gidx = sb("gidx", [P, RING, TPS], I32)
        sidx = sb("sidx", [P, TPS, TPS], I32)
        dupd = sb("dupd", [P, TPS])
        bases = sb("bases", [P, NB, D])
        table = sb("table", [64, NB])
        alpha = sb("alpha", [64, 1])
        w_up = sb("w_up", [P, D])
        w_m0 = sb("w_m0", [P, GROUPS // 2, P])
        w_m1 = sb("w_m1", [P, P])
        w_m2 = sb("w_m2", [P, 2, P])
        b_m = sb("b_m", [P, 2])
        b2_row = sb("b2_row", [1, D])
        b2_four = sb("b2_four", [P, TPS, D])
        ones = sb("ones", [P, P])
        w_o = sb("w_o", [P, 2, D])
        w_o1 = sb("w_o1", [P, MUL])
        zero_b = sb("zero_b", [P, P], BF16)
        stats = sb("stats", [P, NT, 6])
        rstd = sb("rstd", [P, NT])
        nbias = sb("nbias", [P, NT])
        deg = sb("deg", [NT, P])
        dinv = sb("dinv", [P, NT])
        dpos = sb("dpos", [P, NT])
        hrow = sb("hrow", [P, 2, D])
        hrowT = sb("hrowT", [P, 2, D])
        tT = sb("tT", [P, 2, 2 * D])
        moment = sb("moment", [P, 3, NT])

        bank = [ps(f"bank{i}", [P, 512]) for i in range(8)]

        ld_src, ld_dst, ld_attr, ld_x, ld_const = (sem(f"ld_{k}") for k in ("src", "dst", "attr", "x", "const"))
        ld_w, ld_w0 = sem("ld_w"), sem("ld_w0")
        padded = sem("padded")
        zeroed = sem("zeroed")
        ld_typ = [sem("ld_typ0"), sem("ld_typ1")]
        rows_ok = sem("rows_ok")
        turned = sem("turned")
        turned_out = sem("turned_out")
        dve_own = sem("dve_own")
        hots, chunk_mm = sem("hots"), sem("chunk_mm")
        deg_mm, deg_row, deg_t = sem("deg_mm"), sem("deg_row"), sem("deg_t")
        vec_done, root_done = sem("vec_done"), sem("root_done")
        scale_done = sem("scale_done")
        wprep = sem("wprep")
        based, based_mm = sem("based"), sem("based_mm")
        ext_ok, ext_mm, viol_ok, viol_mm = sem("ext_ok"), sem("ext_mm"), sem("viol_ok"), sem("viol_mm")
        flag_ok = sem("flag_ok")
        typ_hots, coef_mm, coef_out = sem("typ_hots"), sem("coef_chunk_mm"), sem("coef_out")
        h_done, h_turned, hT_out, node_mm, node_ev = (sem(k) for k in ("h_done", "h_turned", "hT_out", "node_mm", "node_ev"))
        st_tab = [sem("st_tab0"), sem("st_tab1")]
        ld_acc = [sem("ld_acc0"), sem("ld_acc1")]
        acc_used, x_done = sem("acc_used"), sem("x_done")
        blk = [sem(f"blk{n}") for n in range(4)]
        layer_in = sem("layer_in")
        emb_ld, emb_v, emb_a = sem("emb_ld"), sem("emb_v"), sem("emb_a")
        ld_fold = [sem("ld_fold0"), sem("ld_fold1")]
        fold_t, fold_c, fold_mm = sem("fold_t"), sem("fold_c"), sem("fold_mm")
        layer_done = [sem("layer_done0"), sem("layer_done1")]
        pool_done = [sem("pool_done0"), sem("pool_done1")]
        st_out = sem("st_out")

        COUNTS = {
            "f0": {"dve": "staged hot_ok near_ok same_ok le_ok tmp_ok sidx_ok", "pe": "spread coef_mm m_mm ranked summed",
                   "act": "m_ok sum_ok", "pool": "out_free let_go"},
            "g0": {"dve": "staged same_ok tmp_ok sidx_ok", "pe": "spread ranked summed", "act": "scaled sum_ok", "pool": "out_free let_go"},
            "f1": {"dve": "staged near_ok mids_ok", "pe": "h0_mm h1_mm w_mm summed", "act": "h0_ok h1_ok sum_ok", "pool": "let_go"},
            "g1": {"dve": "staged same_ok tmp_ok sidx_ok mids_ok", "pe": "spread ranked h0_mm h1_mm w_mm summed",
                   "act": "h0_ok h1_ok sum_ok", "pool": "out_free let_go"},
        }
        K = {k: {n: sem(f"{n}_{k}") for names in v.values() for n in names.split()} for k, v in COUNTS.items()}
        added = {k: [sem(f"added{i}_{k}") for i in range(TPS if k in ("f0", "g0") else 1)] for k in K}
        got = {k: [sem(f"got{i}_{k}") for i in range(GSLOT0 if k == "g0" else GSLOT)] for k in ("g0", "f1", "g1")}
        win_in = [sem(f"win_in{i}") for i in range(TPS)]
        mids_own = {k: [sem(f"mids_own{n}_{k}") for n in range(4)] for k in ("f1", "g1")}
        MORE = {"pe": [chunk_mm, node_mm, h_turned, fold_t, fold_mm, coef_mm], "act": [hT_out, node_ev, coef_out, fold_c],
                "dve": [x_done, acc_used, hots, typ_hots], "pool": [], "sp": []}

        def start(eng, who):
            for k, v in COUNTS.items():
                for n in v.get(who, "").split():
                    eng.sem_inc(K[k][n], LEAD)
            for s in MORE[who]:
                eng.sem_inc(s, LEAD)
            if who == "sp":
                for s in st_tab:
                    eng.sem_inc(s, 16 * LEAD)

        def steps(j, n):
            return j * RING + (n + LEAD)

        def hold(eng):
            eng.wait_ge(padded, 1)

        def window_flag(eng):
            eng.wait_ge(flag_ok, 1)
            return eng.value_load(flags[0:1, 0:1], min_val=0, max_val=8)

        block = ctx.enter_context(nc.Block())
        full = 12 * P * P
        more = EDGES // P - 12 * P
        tail = EDGES % P
        whole, rest = NODES // P, NODES % P
        TYPES = CHUNK * P
        LASTTYPES = EDGES - (NCH - 1) * TYPES

        @block.sync
        def _(sp):
            start(sp, "sp")
            sp.dma_start(ident[:, :], a["c_ident"]).then_inc(ld_const, 16)
            sp.dma_start(iota[:, :], a["c_iota"]).then_inc(ld_const, 16)
            sp.dma_start(pcol[:, :], a["c_pcol"]).then_inc(ld_const, 16)
            sp.wait_ge(padded, 1)
            for v, name, w, s in ((src_rows, "src", 1, ld_src), (dst_rows, "dst", 1, ld_dst), (attr_rows, "edge_attr_3", 3, ld_attr)):
                d = a[name] if w == 1 else a[name].rearrange("e c -> (e c)")
                sp.dma_start(v[:, 0:12, :], d[0:full * w].rearrange("(j q e) -> q j e", q=P, e=P * w)).then_inc(s, 16)
                sp.dma_start(v[0:more, 12, :], d[full * w:(full + more * P) * w].rearrange("(q e) -> q e", e=P * w)).then_inc(s, 16)
                sp.dma_start(v[more:more + 1, 12, 0:tail * w], d[(full + more * P) * w:EDGES * w].rearrange("(q e) -> q e", q=1)).then_inc(s, 16)
                if name == "src":
                    sp.dma_start(xn[:, 0:whole, :], a["x"][0:whole * P, :].rearrange("(t p) d -> p t d", p=P)).then_inc(ld_x, 16)
                    sp.dma_start(xn[0:rest, whole, :], a["x"][whole * P:NODES, :]).then_inc(ld_x, 16)
            sp.dma_start(table[0:NREL, :], a["L0_gnn_comps"]).then_inc(ld_w, 16)
            sp.dma_start(alpha[0:NREL, :], a["L0_gnn_alpha"]).then_inc(ld_w, 16)
            sp.dma_start(bases[:, :, :], a["L0_gnn_bases"].rearrange("b d f -> d b f")).then_inc(ld_w, 16)
            sp.dma_start(w_up[0:MUL, 0:MUL], a["L1_gnn_W_up0"]).then_inc(ld_w, 16)
            for c in range(3):
                sp.dma_start(w_up[MUL + c:MUL + c + 3 * (MUL - 1) + 1:3, MUL * (c + 1):MUL * (c + 2)], a["L1_gnn_W_up1"]).then_inc(ld_w, 16)
            for q in range(GROUPS // 2):
                for h in range(2):
                    r = 2 * CENTERS * q + CENTERS * h
                    sp.dma_start(w_m0[r:r + CENTERS, q, HID * h:HID * (h + 1)], a["L1_gnn_mlp_w0"]).then_inc(ld_w0, 16)
            for h in range(2):
                r = slice(HID * h, HID * (h + 1))
                sp.dma_start(w_m1[r, r], a["L1_gnn_mlp_w1"]).then_inc(ld_w, 16)
                sp.dma_start(w_m2[r, h, :], a["L1_gnn_mlp_w2"]).then_inc(ld_w, 16)
                sp.dma_start(b_m[r, 0:1], a["L1_gnn_mlp_b0"].rearrange("(p o) -> p o", o=1)).then_inc(ld_w, 16)
                sp.dma_start(b_m[r, 1:2], a["L1_gnn_mlp_b1"].rearrange("(p o) -> p o", o=1)).then_inc(ld_w, 16)
                sp.dma_start(w_o1[r, :], a["L1_gnn_W_out1"]).then_inc(ld_w, 16)
            sp.dma_start(b2_row[:, :], a["L1_gnn_mlp_b2"].rearrange("(o f) -> o f", o=1)).then_inc(ld_w, 16)
            sp.dma_start(w_o[0:2 * MUL, 0, 0:MUL], a["L1_gnn_W_out0"]).then_inc(ld_w, 16)
            for acc, w in [(x, D) for x in acc0] + [(acc1, 2 * D)]:
                k = NPAD * w // P // 800
                sp.dma_start(acc.rearrange("(p r) d -> p (r d)", p=P).rearrange("p (k x) -> p k x", k=k),
                             zero[:, :].unsqueeze(1).to_broadcast([P, k, 800])).then_inc(zeroed, 16)

            def types(b, e0, n=TYPES):
                sp.dma_start(typ[:, b, 0:n], a["edge_type_50"].rearrange("(o e) -> o e", o=1)[:, bass.ds(e0, n)].to_broadcast([64, n])).then_inc(ld_typ[b], 16)
            types(0, 0)
            types(1, TYPES)

            def tables(tab, w, base):
                with sp.Fori(0, NT // 2) as t:
                    for b in range(2):
                        sp.wait_ge(node_ev, t * 2 + (base + b + 1 + LEAD))
                        sp.dma_start(tab[bass.ds(t * (2 * P) + b * P, P), :], node_out[:, b, 0:w]).then_inc(st_tab[b], 16)
            tables(ytab, NB * D, 0)
            flag = window_flag(sp)
            for b in range(2):
                sp.wait_ge(st_tab[b], 16 * (NT // 2 + LEAD))
            rows = ytab.rearrange("n (b d) -> (n b) d", b=NB)
            with sp.If(flag == 0):
                F = K["f0"]

                def window(j, q):
                    node = sp.value_load(base_row[0:1, bass.ds(j * RING + q, 1)], min_val=0, max_val=PAD_NODE)
                    sp.wait_ge(F["summed"], steps(j, q - TPS + 1))
                    sp.dma_start(win[:, q % TPS, :], rows[bass.ds(node * NB, P), :]).then_inc(win_in[q % TPS], 16)

                def one_pass(j, loads):
                    for q in range(RING):
                        window(j, q)
                        if q % 4 == 3 and q // 4 < len(loads):
                            b = q // 4
                            sp.wait_ge(F["hot_ok"], steps(j, q + 1))
                            types(b, *loads[b])
                with sp.Fori(0, PASSES - 2) as j:
                    one_pass(j, [(j * (2 * TYPES) + 2 * TYPES, TYPES), (j * (2 * TYPES) + 3 * TYPES, TYPES)])
                one_pass(PASSES - 2, [((NCH - 2) * TYPES, TYPES), ((NCH - 1) * TYPES, LASTTYPES)])
                one_pass(PASSES - 1, [(0, TYPES)])
                for i in range(TPS):
                    sp.wait_ge(added["f0"][i], 16 * (STEPS + LEAD))
            with sp.Else():
                with sp.Fori(1, NCH // 2 - 1) as c:
                    for b in range(2):
                        sp.wait_ge(typ_hots, c * 2 + (b - 1 + LEAD))
                        types(b, c * (2 * TYPES) + b * TYPES)
                sp.wait_ge(typ_hots, NCH - 3 + LEAD)
                types(0, (NCH - 2) * TYPES)
                sp.wait_ge(typ_hots, NCH - 2 + LEAD)
                types(1, (NCH - 1) * TYPES, LASTTYPES)
                for i in range(TPS):
                    sp.wait_ge(added["g0"][i], 16 * (STEPS + LEAD))
            sp.sem_inc(layer_done[0], 1)

            def bring(k, b):
                for r in range(TPS):
                    sp.dma_start(accin[:, b, r, :].rearrange("p (t d) -> p t d", t=DB),
                                 acc0[r][bass.ds(k * (DB * P), DB * P), :].rearrange("(t p) d -> p t d", p=P)).then_inc(ld_acc[b], 16)
            with sp.Fori(0, NT // DB // 2) as k:
                for b in range(2):
                    sp.wait_ge(acc_used, k * 2 + (b - 1 + LEAD))
                    bring(k * 2 + b, b)
            tables(xtab, D, NT)
            sp.wait_ge(emb_v, 1)
            for g in range(GROUPS):
                n = min(EPG, EDGES - g * EPG)
                sp.dma_start(emb[CENTERS * g:CENTERS * (g + 1), 0:n],
                             a["edge_weight"].rearrange("(o e) -> o e", o=1)[:, g * EPG:g * EPG + n].to_broadcast([CENTERS, n])).then_inc(emb_ld, 16)
            with sp.If(flag == 0):
                sp.wait_ge(added["f1"][0], 16 * (STEPS // 2 + LEAD))
                sp.wait_ge(K["f1"]["w_mm"], STEPS + 1 + LEAD)
            with sp.Else():
                sp.wait_ge(added["g1"][0], 16 * (TILES + LEAD))
                sp.wait_ge(K["g1"]["w_mm"], STEPS + 1 + LEAD)
            sp.sem_inc(layer_done[1], 1)
            for k in range(NT // DB):
                if k >= 2:
                    sp.wait_ge(fold_c, (k - 1) * DB + LEAD)
                sp.dma_start(fold_in[:, k % 2, :, :], acc1[k * DB * P:(k + 1) * DB * P, :].rearrange("(t p) d -> p t d", p=P)).then_inc(ld_fold[k % 2], 16)
            for k in range(NT // DB):
                sp.wait_ge(x_done, (k + 1) * DB + LEAD)
                t1 = min((k + 1) * DB, whole)
                sp.dma_start(out[k * DB * P:t1 * P, :].rearrange("(t p) d -> p t d", p=P), xn[:, k * DB:t1, :]).then_inc(st_out, 16)
            sp.dma_start(out[whole * P:NODES, :], xn[0:rest, whole, :]).then_inc(st_out, 16)
            sp.wait_ge(st_out, 16 * (NT // DB + 1))

        @block.gpsimd
        def _(pool):
            start(pool, "pool")
            IX = bass.IndirectOffsetOnAxis

            def gather(k, tab, gat, slots, j, s):
                pool.wait_ge(K[k]["staged"], steps(j, s + 1))
                pool.sem_inc(K[k]["let_go"], 1)
                for i in range(TPS):
                    pool.indirect_dma_start(gat[:, s % slots, i, :], None, tab, IX(ap=gidx[:, s % RING, i:i + 1], axis=0)).then_inc(got[k][s % slots], 16)

            def add_step(k, j, q):
                S = K[k]
                pool.wait_ge(S["sidx_ok"], steps(j, q + 1))
                pool.wait_ge(S["sum_ok"], steps(j, q + 1))
                for i in range(TPS):
                    pool.wait_ge(added[k][i], j * (16 * RING) + 16 * (q + LEAD))
                    pool.sem_inc(S["out_free" if i == TPS - 1 else "let_go"], 1)
                    pool.indirect_dma_start(acc0[i], IX(ap=sidx[:, q % TPS, i:i + 1], axis=0),
                                            sum_out0[:, q % TPS, i, :], None, compute_op=ALU.add).then_inc(added[k][i], 16)

            flag = window_flag(pool)
            pool.wait_ge(zeroed, 16 * (TPS + 1))

            def prime(k, accs):
                for acc, s in zip(accs, added[k]):
                    for n in range(LEAD):
                        r = (NT - 1) * P + n * (P // LEAD)
                        pool.dma_start(acc[r:r + P // LEAD, 0:D], zero[0:P // LEAD, 0:D]).then_inc(s, 16)
            with pool.If(flag == 0):
                prime("f0", acc0)
                with pool.Fori(0, PASSES) as j:
                    for q in range(RING):
                        add_step("f0", j, q)
            with pool.Else():
                G = K["g0"]
                prime("g0", acc0)
                for b in range(2):
                    pool.wait_ge(st_tab[b], 16 * (NT // 2 + LEAD))
                pool.wait_ge(layer_in, 1)
                for s in range(GSLOT0 - 1):
                    gather("g0", ytab, gat0, GSLOT0, 0, s)
                with pool.Fori(0, PASSES) as j:
                    for q in range(RING):
                        pool.wait_ge(G["summed"], steps(j, q))
                        gather("g0", ytab, gat0, GSLOT0, j, q + GSLOT0 - 1)
                        add_step("g0", j, q)
                for n in range(GSLOT0):
                    pool.wait_ge(got["g0"][n], 16 * TPS * (STEPS // GSLOT0 + (n < GSLOT0 - 1)))
            pool.sem_inc(pool_done[0], 1)

            for b in range(2):
                pool.wait_ge(st_tab[b], 16 * (NT + LEAD))
            with pool.If(flag == 0):
                F = K["f1"]
                prime("f1", [acc1])
                for s in range(GSLOT - 1):
                    gather("f1", xtab, gat1, GSLOT, 0, s)
                with pool.Fori(0, PASSES) as j:
                    for q in range(RING):
                        pool.wait_ge(F["mids_ok"], steps(j, q))
                        gather("f1", xtab, gat1, GSLOT, j, q + GSLOT - 1)
                        if q % 2:
                            h = q // 2
                            pool.wait_ge(F["sum_ok"], j * (RING // 2) + (h + 1 + LEAD))
                            pool.wait_ge(added["f1"][0], j * (16 * RING // 2) + 16 * (h + LEAD))
                            pool.sem_inc(F["let_go"], 1)
                            pool.indirect_dma_start(acc1, IX(ap=fidx[:, h:h + 1], axis=0), sum_out[:, h % 2, 0, :], None,
                                                    compute_op=ALU.add).then_inc(added["f1"][0], 16)
                for n in range(GSLOT):
                    pool.wait_ge(got["f1"][n], 16 * TPS * (STEPS // GSLOT + (n < GSLOT - 1)))
            with pool.Else():
                G = K["g1"]
                prime("g1", [acc1])
                for s in range(GSLOT - 1):
                    gather("g1", xtab, gat1, GSLOT, 0, s)
                with pool.Fori(0, PASSES) as j:
                    for q in range(RING):
                        pool.wait_ge(G["summed"], steps(j, q))
                        gather("g1", xtab, gat1, GSLOT, j, q + GSLOT - 1)
                        pool.wait_ge(G["sidx_ok"], steps(j, q + 1))
                        pool.wait_ge(G["sum_ok"], steps(j, q + 1))
                        for i in range(TPS):
                            pool.wait_ge(added["g1"][0], j * (16 * RING * TPS) + 16 * (q * TPS + i + LEAD))
                            pool.sem_inc(G["let_go"], 1)
                            pool.indirect_dma_start(acc1, IX(ap=sidx[:, q % TPS, i:i + 1], axis=0), sum_out[:, q % 2, i, :], None,
                                                    compute_op=ALU.add).then_inc(added["g1"][0], 16)
                        pool.wait_ge(added["g1"][0], j * (16 * RING * TPS) + 16 * ((q + 1) * TPS + LEAD))
                        pool.sem_inc(G["out_free"], 1)
                for n in range(GSLOT):
                    pool.wait_ge(got["g1"][n], 16 * TPS * (STEPS // GSLOT + (n < GSLOT - 1)))
            pool.sem_inc(pool_done[1], 1)

        @block.scalar
        def _(act):
            start(act, "act")
            C = nc.scalar.copy
            n = 0
            for f in range(5):
                for b0 in range(0, BLOCKS, 4):
                    k = min(4, BLOCKS - b0)
                    act.wait_ge(turned, n + 1)
                    C(edge[:, b0 * P:(b0 + k) * P, f], bank[n % 4][:, 0:k * P]).then_inc(turned_out, 1)
                    n += 1

            def roots(v, n):
                act.wait_ge(vec_done, n)
                nc.scalar.activation(v, v, ACT.Sqrt).then_inc(root_done, 1)
            roots(rstd[:, :], 1)
            roots(dinv[:, :], 2)
            act.wait_ge(scale_done, 1)

            def node_rows(base, w):
                def norm(n, b):
                    hold(act)
                    act.wait_ge(h_turned, n + (base - 1 + LEAD))
                    nc.scalar.activation(hrow[:, b, :], xn[:, bass.ds(n, 1), :].rearrange("p o d -> p (o d)"), ACT.Relu,
                                         bias=nbias[:, bass.ds(n, 1)], scale=rstd[:, bass.ds(n, 1)]).then_inc(h_done, 1)

                def turned_copy(n, b):
                    act.wait_ge(node_mm, n + (base - 1 + LEAD))
                    act.wait_ge(h_turned, n + (base + 1 + LEAD))
                    C(hrowT[:, b, :], bank[6 + b][:, 0:P]).then_inc(hT_out, 1)

                def evict(n, t, b):
                    act.wait_ge(node_mm, n + (base + 1 + LEAD))
                    act.wait_ge(st_tab[b], t * 16 + 16 * (base // 2 + LEAD))
                    C(node_out[:, b, 0:w], bank[4 + b][:, 0:w]).then_inc(node_ev, 1)
                norm(0, 0)
                norm(1, 1)
                turned_copy(0, 0)
                with act.Fori(0, NT // 2 - 1) as t:
                    for b in range(2):
                        norm(t * 2 + (b + 2), b)
                        turned_copy(t * 2 + (b + 1), 1 - b)
                        evict(t * 2 + b, t, b)
                turned_copy(NT - 1, 1)
                for b in range(2):
                    evict(NT - 2 + b, NT // 2 - 1, b)

            node_rows(0, NB * D)
            roots(ulen, 3)
            flag = window_flag(act)
            with act.If(flag == 0):
                F = K["f0"]
                with act.Fori(0, PASSES) as j:
                    for q in range(RING):
                        act.wait_ge(F["m_mm"], steps(j, q + 1))
                        act.wait_ge(F["summed"], steps(j, q - 1))
                        C(wsum[:, q % 2, :], bank[4 + q % 2][:, :]).then_inc(F["m_ok"], 1)
                        act.wait_ge(F["summed"], steps(j, q + 1))
                        act.wait_ge(F["out_free"], steps(j, q - 2))
                        C(sum_out0[:, q % TPS, :, :], bank[q % 2][:, :].rearrange("p (i x) -> p i x", i=TPS)).then_inc(F["sum_ok"], 1)
            with act.Else():
                with act.Fori(0, NCH // 2) as c:
                    for b in range(2):
                        hold(act)
                        act.wait_ge(coef_mm, c * 2 + (b + 1 + LEAD))
                        C(coef_mem[:, bass.ds(c * (2 * CHUNK * NB) + b * CHUNK * NB, CHUNK * NB)], bank[b][:, 0:CHUNK * NB]).then_inc(coef_out, 1)
                act.wait_ge(coef_out, NCH + LEAD)
                G = K["g0"]
                with act.Fori(0, PASSES) as j:
                    for q in range(RING):
                        hold(act)
                        act.wait_ge(got["g0"][q % GSLOT0], j * (16 * TPS * RING // GSLOT0) + 16 * TPS * (q // GSLOT0 + 1))
                        for i in range(TPS):
                            for b in range(NB):
                                g = gat0[:, q % GSLOT0, i, b * D:(b + 1) * D]
                                last = nc.scalar.mul(g, g, coef_mem[:, bass.ds(j * (RING * TPS * NB) + (q * TPS + i) * NB + b, 1)])
                        last.then_inc(G["scaled"], 1)
                        act.wait_ge(G["summed"], steps(j, q + 1))
                        act.wait_ge(G["out_free"], steps(j, q - 2))
                        C(sum_out0[:, q % TPS, :, :], bank[q % 2][:, :].rearrange("p (i x) -> p i x", i=TPS)).then_inc(G["sum_ok"], 1)

            act.wait_ge(pool_done[0], 1)
            roots(rstd[:, :], 4)
            act.wait_ge(scale_done, 2)
            node_rows(NT, D)

            for n, (lo, hi) in enumerate(EMB_PARTS):
                act.wait_ge(emb_v, 2 + n)
                nc.scalar.activation(emb[:, lo:hi], emb[:, lo:hi], ACT.Square, bias=pcol[:, 4:5], scale=float(CENTERS - 1)).then_inc(emb_a, 1)
            for n, (lo, hi) in enumerate(EMB_PARTS):
                act.wait_ge(emb_a, n + 1)
                nc.scalar.activation(emb[:, lo:hi], emb[:, lo:hi], ACT.Exp, scale=-0.5).then_inc(emb_a, 1)

            def mlp(S, j, n):
                act.wait_ge(S["h0_mm"], steps(j, n))
                nc.scalar.activation(hid0, bank[6][:, 0:256], ACT.Silu, bias=b_m[:, 0:1]).then_inc(S["h0_ok"], 1)
                act.wait_ge(S["h1_mm"], steps(j, n))
                nc.scalar.activation(hid1, bank[6][:, 256:512], ACT.Silu, bias=b_m[:, 1:2]).then_inc(S["h1_ok"], 1)
            with act.If(flag == 0):
                F = K["f1"]
                mlp(F, 0, 1)
                act.wait_ge(added["f1"][0], 16 * LEAD)
                with act.Fori(0, PASSES) as j:
                    for q in range(RING):
                        mlp(F, j, q + 2)
                        if q % 2:
                            h = q // 2
                            act.wait_ge(F["summed"], steps(j, q + 1))
                            act.wait_ge(added["f1"][0], j * (16 * RING // 2) + 16 * (h - 1 + LEAD))
                            C(sum_out[:, h % 2, 0, :], bank[h % 2][:, 0:2 * D]).then_inc(F["sum_ok"], 1)
            with act.Else():
                G = K["g1"]
                mlp(G, 0, 1)
                with act.Fori(0, PASSES) as j:
                    for q in range(RING):
                        mlp(G, j, q + 2)
                        act.wait_ge(G["summed"], steps(j, q + 1))
                        act.wait_ge(G["out_free"], steps(j, q - 1))
                        for h in range(2):
                            last = C(sum_out[:, q % 2, 2 * h:2 * h + 2, :], bank[h][:, :].rearrange("p (i x) -> p i x", i=2))
                        last.then_inc(G["sum_ok"], 1)

            with act.Fori(0, NT // 2) as t:
                for b in range(2):
                    act.wait_ge(fold_t, t * 2 + (b + 1 + LEAD))
                    act.wait_ge(fold_mm, t * 2 + (b - 1 + LEAD))
                    C(tT[:, b, :], bank[6 + b][:, 0:2 * D]).then_inc(fold_c, 1)

        @block.vector
        def _(dve):
            start(dve, "dve")
            own = [0]

            def link(ins):
                own[0] += 1
                ins.then_inc(dve_own, 1)
                dve.wait_ge(dve_own, own[0])

            V = nc.vector
            V.memset(src_rows[:, 12, :], PAD_NODE)
            V.memset(dst_rows[:, 12, :], PAD_NODE)
            V.memset(attr_rows[:, 12, :], 0.0)
            V.memset(xn[:, NODES // P:NT, :], 0.0)
            V.memset(w_up[:, :], 0.0)
            V.memset(w_m0[:, :, :], 0.0)
            V.memset(w_m1[:, :], 0.0)
            V.memset(w_m2[:, :, :], 0.0)
            V.memset(b2_four[:, :, :], 0.0)
            V.memset(w_o[:, :, :], 0.0)
            V.memset(table[:, :], 0.0)
            V.memset(alpha[:, :], 0.0)
            V.memset(edge[:, :, 5], 0.0)
            V.memset(zero[:, :], 0.0)
            V.memset(zero_b[:, :], 0.0)
            V.memset(ones[:, :], 1.0).then_inc(padded, 1)

            ids = BLOCKS * P
            dve.wait_ge(ld_src, 48)
            V.tensor_copy(arena[:, 0:ids], rows_i[:, 0:ids]).then_inc(rows_ok, 1)
            dve.wait_ge(ld_dst, 48)
            V.tensor_copy(arena[:, ids:2 * ids], rows_i[:, ids:2 * ids]).then_inc(rows_ok, 1)

            dve.wait_ge(ld_const, 48)
            dve.wait_ge(turned_out, 4)
            ii, hh = lo_f.bitcast(I32), hi_f[:, :].bitcast(I32)
            link(V.tensor_copy(ii, edge[:, :, 0]))
            link(V.tensor_scalar(hh, ii, 7, None, ALU.logical_shift_right))
            link(V.tensor_scalar(ii, ii, 127, None, ALU.bitwise_and))
            link(V.tensor_copy(hi_f[:, :], hh))
            link(V.tensor_copy(lo_f, ii))

            mean, gap, var = (moment[:, k, :] for k in range(3))

            dve.wait_ge(ld_x, 32)
            with dve.Fori(0, NT // DB) as k:
                for t in range(DB):
                    last = V.bn_stats(stats[:, bass.ds(k * DB + t, 1), :].rearrange("p o s -> p (o s)"),
                                      xn[:, bass.ds(k * DB + t, 1), :].rearrange("p o d -> p (o d)"))
            link(V.memset(dupd[:, :], 0.0))
            V.tensor_tensor(mean, stats[:, :, 1], stats[:, :, 4], ALU.add)
            V.tensor_tensor(var, stats[:, :, 2], stats[:, :, 5], ALU.add)
            link(V.tensor_tensor(gap, stats[:, :, 1], stats[:, :, 4], ALU.subtract))
            link(V.tensor_tensor(gap, gap, gap, ALU.mult))
            V.tensor_scalar(mean, mean, 0.5, None, ALU.mult)
            link(V.scalar_tensor_tensor(var, gap, D / 4.0, var, ALU.mult, ALU.add))
            V.tensor_scalar(rstd[:, :], var, 1.0 / D, EPS, ALU.mult, ALU.add).then_inc(vec_done, 1)

            with dve.Fori(0, NCH // 2) as c:
                for b in range(2):
                    t0 = c * (2 * CHUNK) + b * CHUNK
                    dve.wait_ge(chunk_mm, c * 2 + (b - 1 + LEAD))
                    V.tensor_tensor(lo_hot[:, b, :, :], iota[:, :].unsqueeze(1).to_broadcast([P, CHUNK, P]),
                                    lo_f[:, bass.ds(t0, CHUNK)].unsqueeze(2).to_broadcast([P, CHUNK, P]), ALU.is_equal)
                    V.tensor_tensor(hi_hot[:, b, :, :], iota[:, 0:NT].unsqueeze(1).to_broadcast([P, CHUNK, NT]),
                                    hi_f[:, bass.ds(t0, CHUNK)].unsqueeze(2).to_broadcast([P, CHUNK, NT]), ALU.is_equal).then_inc(hots, 1)
            dve.wait_ge(deg_mm, 1)
            V.tensor_copy(deg[:, :], bank[2][0:NT, 0:P]).then_inc(deg_row, 1)
            dve.wait_ge(deg_t, 1)
            link(V.tensor_scalar(dpos[:, :], bank[3][:, 0:NT], 0.0, None, ALU.is_gt))
            V.tensor_scalar(dinv[:, :], bank[3][:, 0:NT], 1.0, None, ALU.max).then_inc(vec_done, 1)
            dve.wait_ge(root_done, 2)
            link(V.reciprocal(rstd[:, :], rstd[:, :]))
            link(V.reciprocal(dinv[:, :], dinv[:, :]))
            link(V.tensor_tensor(dinv[:, :], dinv[:, :], dpos[:, :], ALU.mult))
            link(V.tensor_tensor(rstd[:, :], rstd[:, :], dinv[:, :], ALU.mult))
            V.scalar_tensor_tensor(nbias[:, :], mean, -1.0, rstd[:, :], ALU.mult, ALU.mult).then_inc(scale_done, 1)

            dve.wait_ge(turned_out, 20)
            dve.wait_ge(based_mm, 1)
            V.tensor_copy(wbase0, bank[0][:, 0:STEPS])
            for h in range(2):
                last = V.tensor_copy(wbase1[:, h * TPG * 4:(h + 1) * TPG * 4], bank[1 + h][:, 0:TPG * 4])
            link(V.tensor_copy(base_row[0:1, 0:STEPS], bank[0][0:1, 0:STEPS]))
            V.memset(local0[:, TILES:COLS], 0.0)
            V.tensor_tensor(local0[:, 0:TILES].rearrange("p (s i) -> p s i", i=TPS), edge[:, 0:TILES, 1].rearrange("p (s i) -> p s i", i=TPS),
                            wbase0.unsqueeze(2).to_broadcast([P, STEPS, TPS]), ALU.subtract)
            l1 = edge[:, 0:TILES, 5].rearrange("p (s i) -> p s i", i=2)
            V.tensor_tensor(l1, edge[:, 0:TILES, 1].rearrange("p (s i) -> p s i", i=2),
                            wbase1.unsqueeze(2).to_broadcast([P, TILES // 2, 2]), ALU.subtract)
            by = wbase1.rearrange("p (h c j) -> p c j h", h=RING // 2, c=4)
            for c in range(4):
                r = slice(WIN * c, WIN * (c + 1))
                V.tensor_scalar(fidx_all[r, :].rearrange("p (j h) -> p j h", h=RING // 2), by[r, c], pcol[r, 5:6], None, ALU.add)
            link(V.tensor_tensor(lo_f[:, 0:(GROUPS - 1) * PASSES], wbase1[:, PASSES:], wbase1[:, 0:(GROUPS - 1) * PASSES], ALU.subtract))
            MX, MN = ALU.max, ALU.min
            V.tensor_reduce(ext[:, 0:1], local0[:, 0:TILES], AXX, MX)
            V.tensor_reduce(ext[:, 1:2], local0[:, 0:TILES], AXX, MN)
            V.tensor_reduce(ext[:, 2:3], edge[:, 0:TILES, 5], AXX, MX)
            V.tensor_reduce(ext[:, 3:4], edge[:, 0:TILES, 5], AXX, MN)
            link(V.tensor_reduce(ext[:, 4:5], lo_f[:, 0:(GROUPS - 1) * PASSES], AXX, MN))
            link(V.tensor_scalar(ext[:, 1:2], ext[:, 1:2], -1.0, None, ALU.mult))
            V.tensor_scalar(ext[:, 3:5], ext[:, 3:5], -1.0, None, ALU.mult).then_inc(ext_ok, 1)
            dve.wait_ge(ext_mm, 1)
            link(V.tensor_reduce(ext_t[0:5, 0:1], bank[0][0:5, 0:P], AXX, MX))
            V.tensor_scalar(ext_t[0:5, 1:2], ext_t[0:5, 0:1], pcol[0:5, 6:7], None, ALU.is_gt).then_inc(viol_ok, 1)
            dve.wait_ge(viol_mm, 1)
            V.tensor_copy(flags[0:1, 0:1], bank[1][0:1, 0:1]).then_inc(flag_ok, 1)

            dve.wait_ge(ld_w, 16 * 19)
            link(V.tensor_scalar(table[:, :], table[:, :], alpha[:, 0:1], None, ALU.mult))
            flag = window_flag(dve)

            ex = [edge[:, :, 2 + c] for c in range(3)]
            link(V.tensor_tensor(ulen, ex[0], ex[0], ALU.mult))
            for c in (1, 2):
                link(V.tensor_tensor(utmp, ex[c], ex[c], ALU.mult))
                link(V.tensor_tensor(ulen, ulen, utmp, ALU.add))
            V.tensor_scalar(ulen, ulen, 1.3e-35, None, ALU.max).then_inc(vec_done, 1)
            dve.wait_ge(ld_w0, 16 * GROUPS)
            V.tensor_scalar(w_up[:, :], w_up[:, :], MUL ** -0.5, None, ALU.mult)
            V.tensor_scalar(w_m0[:, :, :], w_m0[:, :, :], CENTERS ** 0.5, None, ALU.mult)
            V.tensor_scalar(w_m2[:, :, MUL:2 * MUL], w_m2[:, :, MUL:2 * MUL], SQ3, None, ALU.mult)
            link(V.tensor_scalar(b2_row[:, MUL:2 * MUL], b2_row[:, MUL:2 * MUL], SQ3, None, ALU.mult))
            V.tensor_copy(b2_four[0:1, :, :], b2_row[:, :].unsqueeze(1).to_broadcast([1, TPS, D]))
            out_scale = (2 * MUL) ** -0.5 / 16.0
            h0, h1 = slice(0, 2 * MUL), slice(2 * MUL, 4 * MUL)
            V.tensor_scalar(w_o[h0, 0, 0:MUL], w_o[h0, 0, 0:MUL], out_scale, None, ALU.mult)
            V.tensor_scalar(w_o[h1, 0, MUL:D:3], w_o1[h1, :], out_scale, None, ALU.mult)
            V.tensor_scalar(w_o[h0, 1, MUL + 1:D:3], w_o1[h0, :], out_scale, None, ALU.mult)
            V.tensor_scalar(w_o[h1, 1, MUL + 2:D:3], w_o1[h1, :], out_scale, None, ALU.mult).then_inc(wprep, 1)
            dve.wait_ge(root_done, 3)
            link(V.tensor_scalar(ulen, ulen, 1e-12, None, ALU.add))
            link(V.reciprocal(utmp, ulen))
            for c in range(3):
                last = V.tensor_tensor(ex[c], ex[c], utmp, ALU.mult)
            link(last)
            dve.wait_ge(node_ev, NT + LEAD)
            for b in range(2):
                dve.wait_ge(st_tab[b], 16 * (NT // 2 + LEAD))
            dve.sem_inc(layer_in, 1)

            def same_rows(k, j, q):
                S, L = K[k], int(k[1])
                dve.wait_ge(S["spread"], steps(j, q + 1))
                V.tensor_tensor(same[:, q % 2, :, :], bank[2][:, :].rearrange("p (i x) -> p i x", i=TPS),
                                st_edge[:, q % RING, :, L:L + 1].to_broadcast([P, TPS, P]), ALU.is_equal).then_inc(S["same_ok"], 1)

            def scatter_rows(k, j, q):
                S, L = K[k], int(k[1])
                dve.wait_ge(S["sidx_ok"], steps(j, q))
                dve.wait_ge(S["ranked"], steps(j, q + 1))
                V.tensor_scalar(dupd[:, :], bank[3][:, TPS * (q % 2):TPS * (q % 2) + TPS], pcol[:, 2:3], pcol[:, 3:4], ALU.is_gt, ALU.mult).then_inc(S["tmp_ok"], 1)
                dve.wait_ge(S["tmp_ok"], steps(j, q + 1))
                V.tensor_tensor(sidx[:, q % TPS, :], dupd[:, :], st_edge[:, q % RING, :, L], ALU.max).then_inc(S["sidx_ok"], 1)

            def stage0(k, j, s, rows):
                c0 = j * (RING * TPS) + s * TPS
                last = V.tensor_copy(st_edge[:, s % RING, :, 0:2], edge[:, bass.ds(c0, TPS), 0:2])
                if rows:
                    last = V.tensor_copy(gidx[:, s % RING, :], edge[:, bass.ds(c0, TPS), 1])
                last.then_inc(K[k]["staged"], 1)

            def stage1(k, j, s):
                q = s % RING
                for g in range(2):
                    c0 = (j + s // RING) * 2 + (2 * q + g) * TPG
                    V.tensor_copy(st_edge[:, q, 2 * g:2 * g + 2, :], edge[:, bass.ds(c0, 2), :])
                    last = V.tensor_copy(gidx[:, q, 2 * g:2 * g + 2], edge[:, bass.ds(c0, 2), 0])
                last.then_inc(K[k]["staged"], 1)

            def mids(k, j, q):
                S, own = K[k], mids_own[k]
                w = bank[4 + q % 2][:, :].rearrange("p (i x) -> p i x", i=TPS)
                g = gat1[:, q % GSLOT, :, :]
                gv = g[:, :, MUL:].rearrange("p i (c k) -> p i c k", c=3)
                m = mid[:, q % 2, :, :]
                mc = m[:, :, 2 * MUL:].rearrange("p i (c k) -> p i c k", c=3)
                unit = st_edge[:, q % RING, :, 2:5].unsqueeze(3).to_broadcast([P, TPS, 3, MUL])
                done = j * RING + (q + 1)
                dve.wait_ge(got[k][q % GSLOT], j * (16 * TPS * RING // GSLOT) + 16 * TPS * (q // GSLOT + 1))
                V.tensor_tensor(vdot[:, :, :, :], gv, unit, ALU.mult).then_inc(own[0], 1)
                dve.wait_ge(S["w_mm"], steps(j, q + 1))
                V.tensor_tensor(w01s, w[:, :, MUL:2 * MUL], g[:, :, 0:MUL], ALU.mult).then_inc(own[1], 1)
                dve.wait_ge(own[0], done)
                V.tensor_tensor(vsum[:, :, 0, :], vdot[:, :, 0, :], vdot[:, :, 1, :], ALU.add).then_inc(own[2], 1)
                V.tensor_tensor(m[:, :, 0:MUL], w[:, :, 0:MUL], g[:, :, 0:MUL], ALU.mult)
                V.tensor_tensor(mc[:, :, :, MUL:], w[:, :, 2 * MUL:3 * MUL].unsqueeze(2).to_broadcast([P, TPS, 3, MUL]), gv, ALU.mult)
                dve.wait_ge(own[2], done)
                V.tensor_tensor(vsum[:, :, 1, :], vsum[:, :, 0, :], vdot[:, :, 2, :], ALU.add).then_inc(own[3], 1)
                dve.wait_ge(own[1], done)
                V.tensor_tensor(mc[:, :, :, 0:MUL], w01s.unsqueeze(2).to_broadcast([P, TPS, 3, MUL]), unit, ALU.mult)
                dve.wait_ge(own[3], done)
                V.tensor_tensor(m[:, :, MUL:2 * MUL], w[:, :, 3 * MUL:], vsum[:, :, 1, :], ALU.mult).then_inc(S["mids_ok"], 1)

            with dve.If(flag == 0):
                F = K["f0"]

                def hot(j, s):
                    b = (s // 4) % 2
                    if s % 4 == 0 or isinstance(j, int):
                        dve.wait_ge(ld_typ[b], (j + s // 8) * 16 + 16)
                    dve.wait_ge(F["coef_mm"], steps(j, s - 1))
                    V.tensor_scalar(thot[:, s % 2, :], typ[:, b, (s % 4) * TPS * P:(s % 4 + 1) * TPS * P], pcol[0:64, 0:1], None, ALU.is_equal).then_inc(F["hot_ok"], 1)

                def near_rows(j, s):
                    V.tensor_tensor(near[:, s % 2, :, :], iota[:, 0:WIN].unsqueeze(1).to_broadcast([P, TPS, WIN]),
                                    local0[:, bass.ds(j * (RING * TPS) + s * TPS, TPS)].unsqueeze(2).to_broadcast([P, TPS, WIN]), ALU.is_equal).then_inc(F["near_ok"], 1)

                def edge_weights(j, s):
                    dve.wait_ge(F["near_ok"], steps(j, s + 1))
                    dve.wait_ge(F["coef_mm"], steps(j, s + 1))
                    cf = bank[6 + s % 2][:, 0:TPS * NB].rearrange("p (i b) -> p i b", b=NB)
                    V.tensor_tensor(wedge[:, s % 2, :, :].rearrange("p i (n b) -> p i n b", b=NB),
                                    near[:, s % 2, :, :].unsqueeze(3).to_broadcast([P, TPS, WIN, NB]),
                                    cf.unsqueeze(2).to_broadcast([P, TPS, WIN, NB]), ALU.mult).then_inc(F["le_ok"], 1)
                for s in range(3):
                    stage0("f0", 0, s, False)
                hot(0, 0)
                hot(0, 1)
                near_rows(0, 0)
                same_rows("f0", 0, 0)
                edge_weights(0, 0)
                scatter_rows("f0", 0, 0)
                with dve.Fori(0, PASSES) as j:
                    for q in range(RING):
                        hold(dve)
                        dve.wait_ge(F["summed"], steps(j, q))
                        stage0("f0", j, q + 3, False)
                        hot(j, q + 2)
                        near_rows(j, q + 1)
                        same_rows("f0", j, q + 1)
                        edge_weights(j, q + 1)
                        dve.wait_ge(F["out_free"], steps(j, q - 1))
                        scatter_rows("f0", j, q + 1)
            with dve.Else():
                G = K["g0"]
                with dve.Fori(0, NCH // 2) as c:
                    for b in range(2):
                        dve.wait_ge(ld_typ[b], c * 16 + 16)
                        dve.wait_ge(coef_mm, c * 2 + (b - 1 + LEAD))
                        V.tensor_scalar(typ_hot[:, b, :], typ[:, b, :], pcol[0:64, 0:1], None, ALU.is_equal).then_inc(typ_hots, 1)
                dve.wait_ge(coef_mm, NCH + LEAD)
                for s in range(GSLOT0):
                    stage0("g0", 0, s, True)
                same_rows("g0", 0, 0)
                scatter_rows("g0", 0, 0)
                with dve.Fori(0, PASSES) as j:
                    for q in range(RING):
                        hold(dve)
                        dve.wait_ge(G["summed"], steps(j, q))
                        stage0("g0", j, q + GSLOT0, True)
                        same_rows("g0", j, q + 1)
                        dve.wait_ge(G["out_free"], steps(j, q - 1))
                        scatter_rows("g0", j, q + 1)

            dve.wait_ge(layer_done[0], 1)
            with dve.Fori(0, NT // DB // 2) as k:
                for b in range(2):
                    kk = k * 2 + b
                    dve.wait_ge(ld_acc[b], k * (16 * TPS) + 16 * TPS)
                    w = accin[:, b, :, :]
                    V.tensor_tensor(w[:, 0, :], w[:, 0, :], w[:, 1, :], ALU.add)
                    V.tensor_tensor(w[:, 2, :], w[:, 2, :], w[:, 3, :], ALU.add).then_inc(blk[0], 1)
                    dve.wait_ge(blk[0], kk + 1)
                    V.tensor_tensor(w[:, 0, :], w[:, 0, :], w[:, 2, :], ALU.add).then_inc(blk[1], 1)
                    dve.wait_ge(blk[1], kk + 1)
                    w3 = w[:, 0, :].rearrange("p (t d) -> p t d", t=DB)
                    V.tensor_tensor(w3, w3, dinv[:, bass.ds(kk * DB, DB)].unsqueeze(2).to_broadcast([P, DB, D]), ALU.mult).then_inc(blk[2], 1)
                    dve.wait_ge(blk[2], kk + 1)
                    xb = xn[:, bass.ds(kk * DB, DB), :]
                    V.tensor_tensor(xb, xb, w3, ALU.add).then_inc(acc_used, 1)
                    dve.wait_ge(acc_used, kk + (1 + LEAD))
                    for t in range(DB):
                        last = V.bn_stats(stats[:, bass.ds(kk * DB + t, 1), :].rearrange("p o s -> p (o s)"),
                                          xn[:, bass.ds(kk * DB + t, 1), :].rearrange("p o d -> p (o d)"))
                    last.then_inc(blk[3], 1)
            dve.wait_ge(blk[3], NT // DB)
            V.tensor_tensor(mean, stats[:, :, 1], stats[:, :, 4], ALU.add)
            V.tensor_tensor(var, stats[:, :, 2], stats[:, :, 5], ALU.add)
            link(V.tensor_tensor(gap, stats[:, :, 1], stats[:, :, 4], ALU.subtract))
            link(V.tensor_tensor(gap, gap, gap, ALU.mult))
            V.tensor_scalar(mean, mean, 0.5, None, ALU.mult)
            link(V.scalar_tensor_tensor(var, gap, D / 4.0, var, ALU.mult, ALU.add))
            V.tensor_scalar(rstd[:, :], var, 1.0 / D, EPS, ALU.mult, ALU.add).then_inc(vec_done, 1)
            V.memset(emb[:, :], 0.0).then_inc(emb_v, 1)
            dve.wait_ge(root_done, 4)
            link(V.reciprocal(rstd[:, :], rstd[:, :]))
            V.scalar_tensor_tensor(nbias[:, :], mean, -1.0, rstd[:, :], ALU.mult, ALU.mult).then_inc(scale_done, 1)
            dve.wait_ge(emb_ld, 16 * GROUPS)
            for n, (lo, hi) in enumerate(EMB_PARTS):
                link(V.tensor_scalar(emb_tmp[:, 0:hi - lo], emb[:, lo:hi], 1.0, 1e9, ALU.is_gt, ALU.mult))
                link(V.tensor_scalar(emb[:, lo:hi], emb[:, lo:hi], 0.0, 1.0, ALU.max, ALU.min))
                V.tensor_tensor(emb[:, lo:hi], emb[:, lo:hi], emb_tmp[:, 0:hi - lo], ALU.add).then_inc(emb_v, 1)
                dve.wait_ge(emb_v, n + 2)

            with dve.If(flag == 0):
                F = K["f1"]

                def near_rows1(j, s):
                    dve.wait_ge(F["staged"], steps(j, s + 1))
                    V.tensor_tensor(near1[:, s % 2, :, :], iota[:, 0:WIN].unsqueeze(1).to_broadcast([P, TPS, WIN]),
                                    st_edge[:, s % RING, :, 5:6].to_broadcast([P, TPS, WIN]), ALU.is_equal).then_inc(F["near_ok"], 1)
                for s in range(GSLOT):
                    stage1("f1", 0, s)
                near_rows1(0, 0)
                dve.wait_ge(added["f1"][0], 16 * LEAD)
                with dve.Fori(0, PASSES) as j:
                    for q in range(RING):
                        hold(dve)
                        dve.wait_ge(F["summed"], steps(j, q))
                        dve.wait_ge(F["mids_ok"], steps(j, q))
                        stage1("f1", j, q + GSLOT)
                        if q % 2 == 0:
                            h = q // 2
                            hold(dve)
                            dve.wait_ge(added["f1"][0], j * (16 * RING // 2) + 16 * (h - 3 + LEAD))
                            V.tensor_copy(fidx[:, h:h + 1], fidx_all[:, bass.ds(j * (RING // 2) + h, 1)])
                        near_rows1(j, q + 1)
                        mids("f1", j, q)
            with dve.Else():
                G = K["g1"]
                for s in range(GSLOT):
                    stage1("g1", 0, s)
                same_rows("g1", 0, 0)
                scatter_rows("g1", 0, 0)
                with dve.Fori(0, PASSES) as j:
                    for q in range(RING):
                        hold(dve)
                        dve.wait_ge(G["summed"], steps(j, q))
                        stage1("g1", j, q + GSLOT)
                        same_rows("g1", j, q + 1)
                        mids("g1", j, q)
                        dve.wait_ge(G["out_free"], steps(j, q - 2))
                        scatter_rows("g1", j, q + 1)

            with dve.Fori(0, NT // 2) as t:
                for b in range(2):
                    hold(dve)
                    dve.wait_ge(fold_mm, t * 2 + (b + 1 + LEAD))
                    x = xn[:, bass.ds(t * 2 + b, 1), :].rearrange("p o d -> p (o d)")
                    V.tensor_tensor(x, bank[4 + b][:, 0:D], x, ALU.add).then_inc(x_done, 1)

        @block.tensor
        def _(pe):
            start(pe, "pe")
            T = nc.tensor
            pe.wait_ge(ld_const, 48)
            n = 0
            for f in range(5):
                if f < 2:
                    pe.wait_ge(rows_ok, f + 1)
                if f == 2:
                    pe.wait_ge(ld_attr, 48)
                for b0 in range(0, BLOCKS, 4):
                    k = min(4, BLOCKS - b0)
                    if n >= 4:
                        pe.wait_ge(turned_out, n - 3)
                    for b in range(b0, b0 + k):
                        r = arena[:, f * BLOCKS * P + b * P:f * BLOCKS * P + (b + 1) * P] if f < 2 else \
                            attr_rows[:, b, f - 2:3 * P:3]
                        last = T.transpose(bank[n % 4][:, (b - b0) * P:(b - b0 + 1) * P], r, ident[:, :])
                    last.then_inc(turned, 1)
                    n += 1
            pe.wait_ge(turned_out, n)

            T.matmul(bank[2][0:NT, 0:P], zero_b[:, 0:NT], zero_b[:, :], start=True, stop=False)
            with pe.Fori(0, NCH // 2) as c:
                for b in range(2):
                    pe.wait_ge(hots, c * 2 + (b + 1 + LEAD))
                    for i in range(CHUNK):
                        last = T.matmul(bank[2][0:NT, 0:P], hi_hot[:, b, i, :], lo_hot[:, b, i, :], start=False, stop=False)
                    last.then_inc(chunk_mm, 1)
            T.matmul(bank[2][0:NT, 0:P], zero_b[:, 0:NT], zero_b[:, :], start=False, stop=True).then_inc(deg_mm, 1)
            pe.wait_ge(deg_row, 1)
            T.transpose(bank[3][:, 0:NT], deg[:, :], ident[0:NT, 0:NT]).then_inc(deg_t, 1)
            half = GROUPS * PASSES // 2
            T.matmul(bank[0][:, 0:STEPS], ones[0:1, :], edge[0:1, 0:TILES:TPS, 1], start=True, stop=True)
            T.matmul(bank[1][:, 0:half], ones[0:1, :], edge[0:1, 0:TILES // 2:2, 1], start=True, stop=True)
            pe.wait_ge(deg_mm, 1)
            pe.wait_ge(scale_done, 1)
            T.matmul(bank[2][:, 0:half], ones[0:1, :], edge[0:1, TILES // 2:TILES:2, 1], start=True, stop=True).then_inc(based_mm, 1)

            def node_product(base, weights, w, extra=None):
                def turn(n, b):
                    pe.wait_ge(h_done, n + (base + 1))
                    pe.wait_ge(hT_out, n + (base - 1 + LEAD))
                    T.transpose(bank[6 + b][:, 0:P], hrow[:, b, :], ident[:, :]).then_inc(h_turned, 1)

                def prod(n, b):
                    pe.wait_ge(hT_out, n + (base + 1 + LEAD))
                    pe.wait_ge(node_ev, n + (base - 1 + LEAD))
                    T.matmul(bank[4 + b][:, 0:w], hrowT[:, b, :], weights, start=True, stop=True).then_inc(node_mm, 1)
                for b in range(2):
                    turn(b, b)
                with pe.Fori(0, NT // 2 - 1) as t:
                    for b in range(2):
                        prod(t * 2 + b, b)
                        turn(t * 2 + (b + 2), b)
                for b in range(2):
                    prod(NT - 2 + b, b)

            pe.wait_ge(ld_w, 16 * 19)
            node_product(0, bases[:, :, :].rearrange("p b d -> p (b d)"), NB * D)
            pe.wait_ge(ext_ok, 1)
            T.transpose(bank[0][0:5, 0:P], ext[:, 0:5], ident[:, :]).then_inc(ext_mm, 1)
            pe.wait_ge(viol_ok, 1)
            T.matmul(bank[1][0:1, 0:1], ext_t[0:5, 1:2], ones[0:5, 0:1], start=True, stop=True).then_inc(viol_mm, 1)
            flag = window_flag(pe)
            pe.wait_ge(layer_in, 1)

            def spread(k, j, q):
                S, L = K[k], int(k[1])
                pe.wait_ge(S["staged"], steps(j, q + 1))
                pe.wait_ge(S["same_ok"], steps(j, q))
                for i in range(TPS):
                    last = T.transpose(bank[2][:, i * P:(i + 1) * P], st_edge[:, q % RING, i, L:L + 1].to_broadcast([P, P]), ident[:, :])
                last.then_inc(S["spread"], 1)

            def rank(k, j, q):
                S = K[k]
                pe.wait_ge(S["same_ok"], steps(j, q + 1))
                pe.wait_ge(S["sidx_ok"], steps(j, q - 1))
                for i in range(TPS):
                    last = T.matmul(bank[3][:, TPS * (q % 2) + i:TPS * (q % 2) + i + 1], same[:, q % 2, i, :], pcol[:, 1:2], start=True, stop=True)
                last.then_inc(S["ranked"], 1)

            with pe.If(flag == 0):
                F = K["f0"]

                def coefs(j, q):
                    pe.wait_ge(F["hot_ok"], steps(j, q + 1))
                    pe.wait_ge(F["le_ok"], steps(j, q - 1))
                    for i in range(TPS):
                        last = T.matmul(bank[6 + q % 2][:, NB * i:NB * (i + 1)], thot[:, q % 2, i * P:(i + 1) * P], table[:, :], start=True, stop=True)
                    last.then_inc(F["coef_mm"], 1)
                spread("f0", 0, 0)
                coefs(0, 0)
                spread("f0", 0, 1)
                coefs(0, 1)
                rank("f0", 0, 0)
                with pe.Fori(0, PASSES) as j:
                    for q in range(RING):
                        pe.wait_ge(F["le_ok"], steps(j, q + 1))
                        pe.wait_ge(F["m_ok"], steps(j, q - 1))
                        for i in range(TPS):
                            last = T.matmul(bank[4 + q % 2][:, i * P:(i + 1) * P], wedge[:, q % 2, i, :], same[:, q % 2, i, :], start=True, stop=True)
                        last.then_inc(F["m_mm"], 1)
                        rank("f0", j, q + 1)
                        spread("f0", j, q + 2)
                        coefs(j, q + 2)
                        pe.wait_ge(F["m_ok"], steps(j, q + 1))
                        pe.wait_ge(win_in[q % TPS], j * (16 * RING // TPS) + 16 * (q // TPS + 1))
                        pe.wait_ge(F["sum_ok"], steps(j, q - 1))
                        for i in range(TPS):
                            last = T.matmul(bank[q % 2][:, i * D:(i + 1) * D], wsum[:, q % 2, i * P:(i + 1) * P], win[:, q % TPS, :], start=True, stop=True)
                        last.then_inc(F["summed"], 1)
            with pe.Else():
                G = K["g0"]
                with pe.Fori(0, NCH // 2) as c:
                    for b in range(2):
                        pe.wait_ge(typ_hots, c * 2 + (b + 1 + LEAD))
                        pe.wait_ge(coef_out, c * 2 + (b - 1 + LEAD))
                        for i in range(CHUNK):
                            last = T.matmul(bank[b][:, i * NB:(i + 1) * NB], typ_hot[:, b, i * P:(i + 1) * P], table[:, :], start=True, stop=True)
                        last.then_inc(coef_mm, 1)
                pe.wait_ge(coef_out, NCH + LEAD)
                spread("g0", 0, 0)
                rank("g0", 0, 0)
                with pe.Fori(0, PASSES) as j:
                    for q in range(RING):
                        spread("g0", j, q + 1)
                        rank("g0", j, q + 1)
                        pe.wait_ge(G["scaled"], steps(j, q + 1))
                        pe.wait_ge(G["sum_ok"], steps(j, q - 1))
                        for i in range(TPS):
                            for b in range(NB):
                                last = T.matmul(bank[q % 2][:, i * D:(i + 1) * D], same[:, q % 2, i, :], gat0[:, q % GSLOT0, i, b * D:(b + 1) * D],
                                                start=(b == 0), stop=(b == NB - 1))
                        last.then_inc(G["summed"], 1)

            pe.wait_ge(wprep, 1)
            node_product(NT, w_up[:, :], D)
            pe.wait_ge(emb_a, 2 * len(EMB_PARTS))

            def mlp(k, j, q):
                S = K[k]
                pe.wait_ge(S["h1_ok"], steps(j, q))
                T.matmul(bank[6][:, 0:256], w_m0[:, q % RING, :], emb[:, bass.ds((j + q // RING) * 256, 256)], start=True, stop=True).then_inc(S["h0_mm"], 1)
                pe.wait_ge(S["h0_ok"], steps(j, q + 1))
                T.matmul(bank[6][:, 256:512], w_m1[:, :], hid0, start=True, stop=True).then_inc(S["h1_mm"], 1)

            def mlp_out(k, j, q):
                S = K[k]
                pe.wait_ge(S["mids_ok"], steps(j, q - 1))
                wb = bank[4 + q % 2]
                T.matmul(wb[:, :], ones[:, :], b2_four[:, :, :].rearrange("o i d -> o (i d)"), start=True, stop=False)
                pe.wait_ge(S["h1_ok"], steps(j, q + 1))
                for i in range(TPS):
                    last = T.matmul(wb[:, i * P:(i + 1) * P], hid1[:, (i % 2) * P:(i % 2 + 1) * P], w_m2[:, i // 2, :], start=False, stop=(i == TPS - 1))
                last.then_inc(S["w_mm"], 1)

            with pe.If(flag == 0):
                F = K["f1"]
                mlp("f1", 0, 0)
                mlp_out("f1", 0, 0)
                with pe.Fori(0, PASSES) as j:
                    for q in range(RING):
                        h = q // 2
                        mlp("f1", j, q + 1)
                        pe.wait_ge(F["near_ok"], steps(j, q + 1))
                        if q % 2 == 0:
                            pe.wait_ge(F["sum_ok"], j * (RING // 2) + (h - 1 + LEAD))
                        pe.wait_ge(F["mids_ok"], steps(j, q + 1))
                        for i in range(TPS):
                            c = 2 * (q % 2) + i // 2
                            last = T.matmul(bank[h % 2][WIN * c:WIN * (c + 1), 0:2 * D], near1[:, q % 2, i, :], mid[:, q % 2, i, :],
                                            start=(i % 2 == 0), stop=(i % 2 == 1))
                        last.then_inc(F["summed"], 1)
                        mlp_out("f1", j, q + 1)
            with pe.Else():
                G = K["g1"]
                spread("g1", 0, 0)
                mlp("g1", 0, 0)
                mlp_out("g1", 0, 0)
                rank("g1", 0, 0)
                with pe.Fori(0, PASSES) as j:
                    for q in range(RING):
                        spread("g1", j, q + 1)
                        mlp("g1", j, q + 1)
                        mlp_out("g1", j, q + 1)
                        rank("g1", j, q + 1)
                        pe.wait_ge(G["mids_ok"], steps(j, q + 1))
                        pe.wait_ge(G["sum_ok"], steps(j, q))
                        for i in range(TPS):
                            last = T.matmul(bank[i // 2][:, (i % 2) * 2 * D:(i % 2 + 1) * 2 * D], same[:, q % 2, i, :], mid[:, q % 2, i, :], start=True, stop=True)
                        last.then_inc(G["summed"], 1)

            def turn(k, b, t):
                n = k * (2 * DB) + (b * DB + t)
                m = (b * DB + t) % 2
                if t == 0:
                    pe.wait_ge(ld_fold[b], k * 16 + 16)
                pe.wait_ge(fold_c, n + (LEAD - 1))
                for h in range(2):
                    last = T.transpose(bank[6 + m][:, h * P:(h + 1) * P], fold_in[:, b, t, h * P:(h + 1) * P], ident[:, :])
                last.then_inc(fold_t, 1)

            def prod(k, b, t):
                n = k * (2 * DB) + (b * DB + t)
                m = (b * DB + t) % 2
                pe.wait_ge(fold_c, n + (LEAD + 1))
                pe.wait_ge(x_done, n + (LEAD - 1))
                for h in range(2):
                    last = T.matmul(bank[4 + m][:, 0:D], tT[:, m, h * P:(h + 1) * P], w_o[:, h, :], start=(h == 0), stop=(h == 1))
                last.then_inc(fold_mm, 1)
            pe.wait_ge(layer_done[1], 1)
            with pe.Fori(0, NT // DB // 2) as k:
                for m in range(2 * DB):
                    turn(k, m // DB, m % DB)
                    if m:
                        prod(k, (m - 1) // DB, (m - 1) % DB)
                prod(k, 1, DB - 1)


INPUTS = ("x", "src", "dst", "edge_attr_3", "edge_type_50", "edge_weight", "L0_gnn_bases", "L0_gnn_comps",
          "L0_gnn_alpha", "L1_gnn_W_up0", "L1_gnn_W_up1", "L1_gnn_mlp_w0", "L1_gnn_mlp_b0", "L1_gnn_mlp_w1",
          "L1_gnn_mlp_b1", "L1_gnn_mlp_w2", "L1_gnn_mlp_b2", "L1_gnn_W_out0", "L1_gnn_W_out1")


def constants():
    p = np.arange(P)
    pcol = np.zeros((P, 8), np.float32)
    pcol[:, 0] = p
    pcol[:, 1] = 2.0 ** (63 - p)
    pcol[:, 2] = 2.5 * 2.0 ** (63 - p)
    pcol[:, 3] = (NT - 1) * P + p
    pcol[:, 4] = -(p % CENTERS)
    pcol[:, 5] = p % WIN
    pcol[0:5, 6] = [WIN - 1, 0, WIN - 1, 0, -WIN]
    return {"c_ident": np.eye(P, dtype=np.float32), "c_iota": np.tile(p.astype(np.float32), (P, 1)), "c_pcol": pcol}


def kernel(**inputs):
    import concourse.bacc as bacc
    from concourse.bass_utils import run_bass_kernel_spmd

    nc = bacc.Bacc("TRN2", target_bir_lowering=False, num_devices=1)
    arrays = {n: np.ascontiguousarray(inputs[n]) for n in INPUTS} | constants()
    aps = {n: nc.dram_tensor(f"in_{n}", v.shape, mybir.dt.from_np(v.dtype), kind="ExternalInput").ap() for n, v in arrays.items()}
    out = nc.dram_tensor("out", [NODES, D], F32, kind="ExternalOutput").ap()
    build(nc, aps, out)
    r = run_bass_kernel_spmd(nc, [{f"in_{n}": v for n, v in arrays.items()}], core_ids=[0])
    return r.results[0]["out"]
```

```python
import numpy as np
import concourse.bass as bass
import concourse.mybir as mybir
from contextlib import ExitStack

F32, BF16, I32 = mybir.dt.float32, mybir.dt.bfloat16, mybir.dt.int32
ALU = mybir.AluOpType
ACT = mybir.ActivationFunctionType
AXX = mybir.AxisListType.X

P = 128
D = 128
NODES = 6250
NT = -(-NODES // P) + 1
NPAD = NT * P
EDGES = 200000
TPS = 4
RING = 8
GROUPS = 16
TILES = 1568
PASSES = TILES // (TPS * RING)
STEPS = TILES // TPS
BLOCKS = 13
COLS = BLOCKS * P
WIN = P // 4
LEAD = 8
ADD_LEAD = 2
QUARTER = STEPS // 4
STEP_EDGES = TPS * P
ACCS = 2 * TPS
SLOTS = 5
FIRST = 6
EARLY = 8
PAD_NODE = NODES
NB = 4
NREL = 50
CENTERS = 8
HID = 64
MUL = 32
GSLOT = 4
GSLOT0 = 2
CHUNK = 16
NCH = TILES // CHUNK
EPS = 1e-5
DB = 5
SQ3 = 3.0 ** 0.5


def build(nc, a, out):
    ctx = ExitStack()
    with ctx:
        def sb(name, shape, dt=F32):
            return ctx.enter_context(nc.sbuf_tensor(name, shape, dt))

        def ps(name, shape, dt=F32):
            return ctx.enter_context(nc.psum_tensor(name, shape, dt))

        def sem(name):
            return ctx.enter_context(nc.semaphore(name))

        def dram(name, shape):
            return nc.dram_tensor(name, shape, F32, kind="Internal").ap()

        ytab = dram("ytab", [NPAD, NB * D])
        xtab = dram("xtab", [NPAD, D])
        acc0 = [dram(f"acc0_{i}", [NPAD, D]) for i in range(ACCS)]
        acc1 = dram("acc1", [NPAD, 2 * D])

        xn = sb("xn", [P, NT, D])
        edge = sb("edge", [P, COLS, 6])
        arena = sb("arena", [P, 12800])
        emb = arena
        rows_i = arena[:, 0:BLOCKS * 5 * P].bitcast(I32)
        src_rows = rows_i[:, 0:BLOCKS * P].rearrange("q (j e) -> q j e", j=BLOCKS)
        dst_rows = rows_i[:, BLOCKS * P:2 * BLOCKS * P].rearrange("q (j e) -> q j e", j=BLOCKS)
        attr_rows = arena[:, 2 * BLOCKS * P:5 * BLOCKS * P].rearrange("q (j e) -> q j e", j=BLOCKS)
        TY0 = BLOCKS * 5 * P
        typ = arena[0:64, TY0:TY0 + 2 * CHUNK * P].bitcast(I32).rearrange("q (b e) -> q b e", b=2)
        accin = arena[:, 12800 - 2 * ACCS * DB * D:12800].rearrange("p (b r x) -> p b r x", b=2, r=ACCS)
        coef_mem = sb("coef_mem", [P, COLS * NB])
        mid = coef_mem[:, 0:2 * TPS * 2 * D].rearrange("p (s i x) -> p s i x", s=2, i=TPS)
        M0 = 2 * TPS * 2 * D
        hid0 = coef_mem[:, M0:M0 + 256]
        hid1 = coef_mem[:, M0 + 256:M0 + 512]
        w01s = coef_mem[:, M0 + 512:M0 + 640].rearrange("p (i x) -> p i x", i=TPS)
        vdot = coef_mem[:, M0 + 768:M0 + 1152].rearrange("p (i c k) -> p i c k", i=TPS, c=3)
        vsum = coef_mem[:, M0 + 1152:M0 + 1408].rearrange("p (i c k) -> p i c k", i=TPS, c=2)
        gmem = sb("gmem", [P, GSLOT0 * TPS * NB * D])
        gat0 = gmem[:, :].rearrange("p (s i x) -> p s i x", s=GSLOT0, i=TPS)
        gat1 = gmem[:, 0:GSLOT * TPS * D].rearrange("p (s i x) -> p s i x", s=GSLOT, i=TPS)
        OH = 2 * CHUNK * P
        typ_hot = gmem[0:64, 0:OH].rearrange("p (b e) -> p b e", b=2)
        lo_hot = gmem[:, 0:CHUNK * P].bitcast(BF16).rearrange("p (b x t) -> p b x t", b=2, x=P)
        HI0 = CHUNK * P
        hi_hot = gmem[:, HI0:HI0 + CHUNK * NT].bitcast(BF16).rearrange("p (b x t) -> p b x t", b=2, x=NT)
        src_i, src_hi = (coef_mem[:, n * COLS:(n + 1) * COLS].bitcast(I32) for n in range(2))
        W0 = 2 * COLS
        wbase = coef_mem[:, W0:W0 + STEPS]
        wgap = coef_mem[:, W0 + 400:W0 + 400 + STEPS - QUARTER]
        iota_rep = coef_mem[:, W0 + 800:W0 + 800 + CHUNK * P // 2].bitcast(BF16).rearrange("p (x t) -> p x t", x=P)
        hT_all = arena[:, 0:NT * P]
        thot = coef_mem[0:64, 0:1024].rearrange("p (s e) -> p s e", s=2)
        wedge = coef_mem[:, 1024:2048].rearrange("p (s i x) -> p s i x", s=2, i=TPS)
        wsum = coef_mem[:, 2048:3072].rearrange("p (s x) -> p s x", s=2)
        win = coef_mem[:, 3072:3584].rearrange("p (s x) -> p s x", s=TPS)
        near = coef_mem[:, 3584:3840].rearrange("p (s i x) -> p s i x", s=2, i=TPS)
        near1 = coef_mem[:, M0 + 1408:M0 + 1664].rearrange("p (s i x) -> p s i x", s=2, i=TPS)
        above = coef_mem[:, M0 + 1664:M0 + 1920]
        node_out = gmem[:, 0:SLOTS * 512].rearrange("p (b x) -> p b x", b=SLOTS)
        sum_out = sb("sum_out", [P, 2, TPS, 2 * D])
        sum_out0 = sum_out[:, :, :, :].rearrange("p s i x -> p (s i x)").rearrange("p (s i x) -> p s i x", s=TPS, i=TPS)
        fold_in = arena[:, 0:2 * DB * 2 * D].rearrange("p (b t x) -> p b t x", b=2, t=DB)
        same = sb("same", [P, 2, TPS, P])
        zero = sb("zero", [P, 800])
        ident = sb("ident", [P, P])
        iota = sb("iota", [P, P])
        pcol = sb("pcol", [P, 8])
        digits = sb("digits", [P, 2, COLS], BF16)
        lo, hi = digits[:, 0, :], digits[:, 1, :]
        usq, ulen = sb("usq", [P, RING * TPS, 3]), sb("ulen", [P, RING * TPS])
        base_row = sb("base_row", [1, 400], I32)
        fidx_all = sb("fidx_all", [P, QUARTER])
        fidx = sb("fidx", [P, 4], I32)
        ext = sb("ext", [P, 8])
        ext_t = sb("ext_t", [8, 2])
        flags = sb("flags", [1, 2], I32)
        st_edge = sb("st_edge", [P, RING, TPS, 6])
        gidx = sb("gidx", [P, RING, TPS], I32)
        sidx = sb("sidx", [P, TPS, TPS], I32)
        dupd = sb("dupd", [P, TPS])
        bases = sb("bases", [P, NB, D])
        table = sb("table", [64, NB])
        alpha = sb("alpha", [64, 1])
        w_up = sb("w_up", [P, D])
        w_m0 = sb("w_m0", [P, GROUPS // 2, P])
        w_m1 = sb("w_m1", [P, P])
        w_m2 = sb("w_m2", [P, 2, P])
        b_m = sb("b_m", [P, 2])
        b2_rows, b2_part = sb("b2_rows", [65, D]), sb("b2_part", [65, D], BF16)
        b2_parts = sb("b2_parts", [65, TPS, D], BF16)
        ones_b = sb("ones_b", [P, P], BF16)
        ones = sb("ones", [P, P])
        w_o = sb("w_o", [P, 2, D])
        w_o1 = sb("w_o1", [P, MUL])
        zero_b = sb("zero_b", [P, P], BF16)
        stats = sb("stats", [P, NT, 6])
        rstd = sb("rstd", [P, NT])
        nbias = sb("nbias", [P, NT])
        dinv = sb("dinv", [P, NT])
        dpos = sb("dpos", [P, NT])
        hrow = sb("hrow", [P, 2, D])
        hrowT = sb("hrowT", [P, 2, D])
        tT = sb("tT", [P, 2, 2 * D])
        moment = sb("moment", [P, 3, NT])

        bank = [ps(f"bank{i}", [P, 512]) for i in range(8)]

        ld_src, ld_dst, ld_attr, ld_x, ld_const = (sem(f"ld_{k}") for k in ("src", "dst", "attr", "x", "const"))
        ld_w, ld_w0 = sem("ld_w"), sem("ld_w0")
        padded = sem("padded")
        zeroed = sem("zeroed")
        ld_typ = [sem("ld_typ0"), sem("ld_typ1")]
        rows_ok = sem("rows_ok")
        turned = sem("turned")
        turned_out = sem("turned_out")
        dve_own = sem("dve_own")
        hots, chunk_mm = sem("hots"), sem("chunk_mm")
        deg_mm = sem("deg_mm")
        rows_done, rows_turned, rows_kept, sliced = (sem(k) for k in ("rows_done", "rows_turned", "rows_kept", "sliced"))
        unit_own = [sem(f"unit_own{n}") for n in range(4)]
        unit_sq, unit_root, unit_ok = sem("unit_sq"), sem("unit_root"), sem("unit_ok")
        pool_own = sem("pool_own")
        vec_done, root_done = sem("vec_done"), sem("root_done")
        scale_done = sem("scale_done")
        wprep = sem("wprep")
        based, based_mm = sem("based"), sem("based_mm")
        windows_ok = sem("windows_ok")
        ext_ok, ext_mm, viol_ok, viol_mm = sem("ext_ok"), sem("ext_mm"), sem("viol_ok"), sem("viol_mm")
        flag_ok = sem("flag_ok")
        typ_hots, coef_mm, coef_out = sem("typ_hots"), sem("coef_chunk_mm"), sem("coef_out")
        h_done, h_turned, hT_out, node_mm, node_ev = (sem(k) for k in ("h_done", "h_turned", "hT_out", "node_mm", "node_ev"))
        st_tab = [sem(f"st_tab{n}") for n in range(SLOTS)]
        ld_acc = [sem("ld_acc0"), sem("ld_acc1")]
        acc_used, x_done = sem("acc_used"), sem("x_done")
        blk = [sem(f"blk{n}") for n in range(9)]
        carried = sem("carried")
        blk_var, blk_root, blk_ok = sem("blk_var"), sem("blk_root"), sem("blk_ok")
        layer_in = sem("layer_in")
        emb_ld, emb_ld2, emb_b, emb_v, emb_a, emb_ok = (sem(k) for k in ("emb_ld", "emb_ld2", "emb_b", "emb_v", "emb_a", "emb_ok"))
        ld_fold = [sem("ld_fold0"), sem("ld_fold1")]
        fold_t, fold_c, fold_mm = sem("fold_t"), sem("fold_c"), sem("fold_mm")
        layer_done = [sem("layer_done0"), sem("layer_done1")]
        pool_done = [sem("pool_done0"), sem("pool_done1")]
        st_out = sem("st_out")

        COUNTS = {
            0: {"dve": "staged hot_ok near_ok same_ok le_ok tmp_ok sidx_ok", "pe": "spread coef_mm m_mm ranked summed",
                "act": "m_ok scaled sum_ok", "pool": "out_free let_go"},
            1: {"dve": "staged near_ok same_ok tmp_ok sidx_ok mids_ok", "pe": "spread ranked h0_mm h1_mm w_mm summed",
                "act": "h0_ok h1_ok sum_ok", "pool": "out_free let_go"},
        }
        K = {}
        for k, v in COUNTS.items():
            K[f"f{k}"] = K[f"g{k}"] = {n: sem(f"{n}_l{k}") for names in v.values() for n in names.split()}
        added0, added1 = [sem(f"added0_{i}") for i in range(ACCS)], [sem("added1")]
        added = {"f0": added0, "g0": added0, "f1": added1, "g1": added1}
        got0, got1 = [sem(f"got0_{i}") for i in range(GSLOT0)], [sem(f"got1_{i}") for i in range(GSLOT)]
        got = {"g0": got0, "f1": got1, "g1": got1}
        win_in = [sem(f"win_in{i}") for i in range(TPS)]
        mids_own = [sem(f"mids_own{n}") for n in range(4)]
        MORE = {"pe": [chunk_mm, node_mm, rows_turned, h_turned, fold_t, fold_mm, coef_mm], "act": [hT_out, node_ev, coef_out, fold_c, emb_a, emb_ok, rows_kept],
                "dve": [x_done, acc_used, hots, typ_hots, emb_b, emb_v, sliced, unit_ok], "pool": [], "sp": []}

        def start(eng, who):
            for k, v in COUNTS.items():
                for n in v.get(who, "").split():
                    eng.sem_inc(K[f"f{k}"][n], LEAD)
            for s in MORE[who]:
                eng.sem_inc(s, LEAD)
            if who == "sp":
                for s in st_tab:
                    eng.sem_inc(s, 16 * LEAD)

        def steps(j, n):
            return j * RING + (n + LEAD)

        def hold(eng):
            eng.wait_ge(padded, 1)

        def window_flag(eng):
            eng.wait_ge(flag_ok, 1)
            return eng.value_load(flags[0:1, 0:1], min_val=0, max_val=8)

        block = ctx.enter_context(nc.Block())
        turn_bank = [bank[n] for n in (0, 1, 3, 4)]
        assert (STEPS - 1) * STEP_EDGES >= EDGES and 2 * FIRST < NCH // 2 - NT // 2
        full = 12 * P * P
        more = EDGES // P - 12 * P
        tail = EDGES % P
        whole, rest = NODES // P, NODES % P
        TYPES = CHUNK * P
        LASTTYPES = EDGES - (NCH - 1) * TYPES

        @block.sync
        def _(sp):
            start(sp, "sp")
            sp.dma_start(ident[:, :], a["c_ident"]).then_inc(ld_const, 16)
            sp.dma_start(iota[:, :], a["c_iota"]).then_inc(ld_const, 16)
            sp.dma_start(pcol[:, :], a["c_pcol"]).then_inc(ld_const, 16)
            sp.wait_ge(padded, 1)
            for v, name, w, s in ((src_rows, "src", 1, ld_src), (dst_rows, "dst", 1, ld_dst), (attr_rows, "edge_attr_3", 3, ld_attr)):
                d = a[name] if w == 1 else a[name].rearrange("e c -> (e c)")
                sp.dma_start(v[:, 0:12, :], d[0:full * w].rearrange("(j q e) -> q j e", q=P, e=P * w)).then_inc(s, 16)
                sp.dma_start(v[0:more, 12, :], d[full * w:(full + more * P) * w].rearrange("(q e) -> q e", e=P * w)).then_inc(s, 16)
                sp.dma_start(v[more:more + 1, 12, 0:tail * w], d[(full + more * P) * w:EDGES * w].rearrange("(q e) -> q e", q=1)).then_inc(s, 16)
                if name == "src":
                    sp.dma_start(xn[:, 0:whole, :], a["x"][0:whole * P, :].rearrange("(t p) d -> p t d", p=P)).then_inc(ld_x, 16)
                    sp.dma_start(xn[0:rest, whole, :], a["x"][whole * P:NODES, :]).then_inc(ld_x, 16)
            sp.wait_ge(padded, 2)
            sp.dma_start(table[0:NREL, :], a["L0_gnn_comps"]).then_inc(ld_w, 16)
            sp.dma_start(alpha[0:NREL, :], a["L0_gnn_alpha"]).then_inc(ld_w, 16)
            sp.dma_start(bases[:, :, :], a["L0_gnn_bases"].rearrange("b d f -> d b f")).then_inc(ld_w, 16)
            sp.dma_start(w_up[0:MUL, 0:MUL], a["L1_gnn_W_up0"]).then_inc(ld_w, 16)
            for c in range(3):
                sp.dma_start(w_up[MUL + c:MUL + c + 3 * (MUL - 1) + 1:3, MUL * (c + 1):MUL * (c + 2)], a["L1_gnn_W_up1"]).then_inc(ld_w, 16)
            for q in range(GROUPS // 2):
                for h in range(2):
                    r = 2 * CENTERS * q + CENTERS * h
                    sp.dma_start(w_m0[r:r + CENTERS, q, HID * h:HID * (h + 1)], a["L1_gnn_mlp_w0"]).then_inc(ld_w0, 16)
            for h in range(2):
                r = slice(HID * h, HID * (h + 1))
                sp.dma_start(w_m1[r, r], a["L1_gnn_mlp_w1"]).then_inc(ld_w, 16)
                sp.dma_start(w_m2[r, h, :], a["L1_gnn_mlp_w2"]).then_inc(ld_w, 16)
                sp.dma_start(b_m[r, 0:1], a["L1_gnn_mlp_b0"].rearrange("(p o) -> p o", o=1)).then_inc(ld_w, 16)
                sp.dma_start(b_m[r, 1:2], a["L1_gnn_mlp_b1"].rearrange("(p o) -> p o", o=1)).then_inc(ld_w, 16)
                sp.dma_start(w_o1[r, :], a["L1_gnn_W_out1"]).then_inc(ld_w, 16)
            for n in range(3):
                sp.dma_start(b2_rows[32 * n:32 * n + 1, :], a["L1_gnn_mlp_b2"].rearrange("(o f) -> o f", o=1)).then_inc(ld_w, 16)
            sp.dma_start(w_o[0:2 * MUL, 0, 0:MUL], a["L1_gnn_W_out0"]).then_inc(ld_w, 16)
            for acc, w in [(x, D) for x in acc0] + [(acc1, 2 * D)]:
                k = NPAD * w // P // 800
                sp.dma_start(acc.rearrange("(p r) d -> p (r d)", p=P).rearrange("p (k x) -> p k x", k=k),
                             zero[:, :].unsqueeze(1).to_broadcast([P, k, 800])).then_inc(zeroed, 16)

            def types(b, e0, n=TYPES):
                sp.dma_start(typ[:, b, 0:n], a["edge_type_50"].rearrange("(o e) -> o e", o=1)[:, bass.ds(e0, n)].to_broadcast([64, n])).then_inc(ld_typ[b], 16)
            types(0, 0)
            types(1, TYPES)

            def tables(tab, w):
                with sp.Fori(0, NT // (2 * SLOTS)) as t:
                    for m in range(2 * SLOTS):
                        sp.wait_ge(node_ev, t * (2 * SLOTS) + (m + 1 + LEAD))
                        sp.dma_start(tab[bass.ds(t * (2 * SLOTS * P) + m * P, P), :], node_out[:, m % SLOTS, 0:w]).then_inc(st_tab[m % SLOTS], 16)
            tables(ytab, NB * D)
            def emb_rows(c, m):
                r = 2 * CENTERS * (m // 2 * 4 + c) + CENTERS * (m % 2)
                return slice(r, r + CENTERS)

            def weights(p0, p1, done):
                for g in range(GROUPS):
                    c, m = g // 4, g % 4
                    e0, n = c * QUARTER * STEP_EDGES, min(p1, PASSES - (c == 3))
                    w = a["edge_weight"][e0 + p0 * 1024:e0 + n * 1024].rearrange("(j m e) -> m j e", m=4, e=256)
                    sp.dma_start(emb[emb_rows(c, m), p0 * 256:n * 256].rearrange("p (j e) -> p j e", e=256),
                                 w[m:m + 1].to_broadcast([CENTERS, n - p0, 256])).then_inc(done, 16)
            weights(0, EARLY, emb_ld)
            flag = window_flag(sp)
            for b in range(SLOTS):
                sp.wait_ge(st_tab[b], 16 * (NT // SLOTS + LEAD))
            rows = ytab.rearrange("n (b d) -> (n b) d", b=NB)
            with sp.If(flag == 0):
                F = K["f0"]

                def window(j, q):
                    node = sp.value_load(base_row[0:1, bass.ds(j * RING + q, 1)], min_val=0, max_val=PAD_NODE)
                    sp.wait_ge(F["summed"], steps(j, q - TPS + 1))
                    sp.dma_start(win[:, q % TPS, :], rows[bass.ds(node * NB, P), :]).then_inc(win_in[q % TPS], 16)

                def one_pass(j, loads):
                    for q in range(RING):
                        window(j, q)
                        if q % 4 == 3 and q // 4 < len(loads):
                            b = q // 4
                            sp.wait_ge(F["hot_ok"], steps(j, q + 1))
                            types(b, *loads[b])
                with sp.Fori(0, PASSES - 2) as j:
                    one_pass(j, [(j * (2 * TYPES) + 2 * TYPES, TYPES), (j * (2 * TYPES) + 3 * TYPES, TYPES)])
                one_pass(PASSES - 2, [((NCH - 2) * TYPES, TYPES), ((NCH - 1) * TYPES, LASTTYPES)])
                one_pass(PASSES - 1, [(0, TYPES)])
                sp.wait_ge(F["hot_ok"], STEPS + 2 + LEAD)
                for i in range(ACCS):
                    sp.wait_ge(added["f0"][i], 16 * (STEPS // 2 + ADD_LEAD - i // TPS))
            with sp.Else():
                with sp.Fori(1, NCH // 2 - 1) as c:
                    for b in range(2):
                        sp.wait_ge(typ_hots, c * 2 + (b - 1 + LEAD))
                        types(b, c * (2 * TYPES) + b * TYPES)
                sp.wait_ge(typ_hots, NCH - 3 + LEAD)
                types(0, (NCH - 2) * TYPES)
                sp.wait_ge(typ_hots, NCH - 2 + LEAD)
                types(1, (NCH - 1) * TYPES, LASTTYPES)
                sp.wait_ge(typ_hots, NCH + LEAD)
                for i in range(ACCS):
                    sp.wait_ge(added["g0"][i], 16 * (STEPS // 2 + ADD_LEAD))
            sp.sem_inc(layer_done[0], 1)

            def bring(k, b):
                for r in range(ACCS):
                    sp.dma_start(accin[:, b, r, :].rearrange("p (t d) -> p t d", t=DB),
                                 acc0[r][bass.ds(k * (DB * P), DB * P), :].rearrange("(t p) d -> p t d", p=P)).then_inc(ld_acc[b], 16)
            def store_block(k, b):
                for m in range(DB):
                    sp.wait_ge(node_ev, k * DB + (NT + m + 1 + LEAD))
                    sp.dma_start(xtab[bass.ds(k * (DB * P) + m * P, P), :], node_out[:, m, 0:D]).then_inc(st_tab[m], 16)

            def bring_next(k, b):
                sp.wait_ge(acc_used, k + (LEAD - 1))
                bring(k, b)
            BLK = NT // DB
            bring(0, 0)
            bring(1, 1)
            bring_next(2, 0)
            with sp.Fori(0, BLK // 2 - 2) as k:
                for b in range(2):
                    bring_next(k * 2 + (b + 3), 1 - b)
                    store_block(k * 2 + b, b)
            bring_next(BLK - 1, 1)
            store_block(BLK - 4, 0)

            for k in range(BLK - 3, BLK):
                store_block(k, k % 2)
            sp.wait_ge(acc_used, NT // DB + LEAD)
            weights(EARLY, PASSES, emb_ld2)
            for m in range(2):
                e0 = EDGES // 1024 * 1024 + m * 256
                n = min(256, EDGES - e0)
                sp.dma_start(emb[emb_rows(3, m), (PASSES - 1) * 256:(PASSES - 1) * 256 + n],
                             a["edge_weight"].rearrange("(o e) -> o e", o=1)[:, e0:e0 + n].to_broadcast([CENTERS, n])).then_inc(emb_ld2, 16)
            with sp.If(flag == 0):
                sp.wait_ge(added["f1"][0], 16 * (QUARTER + ADD_LEAD))
                sp.wait_ge(K["f1"]["w_mm"], STEPS + 2 + LEAD)
            with sp.Else():
                sp.wait_ge(added["g1"][0], 16 * (TILES + ADD_LEAD))
                sp.wait_ge(K["g1"]["w_mm"], STEPS + 1 + LEAD)
            sp.sem_inc(layer_done[1], 1)
            for k in range(NT // DB):
                if k >= 2:
                    sp.wait_ge(fold_c, (k - 1) * DB + LEAD)
                sp.dma_start(fold_in[:, k % 2, :, :], acc1[k * DB * P:(k + 1) * DB * P, :].rearrange("(t p) d -> p t d", p=P)).then_inc(ld_fold[k % 2], 16)
            for k in range(NT // DB):
                sp.wait_ge(x_done, (k + 1) * DB + LEAD)
                t1 = min((k + 1) * DB, whole)
                sp.dma_start(out[k * DB * P:t1 * P, :].rearrange("(t p) d -> p t d", p=P), xn[:, k * DB:t1, :]).then_inc(st_out, 16)
            sp.dma_start(out[whole * P:NODES, :], xn[0:rest, whole, :]).then_inc(st_out, 16)
            sp.wait_ge(st_out, 16 * (NT // DB + 1))

        @block.gpsimd
        def _(pool):
            start(pool, "pool")
            IX = bass.IndirectOffsetOnAxis

            def gather(k, tab, gat, slots, j, s):
                pool.wait_ge(K[k]["staged"], steps(j, s + 1))
                pool.sem_inc(K[k]["let_go"], 1)
                for i in range(TPS):
                    pool.indirect_dma_start(gat[:, s % slots, i, :], None, tab, IX(ap=gidx[:, s % RING, i:i + 1], axis=0)).then_inc(got[k][s % slots], 16)

            def add_step(k, j, q):
                S = K[k]
                pool.wait_ge(S["sidx_ok"], steps(j, q + 1))
                pool.wait_ge(S["sum_ok"], steps(j, q + 1))
                for i in range(TPS):
                    n = q % 2 * TPS + i
                    pool.wait_ge(added[k][n], j * (16 * RING // 2) + 16 * (q // 2 + ADD_LEAD))
                    pool.sem_inc(S["out_free" if i == TPS - 1 else "let_go"], 1)
                    pool.indirect_dma_start(acc0[n], IX(ap=sidx[:, q % TPS, i:i + 1], axis=0),
                                            sum_out0[:, q % TPS, i, :], None, compute_op=ALU.add).then_inc(added[k][n], 16)

            done = [0]

            def link(ins):
                done[0] += 1
                ins.then_inc(pool_own, 1)
                pool.wait_ge(pool_own, done[0])

            G_ = nc.gpsimd
            pool.wait_ge(ld_const, 48)
            pool.wait_ge(based, 1)
            link(G_.tensor_copy(base_row[0:1, 0:STEPS], wbase[0:1, :]))
            link(G_.tensor_tensor(edge[:, 0:TILES, 5].rearrange("p (s i) -> p s i", i=TPS), edge[:, 0:TILES, 1].rearrange("p (s i) -> p s i", i=TPS),
                                  wbase.unsqueeze(2).to_broadcast([P, STEPS, TPS]), ALU.subtract))
            for c in range(4):
                r = slice(WIN * c, WIN * (c + 1))
                link(G_.tensor_scalar(fidx_all[r, :], wbase[r, c * QUARTER:(c + 1) * QUARTER], pcol[r, 5:6], None, ALU.add))
            G_.tensor_tensor(wgap, wbase[:, QUARTER:], wbase[:, 0:STEPS - QUARTER], ALU.subtract).then_inc(windows_ok, 1)
            pool.wait_ge(windows_ok, 1)

            pool.wait_ge(ld_w, 16 * 21)
            pool.wait_ge(ld_w0, 16 * GROUPS)
            link(G_.tensor_scalar(w_up[:, :], w_up[:, :], MUL ** -0.5, None, ALU.mult))
            link(G_.tensor_scalar(w_m0[:, :, :], w_m0[:, :, :], CENTERS ** 0.5, None, ALU.mult))
            link(G_.tensor_scalar(w_m2[:, :, MUL:2 * MUL], w_m2[:, :, MUL:2 * MUL], SQ3, None, ALU.mult))
            link(G_.tensor_scalar(b2_rows[:, MUL:2 * MUL], b2_rows[:, MUL:2 * MUL], SQ3, None, ALU.mult))
            for n in range(3):
                link(G_.tensor_copy(b2_part[:, :], b2_rows[:, :]))
                link(G_.tensor_copy(b2_parts[32 * n:32 * n + 1, :, :], b2_part[32 * n:32 * n + 1, :].unsqueeze(1).to_broadcast([1, TPS, D])))
                if n < 2:
                    link(G_.tensor_tensor(b2_rows[:, :], b2_rows[:, :], b2_part[:, :], ALU.subtract))
            out_scale = (2 * MUL) ** -0.5 / 16.0
            h0, h1 = slice(0, 2 * MUL), slice(2 * MUL, 4 * MUL)
            link(G_.tensor_scalar(w_o[h0, 0, 0:MUL], w_o[h0, 0, 0:MUL], out_scale, None, ALU.mult))
            link(G_.tensor_scalar(w_o[h1, 0, MUL:D:3], w_o1[h1, :], out_scale, None, ALU.mult))
            link(G_.tensor_scalar(w_o[h0, 1, MUL + 1:D:3], w_o1[h0, :], out_scale, None, ALU.mult))
            G_.tensor_scalar(w_o[h1, 1, MUL + 2:D:3], w_o1[h1, :], out_scale, None, ALU.mult).then_inc(wprep, 1)
            pool.wait_ge(wprep, 1)

            pool.wait_ge(zeroed, 16 * (ACCS + 1))
            for acc, s in zip(acc0 + [acc1], added0 + added1):
                for n in range(ADD_LEAD):
                    r = (NT - 1) * P + n * WIN
                    pool.dma_start(acc[r:r + WIN, 0:D], zero[0:WIN, 0:D]).then_inc(s, 16)
            flag = window_flag(pool)
            with pool.If(flag == 0):
                with pool.Fori(0, PASSES - 1) as j:
                    for q in range(RING):
                        add_step("f0", j, q)
                for q in range(RING - 1):
                    add_step("f0", PASSES - 1, q)
            with pool.Else():
                G = K["g0"]
                for b in range(SLOTS):
                    pool.wait_ge(st_tab[b], 16 * (NT // SLOTS + LEAD))
                pool.wait_ge(layer_in, 1)
                for s in range(GSLOT0 - 1):
                    gather("g0", ytab, gat0, GSLOT0, 0, s)
                with pool.Fori(0, PASSES) as j:
                    for q in range(RING):
                        pool.wait_ge(G["summed"], steps(j, q))
                        gather("g0", ytab, gat0, GSLOT0, j, q + GSLOT0 - 1)
                        add_step("g0", j, q)
                for n in range(GSLOT0):
                    pool.wait_ge(got["g0"][n], 16 * TPS * (STEPS // GSLOT0 + (n < GSLOT0 - 1)))
            pool.sem_inc(pool_done[0], 1)

            for b in range(SLOTS):
                pool.wait_ge(st_tab[b], 16 * (2 * (NT // SLOTS) + LEAD))
            with pool.If(flag == 0):
                F = K["f1"]

                def one_pass(j, last):
                    for q in range(RING):
                        if not last or q + GSLOT - 1 < RING:
                            pool.wait_ge(F["mids_ok"], steps(j, q))
                            gather("f1", xtab, gat1, GSLOT, j, q + GSLOT - 1)
                        if q % 4 == 3:
                            h = q // 4
                            pool.wait_ge(F["sum_ok"], j * 2 + (h + 1 + LEAD))
                            pool.wait_ge(added["f1"][0], j * 32 + 16 * (h + ADD_LEAD))
                            pool.sem_inc(F["let_go"], 1)
                            pool.indirect_dma_start(acc1, IX(ap=fidx[:, h:h + 1], axis=0), sum_out[:, h, 0, :], None,
                                                    compute_op=ALU.add).then_inc(added["f1"][0], 16)
                for s in range(GSLOT - 1):
                    gather("f1", xtab, gat1, GSLOT, 0, s)
                with pool.Fori(0, PASSES - 1) as j:
                    one_pass(j, False)
                one_pass(PASSES - 1, True)
            with pool.Else():
                G = K["g1"]
                for s in range(GSLOT - 1):
                    gather("g1", xtab, gat1, GSLOT, 0, s)
                with pool.Fori(0, PASSES) as j:
                    for q in range(RING):
                        pool.wait_ge(G["summed"], steps(j, q))
                        gather("g1", xtab, gat1, GSLOT, j, q + GSLOT - 1)
                        pool.wait_ge(G["sidx_ok"], steps(j, q + 1))
                        pool.wait_ge(G["sum_ok"], steps(j, q + 1))
                        for i in range(TPS):
                            pool.wait_ge(added["g1"][0], j * (16 * RING * TPS) + 16 * (q * TPS + i + ADD_LEAD))
                            pool.sem_inc(G["let_go"], 1)
                            pool.indirect_dma_start(acc1, IX(ap=sidx[:, q % TPS, i:i + 1], axis=0), sum_out[:, q % 2, i, :], None,
                                                    compute_op=ALU.add).then_inc(added["g1"][0], 16)
                        pool.wait_ge(added["g1"][0], j * (16 * RING * TPS) + 16 * ((q + 1) * TPS + ADD_LEAD))
                        pool.sem_inc(G["out_free"], 1)
                for n in range(GSLOT):
                    pool.wait_ge(got["g1"][n], 16 * TPS * (STEPS // GSLOT + (n < GSLOT - 1)))
            pool.sem_inc(pool_done[1], 1)

        @block.scalar
        def _(act):
            start(act, "act")
            C = nc.scalar.copy
            n = 0
            for f in range(5):
                for b0 in range(0, BLOCKS, 4):
                    k = min(4, BLOCKS - b0)
                    act.wait_ge(turned, n + 1)
                    C(edge[:, b0 * P:(b0 + k) * P, f], turn_bank[n % 4][:, 0:k * P]).then_inc(turned_out, 1)
                    n += 1

            def roots(v, n):
                act.wait_ge(vec_done, n)
                nc.scalar.activation(v, v, ACT.Sqrt).then_inc(root_done, 1)
            act.wait_ge(based_mm, 1)
            C(wbase, bank[0][:, 0:STEPS]).then_inc(based, 1)
            roots(rstd[:, :], 1)
            act.wait_ge(scale_done, 1)
            with act.Fori(0, NT) as n:
                hold(act)
                act.wait_ge(rows_turned, n + LEAD)
                nc.scalar.activation(hrow[:, 0, :], xn[:, bass.ds(n, 1), :].rearrange("p o d -> p (o d)"), ACT.Relu,
                                     bias=nbias[:, bass.ds(n, 1)], scale=rstd[:, bass.ds(n, 1)]).then_inc(rows_done, 1)
                hold(act)
                act.wait_ge(rows_turned, n + (1 + LEAD))
                C(hT_all[:, bass.ds(n * P, P)], bank[6][:, 0:P]).then_inc(rows_kept, 1)
            roots(dinv[:, :], 2)
            act.wait_ge(scale_done, 2)
            with act.Fori(0, NT // (2 * SLOTS)) as t:
                for m in range(2 * SLOTS):
                    hold(act)
                    act.wait_ge(node_mm, t * (2 * SLOTS) + (m + 1 + LEAD))
                    act.wait_ge(st_tab[m % SLOTS], t * 32 + 16 * (m // SLOTS + LEAD))
                    nc.scalar.mul(node_out[:, m % SLOTS, :], bank[4 + m % 2][:, :], dinv[:, bass.ds(t * (2 * SLOTS) + m, 1)]).then_inc(node_ev, 1)

            def node_rows(base, w):
                def scales(k, b):
                    r = slice(b * DB, (b + 1) * DB)
                    act.wait_ge(blk_var, k + 1)
                    nc.scalar.activation(rstd[:, r], rstd[:, r], ACT.Sqrt).then_inc(blk_root, 1)
                    hold(act)
                    act.wait_ge(blk_ok, k + 1)

                def norm(t, m):
                    n, i = t * (2 * SLOTS) + m, m % (2 * DB)
                    if m % DB == 0:
                        scales(t * 2 + m // DB, m // DB % 2)
                    hold(act)
                    act.wait_ge(h_turned, n + (LEAD - 1))
                    nc.scalar.activation(hrow[:, m % 2, :], xn[:, bass.ds(n, 1), :].rearrange("p o d -> p (o d)"), ACT.Relu,
                                         bias=nbias[:, i:i + 1], scale=rstd[:, i:i + 1]).then_inc(h_done, 1)

                def turned_copy(n, b):
                    act.wait_ge(node_mm, n + (base - 1 + LEAD))
                    act.wait_ge(h_turned, n + (1 + LEAD))
                    C(hrowT[:, b, :], bank[6 + b][:, 0:P]).then_inc(hT_out, 1)

                def evict(t, m):
                    act.wait_ge(node_mm, t * (2 * SLOTS) + (base + m + 1 + LEAD))
                    act.wait_ge(st_tab[m % SLOTS], t * 32 + 16 * (base // SLOTS + m // SLOTS + LEAD))
                    C(node_out[:, m % SLOTS, 0:w], bank[4 + m % 2][:, 0:w]).then_inc(node_ev, 1)

                def three(t, m, ahead=2):
                    if ahead > 1:
                        norm(t, m + 2)
                    if ahead > 0:
                        turned_copy(t * (2 * SLOTS) + (m + 1), 1 - m % 2)
                    evict(t, m)
                norm(0, 0)
                norm(0, 1)
                turned_copy(0, 0)
                with act.Fori(0, NT // (2 * SLOTS) - 1) as t:
                    for m in range(2 * SLOTS):
                        three(t, m)
                for m in range(2 * SLOTS):
                    three(NT // (2 * SLOTS) - 1, m, min(2, 2 * SLOTS - 1 - m))

            def unit_roots(j):
                act.wait_ge(unit_sq, j + 1)
                nc.scalar.activation(ulen[:, :], ulen[:, :], ACT.Sqrt).then_inc(unit_root, 1)
            flag = window_flag(act)
            with act.If(flag == 0):
                F = K["f0"]
                with act.Fori(0, PASSES) as j:
                    for q in range(RING):
                        if q == 4:
                            unit_roots(j)
                        act.wait_ge(F["m_mm"], steps(j, q + 1))
                        act.wait_ge(F["summed"], steps(j, q - 1))
                        C(wsum[:, q % 2, :], bank[4 + q % 2][:, :]).then_inc(F["m_ok"], 1)
                        act.wait_ge(F["summed"], steps(j, q + 1))
                        act.wait_ge(F["out_free"], steps(j, q - 1))
                        C(sum_out0[:, q % TPS, :, :], bank[q % 2][:, :].rearrange("p (i x) -> p i x", i=TPS)).then_inc(F["sum_ok"], 1)
            with act.Else():
                with act.Fori(0, NCH // 2) as c:
                    for b in range(2):
                        hold(act)
                        act.wait_ge(coef_mm, c * 2 + (b + 1 + LEAD))
                        C(coef_mem[:, bass.ds(c * (2 * CHUNK * NB) + b * CHUNK * NB, CHUNK * NB)], bank[b][:, 0:CHUNK * NB]).then_inc(coef_out, 1)
                act.wait_ge(coef_out, NCH + LEAD)
                G = K["g0"]
                with act.Fori(0, PASSES) as j:
                    for q in range(RING):
                        if q == 4:
                            unit_roots(j)
                        hold(act)
                        act.wait_ge(got["g0"][q % GSLOT0], j * (16 * TPS * RING // GSLOT0) + 16 * TPS * (q // GSLOT0 + 1))
                        for i in range(TPS):
                            for b in range(NB):
                                g = gat0[:, q % GSLOT0, i, b * D:(b + 1) * D]
                                last = nc.scalar.mul(g, g, coef_mem[:, bass.ds(j * (RING * TPS * NB) + (q * TPS + i) * NB + b, 1)])
                        last.then_inc(G["scaled"], 1)
                        act.wait_ge(G["summed"], steps(j, q + 1))
                        act.wait_ge(G["out_free"], steps(j, q - 1))
                        C(sum_out0[:, q % TPS, :, :], bank[q % 2][:, :].rearrange("p (i x) -> p i x", i=TPS)).then_inc(G["sum_ok"], 1)

            act.wait_ge(layer_done[0], 1)
            act.wait_ge(pool_done[0], 1)
            def radial(p):
                w = emb[:, bass.ds(p * 256, 256)]
                hold(act)
                act.wait_ge(emb_v, p + (1 + LEAD))
                nc.scalar.activation(w, w, ACT.Square, bias=pcol[:, 4:5], scale=float(CENTERS - 1)).then_inc(emb_a, 1)
                hold(act)
                act.wait_ge(emb_a, p + (1 + LEAD))
                nc.scalar.activation(w, w, ACT.Exp, scale=-0.5).then_inc(emb_ok, 1)

            radial(0)
            node_rows(NT, D)

            def mlp(S, j, n):
                act.wait_ge(S["h0_mm"], steps(j, n))
                nc.scalar.activation(hid0, bank[6][:, 0:256], ACT.Silu, bias=b_m[:, 0:1]).then_inc(S["h0_ok"], 1)
                act.wait_ge(S["h1_mm"], steps(j, n))
                nc.scalar.activation(hid1, bank[6][:, 256:512], ACT.Silu, bias=b_m[:, 1:2]).then_inc(S["h1_ok"], 1)
            with act.If(flag == 0):
                F = K["f1"]
                mlp(F, 0, 1)
                mlp(F, 0, 2)
                act.wait_ge(added["f1"][0], 16 * ADD_LEAD)
                with act.Fori(0, PASSES) as j:
                    for q in range(RING):
                        if q == 4:
                            radial(j + 1)
                        mlp(F, j, q + 3)
                        if q % 4 == 3:
                            h = q // 4
                            act.wait_ge(F["summed"], steps(j, q + 1))
                            act.wait_ge(added["f1"][0], j * 32 + 16 * (h - 1 + ADD_LEAD))
                            C(sum_out[:, h, 0, :], bank[h][:, 0:2 * D]).then_inc(F["sum_ok"], 1)
            with act.Else():
                G = K["g1"]
                mlp(G, 0, 1)
                with act.Fori(0, PASSES) as j:
                    for q in range(RING):
                        if q == 4:
                            radial(j + 1)
                        mlp(G, j, q + 2)
                        act.wait_ge(G["summed"], steps(j, q + 1))
                        act.wait_ge(G["out_free"], steps(j, q - 1))
                        for h in range(2):
                            last = C(sum_out[:, q % 2, 2 * h:2 * h + 2, :], bank[h][:, :].rearrange("p (i x) -> p i x", i=2))
                        last.then_inc(G["sum_ok"], 1)

            with act.Fori(0, NT // 2) as t:
                for b in range(2):
                    act.wait_ge(fold_t, t * 2 + (b + 1 + LEAD))
                    act.wait_ge(fold_mm, t * 2 + (b - 1 + LEAD))
                    C(tT[:, b, :], bank[6 + b][:, 0:2 * D]).then_inc(fold_c, 1)

        @block.vector
        def _(dve):
            start(dve, "dve")
            own = [0]

            def link(ins):
                own[0] += 1
                ins.then_inc(dve_own, 1)
                dve.wait_ge(dve_own, own[0])

            V = nc.vector
            V.memset(src_rows[:, 12, :], PAD_NODE)
            V.memset(dst_rows[:, 12, :], PAD_NODE)
            V.memset(attr_rows[:, 12, :], 0.0)
            V.memset(xn[:, NODES // P:NT, :], 0.0).then_inc(padded, 1)
            V.memset(zero_b[:, :], 0.0)
            V.memset(ones[:, :], 1.0)
            V.memset(zero[:, :], 0.0)
            V.memset(w_up[:, :], 0.0)
            V.memset(w_m0[:, :, :], 0.0)
            V.memset(w_m1[:, :], 0.0)
            V.memset(w_m2[:, :, :], 0.0)
            V.memset(w_o[:, :, :], 0.0)
            V.memset(table[:, :], 0.0)
            V.memset(alpha[:, :], 0.0)
            V.memset(b2_rows[:, :], 0.0)
            V.memset(b2_parts[:, :, :], 0.0)
            V.memset(ones_b[:, :], 1.0)
            V.memset(edge[:, :, 5], 0.0)
            V.memset(emb[:, (PASSES - 1) * 256:], 0.0).then_inc(padded, 1)

            ids = BLOCKS * P
            dve.wait_ge(ld_src, 48)
            V.tensor_copy(arena[:, 0:ids], rows_i[:, 0:ids]).then_inc(rows_ok, 1)
            dve.wait_ge(ld_const, 48)
            V.tensor_copy(iota_rep, iota[:, :].unsqueeze(2).to_broadcast([P, P, CHUNK]))
            dve.wait_ge(turned_out, 4)
            link(V.tensor_copy(src_i, edge[:, :, 0]))
            link(V.tensor_scalar(src_hi, src_i, 7, None, ALU.logical_shift_right))
            link(V.tensor_scalar(src_i, src_i, 127, None, ALU.bitwise_and))
            V.tensor_copy(hi[:, :], src_hi)
            link(V.tensor_copy(lo[:, :], src_i))

            mean, gap, var = (moment[:, k, :] for k in range(3))

            def degree_hots(c0, c1):
                with dve.Fori(c0, c1) as c:
                    for b in range(2):
                        t0 = c * (2 * CHUNK) + b * CHUNK
                        hold(dve)
                        dve.wait_ge(chunk_mm, c * 2 + (b - 1 + LEAD))
                        V.tensor_tensor(lo_hot[:, b, :, :], iota_rep, lo[:, bass.ds(t0, CHUNK)].unsqueeze(1).to_broadcast([P, P, CHUNK]), ALU.is_equal)
                        V.tensor_tensor(hi_hot[:, b, :, :], iota_rep[:, 0:NT, :], hi[:, bass.ds(t0, CHUNK)].unsqueeze(1).to_broadcast([P, NT, CHUNK]),
                                        ALU.is_equal).then_inc(hots, 1)
            degree_hots(0, FIRST)
            dve.wait_ge(ld_dst, 48)
            V.tensor_copy(arena[:, ids:2 * ids], rows_i[:, ids:2 * ids]).then_inc(rows_ok, 1)
            dve.wait_ge(ld_x, 32)
            with dve.Fori(0, NT // DB) as k:
                for t in range(DB):
                    last = V.bn_stats(stats[:, bass.ds(k * DB + t, 1), :].rearrange("p o s -> p (o s)"),
                                      xn[:, bass.ds(k * DB + t, 1), :].rearrange("p o d -> p (o d)"))
            link(V.memset(dupd[:, :], 0.0))
            V.tensor_tensor(mean, stats[:, :, 1], stats[:, :, 4], ALU.add)
            V.tensor_tensor(var, stats[:, :, 2], stats[:, :, 5], ALU.add)
            link(V.tensor_tensor(gap, stats[:, :, 1], stats[:, :, 4], ALU.subtract))
            link(V.tensor_tensor(gap, gap, gap, ALU.mult))
            V.tensor_scalar(mean, mean, 0.5, None, ALU.mult)
            link(V.scalar_tensor_tensor(var, gap, D / 4.0, var, ALU.mult, ALU.add))
            V.tensor_scalar(rstd[:, :], var, 1.0 / D, EPS, ALU.mult, ALU.add).then_inc(vec_done, 1)
            degree_hots(FIRST, 2 * FIRST)
            dve.wait_ge(root_done, 1)
            link(V.reciprocal(rstd[:, :], rstd[:, :]))
            V.scalar_tensor_tensor(nbias[:, :], mean, -1.0, rstd[:, :], ALU.mult, ALU.mult).then_inc(scale_done, 1)

            degree_hots(2 * FIRST, NCH // 2)
            dve.wait_ge(deg_mm, 1)
            V.tensor_scalar(dpos[:, :], bank[2][:, 0:NT], 0.0, None, ALU.is_gt)
            V.tensor_scalar(dinv[:, :], bank[2][:, 0:NT], 1.0, None, ALU.max).then_inc(vec_done, 1)
            dve.wait_ge(root_done, 2)
            link(V.reciprocal(dinv[:, :], dinv[:, :]))
            V.tensor_tensor(dinv[:, :], dinv[:, :], dpos[:, :], ALU.mult).then_inc(scale_done, 1)
            dve.wait_ge(rows_kept, NT + LEAD)
            def slices(t0, t1):
                with dve.Fori(t0, t1) as t:
                    for b in range(2):
                        hold(dve)
                        dve.wait_ge(node_mm, t * 2 + (b - 1 + LEAD))
                        V.tensor_copy(hrowT[:, b, :], hT_all[:, bass.ds(t * (2 * P) + b * P, P)]).then_inc(sliced, 1)
            slices(0, NT // 2 - 5)

            dve.wait_ge(windows_ok, 1)
            MX, MN = ALU.max, ALU.min
            V.tensor_reduce(ext[:, 0:1], edge[:, 0:TILES, 5], AXX, MX)
            V.tensor_reduce(ext[:, 1:2], edge[:, 0:TILES, 5], AXX, MN)
            link(V.tensor_reduce(ext[:, 2:3], wgap, AXX, MN))
            V.tensor_scalar(ext[:, 1:3], ext[:, 1:3], -1.0, None, ALU.mult).then_inc(ext_ok, 1)
            dve.wait_ge(ext_mm, 1)
            link(V.tensor_reduce(ext_t[0:3, 0:1], bank[0][0:3, 0:P], AXX, MX))
            V.tensor_scalar(ext_t[0:3, 1:2], ext_t[0:3, 0:1], pcol[0:3, 6:7], None, ALU.is_gt).then_inc(viol_ok, 1)
            dve.wait_ge(viol_mm, 1)
            V.tensor_copy(flags[0:1, 0:1], bank[1][0:1, 0:1]).then_inc(flag_ok, 1)
            dve.wait_ge(ld_w, 16 * 21)
            link(V.tensor_scalar(table[:, :], table[:, :], alpha[:, 0:1], None, ALU.mult))
            flag = window_flag(dve)
            slices(NT // 2 - 5, NT // 2)


            def unit_squares(j):
                hold(dve)
                dve.wait_ge(unit_ok, j + LEAD)
                v = edge[:, bass.ds(j * (RING * TPS), RING * TPS), 2:5]
                V.tensor_tensor(usq[:, :, :], v, v, ALU.mult).then_inc(unit_own[0], 1)
                dve.wait_ge(unit_own[0], j + 1)
                V.tensor_reduce(ulen[:, :], usq[:, :, :], AXX, ALU.add).then_inc(unit_own[1], 1)
                dve.wait_ge(unit_own[1], j + 1)
                V.tensor_scalar(ulen[:, :], ulen[:, :], 1.3e-35, None, ALU.max).then_inc(unit_sq, 1)

            def unit_vectors(j):
                dve.wait_ge(unit_root, j + 1)
                V.tensor_scalar(ulen[:, :], ulen[:, :], 1e-12, None, ALU.add).then_inc(unit_own[2], 1)
                dve.wait_ge(unit_own[2], j + 1)
                V.reciprocal(ulen[:, :], ulen[:, :]).then_inc(unit_own[3], 1)
                hold(dve)
                dve.wait_ge(unit_own[3], j + 1)
                v = edge[:, bass.ds(j * (RING * TPS), RING * TPS), 2:5]
                V.tensor_tensor(v, v, ulen[:, :].unsqueeze(2).to_broadcast([P, RING * TPS, 3]), ALU.mult).then_inc(unit_ok, 1)

            def same_rows(k, j, q):
                S, L = K[k], int(k[1])
                dve.wait_ge(S["spread"], steps(j, q + 1))
                V.tensor_tensor(same[:, q % 2, :, :], bank[2][:, :].rearrange("p (i x) -> p i x", i=TPS),
                                st_edge[:, q % RING, :, L:L + 1].to_broadcast([P, TPS, P]), ALU.is_equal).then_inc(S["same_ok"], 1)

            def scatter_rows(k, j, q):
                S, L = K[k], int(k[1])
                dve.wait_ge(S["sidx_ok"], steps(j, q))
                dve.wait_ge(S["ranked"], steps(j, q + 1))
                V.tensor_scalar(dupd[:, :], bank[3][:, TPS * (q % 2):TPS * (q % 2) + TPS], pcol[:, 2:3], pcol[:, 3:4], ALU.is_gt, ALU.mult).then_inc(S["tmp_ok"], 1)
                dve.wait_ge(S["tmp_ok"], steps(j, q + 1))
                V.tensor_tensor(sidx[:, q % TPS, :], dupd[:, :], st_edge[:, q % RING, :, L], ALU.max).then_inc(S["sidx_ok"], 1)

            def stage0(k, j, s, rows):
                c0 = j * (RING * TPS) + s * TPS
                last = V.tensor_copy(st_edge[:, s % RING, :, 0:2], edge[:, bass.ds(c0, TPS), 0:2])
                if rows:
                    last = V.tensor_copy(gidx[:, s % RING, :], edge[:, bass.ds(c0, TPS), 1])
                last.then_inc(K[k]["staged"], 1)

            def stage1(k, j, s):
                q = s % RING
                c0 = (j + s // RING) * (2 * TPS) + (q % 4 * QUARTER + q // 4) * TPS
                V.tensor_copy(st_edge[:, q, :, :], edge[:, bass.ds(c0, TPS), :])
                last = V.tensor_copy(gidx[:, q, :], edge[:, bass.ds(c0, TPS), 0])
                last.then_inc(K[k]["staged"], 1)

            def mids(k, j, q):
                S, own = K[k], mids_own
                w = bank[4 + q % 2][:, :].rearrange("p (i x) -> p i x", i=TPS)
                g = gat1[:, q % GSLOT, :, :]
                gv = g[:, :, MUL:].rearrange("p i (c k) -> p i c k", c=3)
                m = mid[:, q % 2, :, :]
                mc = m[:, :, 2 * MUL:].rearrange("p i (c k) -> p i c k", c=3)
                unit = st_edge[:, q % RING, :, 2:5].unsqueeze(3).to_broadcast([P, TPS, 3, MUL])
                done = j * RING + (q + 1)
                dve.wait_ge(got[k][q % GSLOT], j * (16 * TPS * RING // GSLOT) + 16 * TPS * (q // GSLOT + 1))
                V.tensor_tensor(vdot[:, :, :, :], gv, unit, ALU.mult).then_inc(own[0], 1)
                dve.wait_ge(S["w_mm"], steps(j, q + 1))
                V.tensor_tensor(w01s, w[:, :, MUL:2 * MUL], g[:, :, 0:MUL], ALU.mult).then_inc(own[1], 1)
                dve.wait_ge(own[0], done)
                V.tensor_tensor(vsum[:, :, 0, :], vdot[:, :, 0, :], vdot[:, :, 1, :], ALU.add).then_inc(own[2], 1)
                V.tensor_tensor(m[:, :, 0:MUL], w[:, :, 0:MUL], g[:, :, 0:MUL], ALU.mult)
                V.tensor_tensor(mc[:, :, :, MUL:], w[:, :, 2 * MUL:3 * MUL].unsqueeze(2).to_broadcast([P, TPS, 3, MUL]), gv, ALU.mult)
                dve.wait_ge(own[2], done)
                V.tensor_tensor(vsum[:, :, 1, :], vsum[:, :, 0, :], vdot[:, :, 2, :], ALU.add).then_inc(own[3], 1)
                dve.wait_ge(own[1], done)
                V.tensor_tensor(mc[:, :, :, 0:MUL], w01s.unsqueeze(2).to_broadcast([P, TPS, 3, MUL]), unit, ALU.mult)
                dve.wait_ge(own[3], done)
                V.tensor_tensor(m[:, :, MUL:2 * MUL], w[:, :, 3 * MUL:], vsum[:, :, 1, :], ALU.mult).then_inc(S["mids_ok"], 1)

            with dve.If(flag == 0):
                F = K["f0"]

                def hot(j, s):
                    b = (s // 4) % 2
                    if s % 4 == 0 or isinstance(j, int):
                        dve.wait_ge(ld_typ[b], (j + s // 8) * 16 + 16)
                    dve.wait_ge(F["coef_mm"], steps(j, s - 1))
                    V.tensor_scalar(thot[:, s % 2, :], typ[:, b, (s % 4) * TPS * P:(s % 4 + 1) * TPS * P], pcol[0:64, 0:1], None, ALU.is_equal).then_inc(F["hot_ok"], 1)

                def near_rows(j, s):
                    V.tensor_tensor(near[:, s % 2, :, :], iota[:, 0:WIN].unsqueeze(1).to_broadcast([P, TPS, WIN]),
                                    edge[:, bass.ds(j * (RING * TPS) + s * TPS, TPS), 5:6].to_broadcast([P, TPS, WIN]), ALU.is_equal).then_inc(F["near_ok"], 1)

                def edge_weights(j, s):
                    dve.wait_ge(F["near_ok"], steps(j, s + 1))
                    dve.wait_ge(F["coef_mm"], steps(j, s + 1))
                    cf = bank[6 + s % 2][:, 0:TPS * NB].rearrange("p (i b) -> p i b", b=NB)
                    V.tensor_tensor(wedge[:, s % 2, :, :].rearrange("p i (n b) -> p i n b", b=NB),
                                    near[:, s % 2, :, :].unsqueeze(3).to_broadcast([P, TPS, WIN, NB]),
                                    cf.unsqueeze(2).to_broadcast([P, TPS, WIN, NB]), ALU.mult).then_inc(F["le_ok"], 1)
                for s in range(3):
                    stage0("f0", 0, s, False)
                hot(0, 0)
                hot(0, 1)
                near_rows(0, 0)
                same_rows("f0", 0, 0)
                edge_weights(0, 0)
                scatter_rows("f0", 0, 0)
                with dve.Fori(0, PASSES) as j:
                    for q in range(RING):
                        if q == 0:
                            unit_squares(j)
                        if q == 6:
                            unit_vectors(j)
                        hold(dve)
                        dve.wait_ge(F["m_mm"], steps(j, q))
                        dve.wait_ge(F["ranked"], steps(j, q))
                        stage0("f0", j, q + 3, False)
                        hot(j, q + 2)
                        near_rows(j, q + 1)
                        same_rows("f0", j, q + 1)
                        edge_weights(j, q + 1)
                        dve.wait_ge(F["out_free"], steps(j, q))
                        scatter_rows("f0", j, q + 1)
            with dve.Else():
                G = K["g0"]
                dve.wait_ge(node_ev, NT + LEAD)
                for b in range(SLOTS):
                    dve.wait_ge(st_tab[b], 16 * (NT // SLOTS + LEAD))
                dve.sem_inc(layer_in, 1)
                with dve.Fori(0, NCH // 2) as c:
                    for b in range(2):
                        dve.wait_ge(ld_typ[b], c * 16 + 16)
                        dve.wait_ge(coef_mm, c * 2 + (b - 1 + LEAD))
                        V.tensor_scalar(typ_hot[:, b, :], typ[:, b, :], pcol[0:64, 0:1], None, ALU.is_equal).then_inc(typ_hots, 1)
                dve.wait_ge(coef_mm, NCH + LEAD)
                for s in range(GSLOT0):
                    stage0("g0", 0, s, True)
                same_rows("g0", 0, 0)
                scatter_rows("g0", 0, 0)
                with dve.Fori(0, PASSES) as j:
                    for q in range(RING):
                        if q == 0:
                            unit_squares(j)
                        if q == 6:
                            unit_vectors(j)
                        hold(dve)
                        dve.wait_ge(G["summed"], steps(j, q))
                        stage0("g0", j, q + GSLOT0, True)
                        same_rows("g0", j, q + 1)
                        dve.wait_ge(G["out_free"], steps(j, q))
                        scatter_rows("g0", j, q + 1)

            def bounded(p):
                w = emb[:, bass.ds(p * 256, 256)]
                V.tensor_scalar(above, w, 1.0, 1e9, ALU.is_gt, ALU.mult)
                hold(dve)
                V.tensor_scalar(w, w, 0.0, 1.0, ALU.max, ALU.min).then_inc(emb_b, 1)
                hold(dve)
                dve.wait_ge(emb_b, p + (1 + LEAD))
                V.tensor_tensor(w, w, above, ALU.add).then_inc(emb_v, 1)
            dve.wait_ge(emb_ld, 16 * GROUPS)
            bounded(0)

            dve.wait_ge(layer_done[0], 1)
            dve.wait_ge(unit_ok, PASSES + LEAD)
            with dve.Fori(0, NT // DB // 2) as k:
                for b in range(2):
                    kk = k * 2 + b
                    dve.wait_ge(ld_acc[b], k * (16 * ACCS) + 16 * ACCS)
                    w = accin[:, b, :, :]
                    for n, half in enumerate((4, 2, 1)):
                        V.tensor_tensor(w[:, 0:half, :], w[:, 0:half, :], w[:, half:2 * half, :], ALU.add).then_inc(blk[n], 1)
                        dve.wait_ge(blk[n], kk + 1)
                    w3 = w[:, 0, :].rearrange("p (t d) -> p t d", t=DB)
                    V.tensor_tensor(w3, w3, dinv[:, bass.ds(kk * DB, DB)].unsqueeze(2).to_broadcast([P, DB, D]), ALU.mult).then_inc(blk[3], 1)
                    dve.wait_ge(blk[3], kk + 1)
                    xb = xn[:, bass.ds(kk * DB, DB), :]
                    V.tensor_tensor(xb, xb, w3, ALU.add).then_inc(acc_used, 1)
                    dve.wait_ge(acc_used, kk + (1 + LEAD))
                    dve.sem_inc(carried, 1)
                    r = slice(b * DB, (b + 1) * DB)
                    for t in range(DB):
                        last = V.bn_stats(stats[:, b * DB + t, :], xn[:, bass.ds(kk * DB + t, 1), :].rearrange("p o d -> p (o d)"))
                    last.then_inc(blk[4], 1)
                    dve.wait_ge(blk[4], kk + 1)
                    V.tensor_tensor(mean[:, r], stats[:, r, 1], stats[:, r, 4], ALU.add)
                    V.tensor_tensor(var[:, r], stats[:, r, 2], stats[:, r, 5], ALU.add)
                    V.tensor_tensor(gap[:, r], stats[:, r, 1], stats[:, r, 4], ALU.subtract).then_inc(blk[5], 1)
                    dve.wait_ge(blk[5], kk + 1)
                    V.tensor_tensor(gap[:, r], gap[:, r], gap[:, r], ALU.mult).then_inc(blk[6], 1)
                    dve.wait_ge(blk[6], kk + 1)
                    V.scalar_tensor_tensor(var[:, r], gap[:, r], D / 4.0, var[:, r], ALU.mult, ALU.add).then_inc(blk[7], 1)
                    dve.wait_ge(blk[7], kk + 1)
                    dve.wait_ge(h_turned, kk * DB + (LEAD - DB))
                    V.tensor_scalar(rstd[:, r], var[:, r], 1.0 / D, EPS, ALU.mult, ALU.add).then_inc(blk_var, 1)
                    dve.wait_ge(blk_root, kk + 1)
                    V.reciprocal(rstd[:, r], rstd[:, r]).then_inc(blk[8], 1)
                    dve.wait_ge(blk[8], kk + 1)
                    V.scalar_tensor_tensor(nbias[:, r], mean[:, r], -0.5, rstd[:, r], ALU.mult, ALU.mult).then_inc(blk_ok, 1)
            dve.wait_ge(blk_ok, NT // DB)

            with dve.If(flag == 0):
                F = K["f1"]

                def near_rows1(j, s):
                    dve.wait_ge(F["staged"], steps(j, s + 1))
                    V.tensor_tensor(near1[:, s % 2, :, :], iota[:, 0:WIN].unsqueeze(1).to_broadcast([P, TPS, WIN]),
                                    st_edge[:, s % RING, :, 5:6].to_broadcast([P, TPS, WIN]), ALU.is_equal).then_inc(F["near_ok"], 1)
                for s in range(GSLOT):
                    stage1("f1", 0, s)
                near_rows1(0, 0)
                dve.wait_ge(added["f1"][0], 16 * ADD_LEAD)
                with dve.Fori(0, PASSES) as j:
                    for q in range(RING):
                        if q == 2:
                            dve.wait_ge(emb_ld2, 16 * (GROUPS + 2))
                            bounded(j + 1)
                        hold(dve)
                        dve.wait_ge(F["summed"], steps(j, q - 1))
                        dve.wait_ge(F["mids_ok"], steps(j, q))
                        stage1("f1", j, q + GSLOT)
                        if q % 4 == 0:
                            h = q // 4
                            hold(dve)
                            dve.wait_ge(added["f1"][0], j * 32 + 16 * (h - 1 + ADD_LEAD))
                            V.tensor_copy(fidx[:, h:h + 1], fidx_all[:, bass.ds(j * 2 + h, 1)])
                        mids("f1", j, q)
                        dve.wait_ge(F["summed"], steps(j, q))
                        near_rows1(j, q + 1)
            with dve.Else():
                G = K["g1"]
                for s in range(GSLOT):
                    stage1("g1", 0, s)
                same_rows("g1", 0, 0)
                scatter_rows("g1", 0, 0)
                with dve.Fori(0, PASSES) as j:
                    for q in range(RING):
                        if q == 2:
                            dve.wait_ge(emb_ld2, 16 * (GROUPS + 2))
                            bounded(j + 1)
                        hold(dve)
                        dve.wait_ge(G["summed"], steps(j, q))
                        stage1("g1", j, q + GSLOT)
                        same_rows("g1", j, q + 1)
                        mids("g1", j, q)
                        dve.wait_ge(G["out_free"], steps(j, q - 2))
                        scatter_rows("g1", j, q + 1)

            with dve.Fori(0, NT // 2) as t:
                for b in range(2):
                    hold(dve)
                    dve.wait_ge(fold_mm, t * 2 + (b + 1 + LEAD))
                    x = xn[:, bass.ds(t * 2 + b, 1), :].rearrange("p o d -> p (o d)")
                    V.tensor_tensor(x, bank[4 + b][:, 0:D], x, ALU.add).then_inc(x_done, 1)

        @block.tensor
        def _(pe):
            start(pe, "pe")
            T = nc.tensor
            pe.wait_ge(ld_const, 48)
            turns = [0]

            def columns(fields):
                for f in fields:
                    if f < 2:
                        pe.wait_ge(rows_ok, f + 1)
                    if f == 2:
                        pe.wait_ge(ld_attr, 48)
                    for b0 in range(0, BLOCKS, 4):
                        n, k = turns[0], min(4, BLOCKS - b0)
                        if n >= 4:
                            pe.wait_ge(turned_out, n - 3)
                        for b in range(b0, b0 + k):
                            r = arena[:, f * BLOCKS * P + b * P:f * BLOCKS * P + (b + 1) * P] if f < 2 else \
                                attr_rows[:, b, f - 2:3 * P:3]
                            last = T.transpose(turn_bank[n % 4][:, (b - b0) * P:(b - b0 + 1) * P], r, ident[:, :])
                        last.then_inc(turned, 1)
                        turns[0] += 1
            columns([0])

            def turn_row(n):
                pe.wait_ge(rows_done, n + 1)
                pe.wait_ge(rows_kept, n + LEAD)
                T.transpose(bank[6][:, 0:P], hrow[:, 0, :], ident[:, :]).then_inc(rows_turned, 1)
            T.matmul(bank[2][:, 0:NT], zero_b[:, :], zero_b[:, 0:NT], start=True, stop=False)
            def degree_chunk(c, b):
                pe.wait_ge(hots, c * 2 + (b + 1 + LEAD))
                for i in range(CHUNK):
                    last = T.matmul(bank[2][:, 0:NT], lo_hot[:, b, :, i], hi_hot[:, b, :, i], start=False, stop=False)
                last.then_inc(chunk_mm, 1)
            def chunks_alone(c0, c1):
                with pe.Fori(c0, c1) as c:
                    for b in range(2):
                        degree_chunk(c, b)
            alone = NCH // 2 - NT // 2
            chunks_alone(0, FIRST)
            columns([1, 2, 3, 4])
            pe.wait_ge(turned_out, turns[0])
            T.matmul(bank[0][:, 0:STEPS], ones[0:1, :], edge[0:1, 0:TILES:TPS, 1], start=True, stop=True).then_inc(based_mm, 1)
            chunks_alone(FIRST, alone)
            with pe.Fori(0, NT // 2) as c:
                for b in range(2):
                    degree_chunk(c + alone, b)
                    turn_row(c * 2 + b)
            T.matmul(bank[2][:, 0:NT], zero_b[:, :], zero_b[:, 0:NT], start=False, stop=True).then_inc(deg_mm, 1)

            def node_product(base, weights, w):
                def turn(n, b):
                    pe.wait_ge(h_done, n + 1)
                    pe.wait_ge(hT_out, n + (LEAD - 1))
                    T.transpose(bank[6 + b][:, 0:P], hrow[:, b, :], ident[:, :]).then_inc(h_turned, 1)

                def prod(n, b):
                    pe.wait_ge(hT_out, n + (1 + LEAD))
                    pe.wait_ge(node_ev, n + (base - 1 + LEAD))
                    T.matmul(bank[4 + b][:, 0:w], hrowT[:, b, :], weights, start=True, stop=True).then_inc(node_mm, 1)
                for b in range(2):
                    turn(b, b)
                with pe.Fori(0, NT // 2 - 1) as t:
                    for b in range(2):
                        prod(t * 2 + b, b)
                        turn(t * 2 + (b + 2), b)
                for b in range(2):
                    prod(NT - 2 + b, b)

            pe.wait_ge(ld_w, 16 * 21)
            def products(t0, t1):
                with pe.Fori(t0, t1) as t:
                    for b in range(2):
                        pe.wait_ge(sliced, t * 2 + (b + 1 + LEAD))
                        pe.wait_ge(node_ev, t * 2 + (b - 1 + LEAD))
                        T.matmul(bank[4 + b][:, :], hrowT[:, b, :], bases[:, :, :].rearrange("p b d -> p (b d)"), start=True, stop=True).then_inc(node_mm, 1)
            products(0, NT // 2 - 5)
            pe.wait_ge(ext_ok, 1)
            T.transpose(bank[0][0:3, 0:P], ext[:, 0:3], ident[:, :]).then_inc(ext_mm, 1)
            pe.wait_ge(viol_ok, 1)
            T.matmul(bank[1][0:1, 0:1], ext_t[0:3, 1:2], ones[0:3, 0:1], start=True, stop=True).then_inc(viol_mm, 1)
            products(NT // 2 - 5, NT // 2)
            flag = window_flag(pe)
            pe.wait_ge(node_ev, NT + LEAD)

            def spread(k, j, q):
                S, L = K[k], int(k[1])
                pe.wait_ge(S["staged"], steps(j, q + 1))
                pe.wait_ge(S["same_ok"], steps(j, q))
                for i in range(TPS):
                    last = T.transpose(bank[2][:, i * P:(i + 1) * P], st_edge[:, q % RING, i, L:L + 1].to_broadcast([P, P]), ident[:, :])
                last.then_inc(S["spread"], 1)

            def rank(k, j, q):
                S = K[k]
                pe.wait_ge(S["same_ok"], steps(j, q + 1))
                pe.wait_ge(S["sidx_ok"], steps(j, q - 1))
                for i in range(TPS):
                    last = T.matmul(bank[3][:, TPS * (q % 2) + i:TPS * (q % 2) + i + 1], same[:, q % 2, i, :], pcol[:, 1:2], start=True, stop=True)
                last.then_inc(S["ranked"], 1)

            with pe.If(flag == 0):
                F = K["f0"]

                def coefs(j, q):
                    pe.wait_ge(F["hot_ok"], steps(j, q + 1))
                    pe.wait_ge(F["le_ok"], steps(j, q - 1))
                    for i in range(TPS):
                        last = T.matmul(bank[6 + q % 2][:, NB * i:NB * (i + 1)], thot[:, q % 2, i * P:(i + 1) * P], table[:, :], start=True, stop=True)
                    last.then_inc(F["coef_mm"], 1)
                spread("f0", 0, 0)
                coefs(0, 0)
                spread("f0", 0, 1)
                coefs(0, 1)
                rank("f0", 0, 0)
                with pe.Fori(0, PASSES) as j:
                    for q in range(RING):
                        pe.wait_ge(F["le_ok"], steps(j, q + 1))
                        pe.wait_ge(F["m_ok"], steps(j, q - 1))
                        for i in range(TPS):
                            last = T.matmul(bank[4 + q % 2][:, i * P:(i + 1) * P], wedge[:, q % 2, i, :], same[:, q % 2, i, :], start=True, stop=True)
                        last.then_inc(F["m_mm"], 1)
                        rank("f0", j, q + 1)
                        spread("f0", j, q + 2)
                        coefs(j, q + 2)
                        pe.wait_ge(F["m_ok"], steps(j, q + 1))
                        pe.wait_ge(win_in[q % TPS], j * (16 * RING // TPS) + 16 * (q // TPS + 1))
                        pe.wait_ge(F["sum_ok"], steps(j, q - 1))
                        for i in range(TPS):
                            last = T.matmul(bank[q % 2][:, i * D:(i + 1) * D], wsum[:, q % 2, i * P:(i + 1) * P], win[:, q % TPS, :], start=True, stop=True)
                        last.then_inc(F["summed"], 1)
            with pe.Else():
                G = K["g0"]
                pe.wait_ge(layer_in, 1)
                with pe.Fori(0, NCH // 2) as c:
                    for b in range(2):
                        pe.wait_ge(typ_hots, c * 2 + (b + 1 + LEAD))
                        pe.wait_ge(coef_out, c * 2 + (b - 1 + LEAD))
                        for i in range(CHUNK):
                            last = T.matmul(bank[b][:, i * NB:(i + 1) * NB], typ_hot[:, b, i * P:(i + 1) * P], table[:, :], start=True, stop=True)
                        last.then_inc(coef_mm, 1)
                pe.wait_ge(coef_out, NCH + LEAD)
                spread("g0", 0, 0)
                rank("g0", 0, 0)
                with pe.Fori(0, PASSES) as j:
                    for q in range(RING):
                        spread("g0", j, q + 1)
                        rank("g0", j, q + 1)
                        pe.wait_ge(G["scaled"], steps(j, q + 1))
                        pe.wait_ge(G["sum_ok"], steps(j, q - 1))
                        for i in range(TPS):
                            for b in range(NB):
                                last = T.matmul(bank[q % 2][:, i * D:(i + 1) * D], same[:, q % 2, i, :], gat0[:, q % GSLOT0, i, b * D:(b + 1) * D],
                                                start=(b == 0), stop=(b == NB - 1))
                        last.then_inc(G["summed"], 1)

            pe.wait_ge(wprep, 1)
            node_product(NT, w_up[:, :], D)
            pe.wait_ge(node_ev, 2 * NT + LEAD)

            def mlp(k, j, q, between=lambda h: None):
                S = K[k]
                if q % RING == 0:
                    pe.wait_ge(emb_ok, j + (q // RING + 1 + LEAD))
                pe.wait_ge(S["h1_ok"], steps(j, q))
                T.matmul(bank[6][:, 0:256], w_m0[:, q % RING, :], emb[:, bass.ds((j + q // RING) * 256, 256)], start=True, stop=True).then_inc(S["h0_mm"], 1)
                pe.wait_ge(S["mids_ok"], steps(j, q - 1))
                T.matmul(bank[4 + q % 2][:, :], ones_b[0:65, :], b2_parts[0:65, :, :].rearrange("o i d -> o (i d)"), start=True, stop=False)
                between(0)
                pe.wait_ge(S["h0_ok"], steps(j, q + 1))
                T.matmul(bank[6][:, 256:512], w_m1[:, :], hid0, start=True, stop=True).then_inc(S["h1_mm"], 1)
                between(1)

            def mlp_out(k, j, q):
                S = K[k]
                wb = bank[4 + q % 2]
                pe.wait_ge(S["h1_ok"], steps(j, q + 1))
                for i in range(TPS):
                    last = T.matmul(wb[:, i * P:(i + 1) * P], hid1[:, (i % 2) * P:(i % 2 + 1) * P], w_m2[:, i // 2, :], start=False, stop=(i == TPS - 1))
                last.then_inc(S["w_mm"], 1)

            with pe.If(flag == 0):
                F = K["f1"]

                def window_sums(j, q, h):
                    if h == 0:
                        pe.wait_ge(F["near_ok"], steps(j, q + 1))
                        pe.wait_ge(F["mids_ok"], steps(j, q + 1))
                        if q % 4 == 0:
                            pe.wait_ge(F["sum_ok"], j * 2 + (q // 4 - 1 + LEAD))
                    c = q % 4
                    for i in (2 * h, 2 * h + 1):
                        last = T.matmul(bank[q // 4][WIN * c:WIN * (c + 1), 0:2 * D], near1[:, q % 2, i, :], mid[:, q % 2, i, :],
                                        start=(i == 0), stop=(i == TPS - 1))
                    if h:
                        last.then_inc(F["summed"], 1)
                for q in range(2):
                    mlp("f1", 0, q)
                    mlp_out("f1", 0, q)
                with pe.Fori(0, PASSES) as j:
                    for q in range(RING):
                        mlp("f1", j, q + 2, lambda h: window_sums(j, q, h))
                        mlp_out("f1", j, q + 2)
            with pe.Else():
                G = K["g1"]
                spread("g1", 0, 0)
                mlp("g1", 0, 0)
                mlp_out("g1", 0, 0)
                rank("g1", 0, 0)
                with pe.Fori(0, PASSES) as j:
                    for q in range(RING):
                        spread("g1", j, q + 1)
                        mlp("g1", j, q + 1)
                        mlp_out("g1", j, q + 1)
                        rank("g1", j, q + 1)
                        pe.wait_ge(G["mids_ok"], steps(j, q + 1))
                        pe.wait_ge(G["sum_ok"], steps(j, q))
                        for i in range(TPS):
                            last = T.matmul(bank[i // 2][:, (i % 2) * 2 * D:(i % 2 + 1) * 2 * D], same[:, q % 2, i, :], mid[:, q % 2, i, :], start=True, stop=True)
                        last.then_inc(G["summed"], 1)

            def turn(k, b, t):
                n = k * (2 * DB) + (b * DB + t)
                m = (b * DB + t) % 2
                if t == 0:
                    pe.wait_ge(ld_fold[b], k * 16 + 16)
                pe.wait_ge(fold_c, n + (LEAD - 1))
                for h in range(2):
                    last = T.transpose(bank[6 + m][:, h * P:(h + 1) * P], fold_in[:, b, t, h * P:(h + 1) * P], ident[:, :])
                last.then_inc(fold_t, 1)

            def prod(k, b, t):
                n = k * (2 * DB) + (b * DB + t)
                m = (b * DB + t) % 2
                pe.wait_ge(fold_c, n + (LEAD + 1))
                pe.wait_ge(x_done, n + (LEAD - 1))
                for h in range(2):
                    last = T.matmul(bank[4 + m][:, 0:D], tT[:, m, h * P:(h + 1) * P], w_o[:, h, :], start=(h == 0), stop=(h == 1))
                last.then_inc(fold_mm, 1)
            pe.wait_ge(layer_done[1], 1)
            with pe.Fori(0, NT // DB // 2) as k:
                for m in range(2 * DB):
                    turn(k, m // DB, m % DB)
                    if m:
                        prod(k, (m - 1) // DB, (m - 1) % DB)
                prod(k, 1, DB - 1)


INPUTS = ("x", "src", "dst", "edge_attr_3", "edge_type_50", "edge_weight", "L0_gnn_bases", "L0_gnn_comps",
          "L0_gnn_alpha", "L1_gnn_W_up0", "L1_gnn_W_up1", "L1_gnn_mlp_w0", "L1_gnn_mlp_b0", "L1_gnn_mlp_w1",
          "L1_gnn_mlp_b1", "L1_gnn_mlp_w2", "L1_gnn_mlp_b2", "L1_gnn_W_out0", "L1_gnn_W_out1")


def constants():
    p = np.arange(P)
    pcol = np.zeros((P, 8), np.float32)
    pcol[:, 0] = p
    pcol[:, 1] = 2.0 ** (63 - p)
    pcol[:, 2] = 2.5 * 2.0 ** (63 - p)
    pcol[:, 3] = (NT - 1) * P + p
    pcol[:, 4] = -(p % CENTERS)
    pcol[:, 5] = p % WIN
    pcol[0:3, 6] = [WIN - 1, 0, -WIN]
    return {"c_ident": np.eye(P, dtype=np.float32), "c_iota": np.tile(p.astype(np.float32), (P, 1)), "c_pcol": pcol}


def kernel(**inputs):
    import concourse.bacc as bacc
    from concourse.bass_utils import run_bass_kernel_spmd

    nc = bacc.Bacc("TRN2", target_bir_lowering=False, num_devices=1)
    arrays = {n: np.ascontiguousarray(inputs[n]) for n in INPUTS} | constants()
    aps = {n: nc.dram_tensor(f"in_{n}", v.shape, mybir.dt.from_np(v.dtype), kind="ExternalInput").ap() for n, v in arrays.items()}
    out = nc.dram_tensor("out", [NODES, D], F32, kind="ExternalOutput").ap()
    build(nc, aps, out)
    r = run_bass_kernel_spmd(nc, [{f"in_{n}": v for n, v in arrays.items()}], core_ids=[0])
    return r.results[0]["out"]
```
